# Optimizing a Trainium2 kernel written in Bass

```python
import numpy as np
import jax
import jax.numpy as jnp

def _softmax(x, axis=-1):
    return jax.nn.softmax(x, axis=axis)

def _gelu(x):
    return jax.nn.gelu(x, approximate=True)

def _silu(x):
    return jax.nn.silu(x)

def _sigmoid(x):
    return jax.nn.sigmoid(x)

def _layernorm(x, axis=-1, eps=1e-05):
    m = jnp.mean(x, axis=axis, keepdims=True)
    v = jnp.var(x, axis=axis, keepdims=True)
    return (x - m) / jnp.sqrt(v + eps)

def _scatter_add(tgt, idx, src, axis=0):
    return tgt.at[idx].add(src)

def _segment_sum(src, seg, n):
    return jax.ops.segment_sum(src, seg, n)
kernel_name = 'mk_macaron_d1_jaxref_r4_0d79b4'

def setup_inputs(seed: int=0):
    np.random.seed(seed)
    _w = jnp.asarray

    def _L0_attn_setup():
        import jax, jax.numpy as jnp
        import numpy as np
        TTT_LR = 0.01
        LN_EPS = 1e-05
        key = jax.random.key(seed)
        ks = jax.random.split(key, 4)
        B, S, D, DS = (4, 512, 256, 64)
        sc = 1.0 / np.sqrt(D).astype(np.float32)
        return {'x': jax.random.normal(ks[0], (B, S, D), dtype=jnp.float32), 'Wk': jax.random.normal(ks[1], (DS, D), dtype=jnp.float32) * sc, 'bk': jnp.zeros((DS,), jnp.float32), 'Wv': jax.random.normal(ks[2], (D, D), dtype=jnp.float32) * sc, 'bv': jnp.zeros((D,), jnp.float32), 'Wq': jax.random.normal(ks[3], (DS, D), dtype=jnp.float32) * sc, 'bq': jnp.zeros((DS,), jnp.float32), 'gamma': jnp.ones((D,), jnp.float32), 'beta': jnp.zeros((D,), jnp.float32)}
    _L0_attn_in = _L0_attn_setup()

    def _L0_ffn_setup():
        import jax, jax.numpy as jnp
        import numpy as np
        DIM = 256
        DEPTH = 2
        HEADS = 8
        DIM_HEAD = 64
        WINDOW = 128
        INNER = HEADS * DIM_HEAD
        HID = int(DIM * 4 * 2 / 3)
        B, N = (2, 2048)
        QK_SCALE = 8.0

        def shift_token(t):
            t1, t2 = jnp.split(t, 2, axis=-1)
            t2 = jnp.pad(t2, ((0, 0), (1, 0), (0, 0)))[:, :-1]
            return jnp.concatenate([t1, t2], axis=-1)

        def l2norm(t):
            return t / jnp.clip(jnp.linalg.norm(t, axis=-1, keepdims=True), 1e-12)

        def rotate_half(x):
            x1, x2 = jnp.split(x, 2, axis=-1)
            return jnp.concatenate([-x2, x1], axis=-1)

        def rotary_xpos(q, k):
            n = q.shape[-2]
            half_idx = jnp.arange(0, DIM_HEAD, 2, dtype=jnp.float32)
            inv_freq = 1.0 / 10000.0 ** (half_idx / DIM_HEAD)
            t = jnp.arange(n, dtype=jnp.float32)
            freqs = t[:, None] * inv_freq[None, :]
            freqs = jnp.concatenate([freqs, freqs], axis=-1)
            base = (half_idx + 0.4 * DIM_HEAD) / (1.4 * DIM_HEAD)
            power = (t - n // 2) / float(WINDOW // 2)
            scale = base[None, :] ** power[:, None]
            scale = jnp.concatenate([scale, scale], axis=-1)
            cos, sin = (jnp.cos(freqs), jnp.sin(freqs))
            q = q * cos * scale + rotate_half(q) * sin * scale
            k = k * cos / scale + rotate_half(k) * sin / scale
            return (q, k)

        def local_attention(q, k, v):
            b, h, n, d = q.shape
            w = n // WINDOW
            bq = q.reshape(b, h, w, WINDOW, d) * QK_SCALE
            bk = k.reshape(b, h, w, WINDOW, d)
            bv = v.reshape(b, h, w, WINDOW, d)

            def look_around(t):
                p = jnp.pad(t, ((0, 0), (0, 0), (1, 0), (0, 0), (0, 0)))
                return jnp.concatenate([p[:, :, :w], p[:, :, 1:]], axis=3)
            bk, bv = (look_around(bk), look_around(bv))
            bt = jnp.arange(n).reshape(w, WINDOW)
            btp = jnp.pad(bt, ((1, 0), (0, 0)), constant_values=-1)
            btk = jnp.concatenate([btp[:w], btp[1:]], axis=1)
            sim = jnp.einsum('bhwid,bhwjd->bhwij', bq, bk)
            i = bt[:, :, None]
            j = btk[:, None, :]
            mask = (i < j) | (i > j + WINDOW) | (j == -1)
            sim = jnp.where(mask, -jnp.finfo(sim.dtype).max, sim)
            attn = jax.nn.softmax(sim, axis=-1)
            out = jnp.einsum('bhwij,bhwjd->bhwid', attn, bv)
            return out.reshape(b, h, n, d)

        def _layer(x, wqkv, qs, ksc, wo, lg, lb, w1, b1, w2, b2):
            b, n, _ = x.shape
            h = shift_token(x)
            qkv = h @ wqkv
            q, k, v = jnp.split(qkv, 3, axis=-1)
            to_heads = lambda t: t.reshape(b, n, HEADS, DIM_HEAD).transpose(0, 2, 1, 3)
            q, k, v = (to_heads(q), to_heads(k), to_heads(v))
            q = l2norm(q) * qs
            k = l2norm(k) * ksc
            q, k = rotary_xpos(q, k)
            o = local_attention(q, k, v)
            o = o.transpose(0, 2, 1, 3).reshape(b, n, INNER)
            x = x + o @ wo
            h = shift_token(x)
            mu = h.mean(-1, keepdims=True)
            var = h.var(-1, keepdims=True)
            h = (h - mu) / jnp.sqrt(var + 1e-05) * lg + lb
            h = h @ w1 + b1
            a, g = jnp.split(h, 2, axis=-1)
            h = a * jax.nn.gelu(g, approximate=False)
            x = x + h @ w2 + b2
            return x
        key = jax.random.key(seed)
        ks = jax.random.split(key, 6)
        return {'x': jax.random.normal(ks[0], (B, N, DIM), jnp.float32), 'wqkv': jax.random.normal(ks[1], (DEPTH, DIM, 3 * INNER), jnp.float32) * 0.02, 'q_scale': jnp.ones((DEPTH, DIM_HEAD), jnp.float32), 'k_scale': jnp.ones((DEPTH, DIM_HEAD), jnp.float32), 'wo': jax.random.normal(ks[2], (DEPTH, INNER, DIM), jnp.float32) * 0.02, 'ln_g': jnp.ones((DEPTH, DIM), jnp.float32), 'ln_b': jnp.zeros((DEPTH, DIM), jnp.float32), 'w1': jax.random.normal(ks[3], (DEPTH, DIM, 2 * HID), jnp.float32) * 0.02, 'b1': jnp.zeros((DEPTH, 2 * HID), jnp.float32), 'w2': jax.random.normal(ks[4], (DEPTH, HID, DIM), jnp.float32) * 0.02, 'b2': jnp.zeros((DEPTH, DIM), jnp.float32)}
    _L0_ffn_in = _L0_ffn_setup()
    _d = {'L0_attn_x': _L0_attn_in['x'], 'L0_attn_Wk': _L0_attn_in['Wk'], 'L0_attn_bk': _L0_attn_in['bk'], 'L0_attn_Wv': _L0_attn_in['Wv'], 'L0_attn_bv': _L0_attn_in['bv'], 'L0_attn_Wq': _L0_attn_in['Wq'], 'L0_attn_bq': _L0_attn_in['bq'], 'L0_attn_gamma': _L0_attn_in['gamma'], 'L0_attn_beta': _L0_attn_in['beta'], 'L0_ffn_wqkv': _L0_ffn_in['wqkv'], 'L0_ffn_q_scale': _L0_ffn_in['q_scale'], 'L0_ffn_k_scale': _L0_ffn_in['k_scale'], 'L0_ffn_wo': _L0_ffn_in['wo'], 'L0_ffn_ln_g': _L0_ffn_in['ln_g'], 'L0_ffn_ln_b': _L0_ffn_in['ln_b'], 'L0_ffn_w1': _L0_ffn_in['w1'], 'L0_ffn_b1': _L0_ffn_in['b1'], 'L0_ffn_w2': _L0_ffn_in['w2'], 'L0_ffn_b2': _L0_ffn_in['b2']}
    _x0 = _d['L0_attn_x']
    _d['L0_attn_x'] = jax.random.normal(jax.random.fold_in(jax.random.key(seed), 1), (8, 512, 256), dtype=_x0.dtype)
    del _x0
    return _d

def reference(L0_attn_x, L0_attn_Wk, L0_attn_bk, L0_attn_Wv, L0_attn_bv, L0_attn_Wq, L0_attn_bq, L0_attn_gamma, L0_attn_beta, L0_ffn_wqkv, L0_ffn_q_scale, L0_ffn_k_scale, L0_ffn_wo, L0_ffn_ln_g, L0_ffn_ln_b, L0_ffn_w1, L0_ffn_b1, L0_ffn_w2, L0_ffn_b2):

    def _L0_attn_ref(x, Wk, bk, Wv, bv, Wq, bq, gamma, beta):
        import jax, jax.numpy as jnp
        import numpy as np
        TTT_LR = 0.01
        LN_EPS = 1e-05
        B, S, D = x.shape
        DS = Wk.shape[0]
        mu = jnp.mean(x, axis=-1, keepdims=True)
        var = jnp.mean((x - mu) ** 2, axis=-1, keepdims=True)
        h = (x - mu) * jax.lax.rsqrt(var + LN_EPS) * gamma + beta
        keys = jnp.einsum('bsd,ed->bse', h, Wk) + bk
        values = jnp.einsum('bsd,ed->bse', h, Wv) + bv
        queries = jnp.einsum('bsd,ed->bse', h, Wq) + bq

        def step(W, qkv):
            q_t, k_t, v_t = qkv
            y_t = jnp.einsum('bds,bs->bd', W, q_t)
            pred = jnp.einsum('bds,bs->bd', W, k_t)
            err = pred - v_t
            W = W - TTT_LR * err[:, :, None] * k_t[:, None, :]
            return (W, y_t)
        W0 = jnp.zeros((B, D, DS), x.dtype)
        qs = jnp.swapaxes(queries, 0, 1)
        ks_ = jnp.swapaxes(keys, 0, 1)
        vs = jnp.swapaxes(values, 0, 1)
        _, ys = jax.lax.scan(step, W0, (qs, ks_, vs))
        y = jnp.swapaxes(ys, 0, 1)
        return x + y

    def _L0_ffn_ref(x, wqkv, q_scale, k_scale, wo, ln_g, ln_b, w1, b1, w2, b2):
        import jax, jax.numpy as jnp
        import numpy as np
        DIM = 256
        DEPTH = 2
        HEADS = 8
        DIM_HEAD = 64
        WINDOW = 128
        INNER = HEADS * DIM_HEAD
        HID = int(DIM * 4 * 2 / 3)
        B, N = (2, 2048)
        QK_SCALE = 8.0

        def shift_token(t):
            t1, t2 = jnp.split(t, 2, axis=-1)
            t2 = jnp.pad(t2, ((0, 0), (1, 0), (0, 0)))[:, :-1]
            return jnp.concatenate([t1, t2], axis=-1)

        def l2norm(t):
            return t / jnp.clip(jnp.linalg.norm(t, axis=-1, keepdims=True), 1e-12)

        def rotate_half(x):
            x1, x2 = jnp.split(x, 2, axis=-1)
            return jnp.concatenate([-x2, x1], axis=-1)

        def rotary_xpos(q, k):
            n = q.shape[-2]
            half_idx = jnp.arange(0, DIM_HEAD, 2, dtype=jnp.float32)
            inv_freq = 1.0 / 10000.0 ** (half_idx / DIM_HEAD)
            t = jnp.arange(n, dtype=jnp.float32)
            freqs = t[:, None] * inv_freq[None, :]
            freqs = jnp.concatenate([freqs, freqs], axis=-1)
            base = (half_idx + 0.4 * DIM_HEAD) / (1.4 * DIM_HEAD)
            power = (t - n // 2) / float(WINDOW // 2)
            scale = base[None, :] ** power[:, None]
            scale = jnp.concatenate([scale, scale], axis=-1)
            cos, sin = (jnp.cos(freqs), jnp.sin(freqs))
            q = q * cos * scale + rotate_half(q) * sin * scale
            k = k * cos / scale + rotate_half(k) * sin / scale
            return (q, k)

        def local_attention(q, k, v):
            b, h, n, d = q.shape
            w = n // WINDOW
            bq = q.reshape(b, h, w, WINDOW, d) * QK_SCALE
            bk = k.reshape(b, h, w, WINDOW, d)
            bv = v.reshape(b, h, w, WINDOW, d)

            def look_around(t):
                p = jnp.pad(t, ((0, 0), (0, 0), (1, 0), (0, 0), (0, 0)))
                return jnp.concatenate([p[:, :, :w], p[:, :, 1:]], axis=3)
            bk, bv = (look_around(bk), look_around(bv))
            bt = jnp.arange(n).reshape(w, WINDOW)
            btp = jnp.pad(bt, ((1, 0), (0, 0)), constant_values=-1)
            btk = jnp.concatenate([btp[:w], btp[1:]], axis=1)
            sim = jnp.einsum('bhwid,bhwjd->bhwij', bq, bk)
            i = bt[:, :, None]
            j = btk[:, None, :]
            mask = (i < j) | (i > j + WINDOW) | (j == -1)
            sim = jnp.where(mask, -jnp.finfo(sim.dtype).max, sim)
            attn = jax.nn.softmax(sim, axis=-1)
            out = jnp.einsum('bhwij,bhwjd->bhwid', attn, bv)
            return out.reshape(b, h, n, d)

        def _layer(x, wqkv, qs, ksc, wo, lg, lb, w1, b1, w2, b2):
            b, n, _ = x.shape
            h = shift_token(x)
            qkv = h @ wqkv
            q, k, v = jnp.split(qkv, 3, axis=-1)
            to_heads = lambda t: t.reshape(b, n, HEADS, DIM_HEAD).transpose(0, 2, 1, 3)
            q, k, v = (to_heads(q), to_heads(k), to_heads(v))
            q = l2norm(q) * qs
            k = l2norm(k) * ksc
            q, k = rotary_xpos(q, k)
            o = local_attention(q, k, v)
            o = o.transpose(0, 2, 1, 3).reshape(b, n, INNER)
            x = x + o @ wo
            h = shift_token(x)
            mu = h.mean(-1, keepdims=True)
            var = h.var(-1, keepdims=True)
            h = (h - mu) / jnp.sqrt(var + 1e-05) * lg + lb
            h = h @ w1 + b1
            a, g = jnp.split(h, 2, axis=-1)
            h = a * jax.nn.gelu(g, approximate=False)
            x = x + h @ w2 + b2
            return x
        for l in range(DEPTH):
            x = _layer(x, wqkv[l], q_scale[l], k_scale[l], wo[l], ln_g[l], ln_b[l], w1[l], b1[l], w2[l], b2[l])
        return x
    x = L0_attn_x
    x = x + 0.5 * _L0_ffn_ref(_layernorm(x, axis=-1), L0_ffn_wqkv, L0_ffn_q_scale, L0_ffn_k_scale, L0_ffn_wo, L0_ffn_ln_g, L0_ffn_ln_b, L0_ffn_w1, L0_ffn_b1, L0_ffn_w2, L0_ffn_b2)
    x = x + _L0_attn_ref(_layernorm(x, axis=-1), L0_attn_Wk, L0_attn_bk, L0_attn_Wv, L0_attn_bv, L0_attn_Wq, L0_attn_bq, L0_attn_gamma, L0_attn_beta)
    x = x + 0.5 * _L0_ffn_ref(_layernorm(x, axis=-1), L0_ffn_wqkv, L0_ffn_q_scale, L0_ffn_k_scale, L0_ffn_wo, L0_ffn_ln_g, L0_ffn_ln_b, L0_ffn_w1, L0_ffn_b1, L0_ffn_w2, L0_ffn_b2)
    return x

_drawn_inputs = setup_inputs


def setup_inputs(seed=0):
    import zlib

    import numpy as np

    out = dict(_drawn_inputs(seed))
    spreads = {'L0_attn_bk': (0.0, 0.1),
     'L0_attn_bv': (0.0, 0.288),
     'L0_attn_bq': (0.0, 0.302),
     'L0_attn_gamma': (1.0, 0.2),
     'L0_attn_beta': (0.0, 0.1),
     'L0_ffn_q_scale': (1.0, 0.6),
     'L0_ffn_k_scale': (1.0, 0.6),
     'L0_ffn_ln_g': (1.0, 0.6),
     'L0_ffn_ln_b': (0.0, 0.8),
     'L0_ffn_b1': (0.0, 0.783),
     'L0_ffn_b2': (0.0, 0.1)}
    factors = {'L0_ffn_wqkv': 2.743}
    for name, (base, spread) in spreads.items():
        noise = np.random.default_rng([zlib.crc32(name.encode()), seed]).standard_normal(out[name].shape)
        drawn = base * np.exp(spread * noise) if base else spread * noise
        out[name] = jnp.asarray(drawn.astype(out[name].dtype))
    for name, factor in factors.items():
        out[name] = (out[name] * factor).astype(out[name].dtype)
    return out
```

```python
import numpy as np
import concourse.bass as bass
from concourse import mybir
from contextlib import ExitStack

F32 = mybir.dt.float32
BF16 = mybir.dt.bfloat16
ALU = mybir.AluOpType
ACT = mybir.ActivationFunctionType
AX = mybir.AxisListType

P = 128
B, N, D = 8, 512, 256
DEPTH, HEADS, DH = 2, 8, 64
INNER = HEADS * DH
WINDOW = 128
HID = int(D * 4 * 2 / 3)
DS = 64
NT = N // P
KT = D // P
PAIRS = HEADS // 2
MT = -(-HID // P)
MLAST = HID - (MT - 1) * P
QK_SCALE = 8.0
NEG = -1e30
TTT_LR = 0.01
LN_EPS = 1e-5
LAYERS = 2 * DEPTH
NLEV = 7


def build(nc, A, passes=2, do_ttt=True):
    ctx = ExitStack()
    with ctx:
        def sb(name, shape, dt=F32):
            return ctx.enter_context(nc.sbuf_tensor(name, shape, dt))

        credits = {}

        def sem(name, credit=1):
            made = ctx.enter_context(nc.semaphore(name))
            credits[id(made)] = (made, credit)
            return made

        def at(which, count):
            value = count + credits[id(which)][1]
            return max(value, 1) if isinstance(value, int) else value

        Y = sb("Y", [P, B * NT, D])
        wqkv = sb("wqkv", [P, DEPTH, KT, 3 * INNER])
        wo = sb("wo", [P, DEPTH, PAIRS, D])
        w1 = sb("w1", [P, DEPTH, KT, 2 * HID])
        w2 = sb("w2", [P, DEPTH, MT, D])
        rot = sb("rot", [P, DEPTH, NT, 4, DH])
        lng = sb("lng", [P, DEPTH, KT])
        lnb = sb("lnb", [P, DEPTH, KT])
        b1 = sb("b1", [P, DEPTH, 2, MT])
        b2 = sb("b2", [P, DEPTH, D])
        ident = sb("ident", [P, P])
        identb = sb("identb", [P, P], BF16)
        maskf = sb("maskf", [P, 2 * WINDOW])
        maskb = sb("maskb", [P, 2, 2 * WINDOW], BF16)
        small = sb("small", [P, 4])
        h = sb("h", [P, NT, D])
        hT = sb("hT", [P, 2, KT, P])
        sq = sb("sq", [P, 2, INNER])
        ss = sb("ss", [P, 2 * HEADS])
        ssg = sb("ssg", [P, 2 * HEADS])
        r = sb("r", [P, NT, 2 * HEADS])
        t1 = sb("t1", [P, 2, INNER])
        t2 = sb("t2", [P, 2, INNER])
        qr = sb("qr", [P, INNER])
        kr = sb("kr", [P, INNER])
        qT = sb("qT", [P, PAIRS, NT, P])
        kT = sb("kT", [P, PAIRS, 2, NT, P])
        v = sb("v", [P, NT, INNER])
        nm = sb("nm", [P, HEADS])
        nb = sb("nb", [P, HEADS])
        pr = sb("pr", [P, HEADS, 2 * WINDOW])
        den = sb("den", [P, HEADS])
        rden = sb("rden", [P, HEADS])
        pT = sb("pT", [P, HEADS, 2, P])
        oT = sb("oT", [P, PAIRS, P])
        h2 = sb("h2", [P, NT, D])
        h2n = sb("h2n", [P, NT, D])
        h2T = sb("h2T", [P, 2, KT, 2 * P])
        st = sb("st", [P, NT, 6])
        mv = sb("mv", [P, NT, 2])
        vare = sb("vare", [P, NT])
        rs = sb("rs", [P, NT])
        gg = sb("gg", [P, 2, 2 * P])
        uT0 = sb("uT", [P, MT, 2 * P])
        xb = sb("xb", [P, NT, D])

        uT = (uT0, pr[:, :, :].rearrange("p h k -> p (h k)")[:, 0:MT * 2 * P].rearrange("p (m c) -> p m c", m=MT))

        bank = [ctx.enter_context(nc.psum_tensor(f"bank{i}", [P, 512], F32)) for i in range(8)]

        s_x = sem("x_loaded", 0)
        s_w = sem("weights_loaded", 0)
        s_const = sem("constants_ready", 0)
        s_settled = sem("settled", 0)
        s_ln = sem("pass_ln_done")
        s_lnst = sem("pass_ln_stats")
        s_lnr = sem("pass_ln_rstd")
        s_res = sem("pass_residual_done")
        s_out = sem("out_stored")
        negmax_done = sem("negmax_done")
        kr_step = sem("kr_step")
        ha_loaded = sem("ha_loaded", 0)
        ht_ps = sem("ht_ps")
        ht_sb = sem("ht_sb")
        q_ps, k_ps, v_ps = sem("q_ps"), sem("k_ps"), sem("v_ps")
        sqq, sqk = sem("sqq"), sem("sqk")
        rotq, rotk = sem("rotq"), sem("rotk")
        ss_done, r_done = sem("ss_done"), sem("r_done")
        qrot, krot = sem("qrot"), sem("krot")
        qt_ps, kt_ps = sem("qt_ps"), sem("kt_ps")
        qt_sb, ktlo_sb, kthi_sb, v_sb = sem("qt_sb"), sem("ktlo_sb"), sem("kthi_sb"), sem("v_sb")
        s_ps = sem("s_ps")
        nb_done = sem("nb_done")
        exp_done = sem("exp_done", 4)
        rden_done = sem("rden_done")
        pn_done = sem("pn_done", 4)
        pt_ps = sem("pt_ps", 4)
        pte_sb, pto_sb = sem("pte_sb"), sem("pto_sb")
        pv_ps = sem("pv_ps")
        o_sb = sem("o_sb")
        wo_ps = sem("wo_ps")
        xa_done = sem("xa_done")
        h2_loaded = [sem("h2_loaded0", 0), sem("h2_loaded1", 0)]
        st_done, mv_done, rs_done = sem("st_done"), sem("mv_done"), sem("rs_done")
        h2n_done = sem("h2n_done", 4)
        h2t_ps = sem("h2t_ps", 2)
        h2t_sb = sem("h2t_sb")
        w1_ps = sem("w1_ps", 12)
        gelu_done = sem("gelu_done")
        u_done = sem("u_done", 2)
        w2_ps = sem("w2_ps", 4)
        xb_done = sem("xb_done")
        xf_done = sem("xf_done", 4)

        def settle(e):
            e.sem_inc(s_settled, 1)

        def idx(L, b, t):
            return 4 * b + (32 * L + t)

        def xt(buf, b, t):
            if isinstance(b, int):
                return buf[:, 4 * b + t, :]
            return buf[:, bass.ds(4 * b + t, 1), :].rearrange("p a d -> p (a d)")

        def xts(buf, b, t, k, lo, hi, p0=0, p1=P):
            if isinstance(b, int):
                return buf[p0:p1, 4 * b + t:4 * b + t + k, lo:hi]
            return buf[p0:p1, bass.ds(4 * b + t, k), lo:hi]

        nX = 16 * 8
        W_DMAS = 2 * (1 + 1 + 1 + 2) + 12

        def mt_bank(job):
            return job % 4

        s_pln = sem("variance_guarded")

        st0 = sb("st0", [P, NT, 6])
        mv0 = sb("mv0", [P, NT, 2])
        va0 = sb("va0", [P, NT])
        rs0 = sb("rs0", [P, NT])
        s_mv0, s_va0, s_rs0 = sem("pass_mv"), sem("pass_var"), sem("pass_rstd")

        xw = (h2n, xb)
        x_in = A["x"].rearrange("b (t p) d -> p b t d", p=P)
        x_out = A["out"].rearrange("b (t p) d -> p b t d", p=P)
        xw_loaded = [sem("xw0_loaded", 0), sem("xw1_loaded", 0)]
        xw_used = [sem("xw0_used", 1), sem("xw1_used", 1)]
        xw_mixed = [sem("xw0_mixed"), sem("xw1_mixed")]
        xw_stored = [sem("xw0_stored", 16), sem("xw1_stored", 16)]

        def seq(ap, b):
            return ap[:, bass.ds(b, 1), :, :].rearrange("p b t d -> p (b t) d")

        def two(b, i):
            return 2 * b + i

        def sp_entry(e):
            with e.Fori(0, B // 2) as bb:
                for i in range(2):
                    e.wait_ge(xw_used[i], at(xw_used[i], bb))
                    settle(e)
                    e.dma_start(xw[i][:, :, :], seq(x_in, 2 * bb + i)).then_inc(xw_loaded[i], 16)

        def dve_entry(e):
            with e.Fori(0, B // 2) as bb:
                for i in range(2):
                    x = xw[i]
                    e.wait_ge(xw_loaded[i], at(xw_loaded[i], 16 * bb + 16))
                    for t in range(NT):
                        m = e.bn_stats(st0[:, t, :], x[:, t, :])
                    m.then_inc(s_lnst, 1)
                    e.wait_ge(s_lnst, at(s_lnst, 2 * bb + i + 1))
                    settle(e)
                    for t in range(NT):
                        m = e.bn_aggr(mv0[:, t, :], st0[:, t, :])
                    m.then_inc(s_mv0, 1)
                    e.wait_ge(s_rs0, at(s_rs0, 2 * bb + i + 1))
                    e.wait_ge(s_mv0, at(s_mv0, 2 * bb + i + 1))
                    for t in range(NT):
                        m = e.tensor_scalar(xt(Y, 2 * bb + i, t), x[:, t, :], mv0[:, t, 0:1], rs0[:, t:t + 1], ALU.subtract, ALU.mult)
                        m.then_inc(s_ln, 1)
                    e.wait_ge(s_ln, at(s_ln, 8 * bb + 4 * i + 4))
                    m = e.nop()
                    m.then_inc(xw_used[i], 1)

        def pool_entry(e):
            with e.Fori(0, B // 2) as bb:
                for i in range(2):
                    g = 2 * bb + i
                    e.wait_ge(s_mv0, at(s_mv0, g + 1))
                    settle(e)
                    e.tensor_scalar(va0[:, :], mv0[:, :, 1], LN_EPS, None, ALU.add).then_inc(s_va0, 1)
                    e.wait_ge(s_va0, at(s_va0, g + 1))
                    e.tensor_tensor(rs0[:, :], va0[:, :], small[:, 0:1].to_broadcast([P, NT]), ALU.pow).then_inc(s_rs0, 1)

        def sp_exit(e, ps):
            src = x_in if ps == 0 else x_out
            e.wait_ge(xf_done, at(xf_done, idx(DEPTH * ps + DEPTH - 1, B - 1, NT - 1) + 1))
            settle(e)
            with e.Fori(0, B // 2) as bb:
                for i in range(2):
                    e.wait_ge(xw_stored[i], at(xw_stored[i], 16 * bb + (64 * ps - 0)))
                    settle(e)
                    e.dma_start(xw[i][:, :, :], seq(src, 2 * bb + i)).then_inc(xw_loaded[i], 16)
                for i in range(2):
                    e.wait_ge(xw_mixed[i], at(xw_mixed[i], bb + 1))
                    settle(e)
                    e.dma_start(seq(x_out, 2 * bb + i), xw[i][:, :, :]).then_inc(xw_stored[i], 16)
            for i in range(2):
                e.wait_ge(xw_stored[i], at(xw_stored[i], 64 * ps + 64))
                settle(e)

        def dve_exit(e, ps):
            with e.Fori(0, B // 2) as bb:
                for i in range(2):
                    e.wait_ge(xw_loaded[i], at(xw_loaded[i], 16 * bb + (64 + 64 * ps) + 16))
                    y = Y[:, bass.ds(8 * bb + 4 * i, NT), :].rearrange("p t d -> p (t d)")
                    x = xw[i][:, :, :].rearrange("p t d -> p (t d)")
                    e.scalar_tensor_tensor(x, y, 0.5, x, ALU.mult, ALU.add).then_inc(xw_mixed[i], 1)

        def flat(ap, lo, n):
            names = "abcde"[:len(ap.shape) - 1]
            return ap.rearrange("p " + " ".join(names) + " -> p (" + " ".join(names) + ")")[:, lo:lo + n]

        def cut(ap, n):
            return ap.rearrange("p (a c) -> p a c", a=n)

        z_T = cut(flat(sq[:, :, :], 0, KT * N), KT)
        kqT = cut(flat(qT[:, :, :, :], 0, 2 * N), 2)
        vt = cut(flat(qT[:, :, :, :], 2 * N, NT * D), NT)
        n_low = cut(flat(pr[:, :, :], 0, N), NT)
        n_up = cut(flat(pr[:, :, :], N, N), NT)
        a_up = cut(flat(pr[:, :, :], 2 * N, N), NT)
        inv = cut(flat(pr[:, :, :], 3 * N, N), NT)
        invT = cut(flat(pT[:, :, :, :], 0, N), NT)
        mx = cut(flat(pT[:, :, :, :], N, N), NT)
        m_up = [cut(flat(pT[:, :, :, :], (2 + i) * N, N), NT) for i in range(2)]
        state = flat(t2[:, :, :], 0, D)
        residue = flat(t2[:, :, :], D, D)
        errT = flat(t2[:, :, :], 2 * D, D)
        kn = cut(flat(t2[:, :, :], 3 * D, NT * DS), NT)
        wv = cut(flat(t1[:, :, :], 0, KT * D), KT)
        tw = cut(flat(t1[:, :, :], KT * D, KT * 2 * DS), KT)
        tri = cut(flat(v[:, :, :], 0, 11 * P), 11)
        bv = flat(v[:, :, :], 11 * P, D)
        tv = flat(v[:, :, :], 11 * P + D, 6)
        T_W = sem("ttt_weights", 0)
        T_ZERO = sem("ttt_zeroed")
        t_x, t_st, t_mv, t_va, t_rs = sem("ttt_x"), sem("ttt_stats"), sem("ttt_mv"), sem("ttt_var"), sem("ttt_rstd")
        t_z, t_h = sem("ttt_z"), sem("ttt_h")
        t_zt_ps, t_zt = sem("ttt_zT_ps"), sem("ttt_zT")
        t_kq_ps, t_kq = sem("ttt_kq_ps"), sem("ttt_kq")
        t_v_ps, t_v = sem("ttt_v_ps"), sem("ttt_v")
        t_kn_ps, t_kn = sem("ttt_kn_ps"), sem("ttt_kn")
        t_g_ps, t_g = sem("ttt_gram_ps"), sem("ttt_gram")
        t_m = sem("ttt_level_masked")
        t_p_ps, t_p = sem("ttt_mx_ps", 2), sem("ttt_mx")
        t_i_ps, t_i = sem("ttt_inverse_ps"), sem("ttt_inverse")
        t_r_ps, t_r = sem("ttt_r_ps"), sem("ttt_r")
        t_e_ps, t_e = sem("ttt_e_ps"), sem("ttt_e")
        t_y_ps, t_y = sem("ttt_y_ps"), sem("ttt_y")
        t_w_ps, t_w = sem("ttt_w_ps"), sem("ttt_w")
        LV = NLEV - 1

        h_flat = h[:, :, :].rearrange("p t d -> p (t d)")

        def sp_mid(e):
            e.wait_ge(xf_done, at(xf_done, idx(DEPTH - 1, B - 1, NT - 1) + 1))
            settle(e)
            for dst, name in ((wv, "wv"), (tw, "tw"), (tri, "tri"), (bv, "bv"), (tv, "tv")):
                e.dma_start(dst, A[name]).then_inc(T_W, 16)
            with e.Fori(0, B // 2) as bb:
                for i in range(2):
                    e.wait_ge(xw_stored[i], at(xw_stored[i], 16 * bb))
                    settle(e)
                    e.dma_start(xw[i][:, :, :], seq(x_in, 2 * bb + i)).then_inc(xw_loaded[i], 16)
                for i in range(2):
                    e.wait_ge(s_ln, at(s_ln, 8 * bb + 4 * i + 32 + 4))
                    settle(e)
                    e.dma_start(seq(x_out, 2 * bb + i), xw[i][:, :, :]).then_inc(xw_stored[i], 16)
            for i in range(2):
                e.wait_ge(xw_stored[i], at(xw_stored[i], 64))
                settle(e)

        T_ZERO0 = sem("ttt_zero_rows")
        T_DONE = sem("ttt_done")

        block = ctx.enter_context(nc.Block())

        @block.sync
        def _(e):
            def load_h(L, b):
                d = D // 2
                if L % 2 == 0:
                    e.wait_ge(s_ln, at(s_ln, 32 * (L // 2) + 4 * b + 4))
                    settle(e)
                else:
                    e.wait_ge(xf_done, at(xf_done, idx(L - 1, b, 3) + 1))
                    settle(e)
                e.wait_ge(ht_ps, at(ht_ps, idx(L, b, 0)))
                settle(e)
                e.dma_start(h[:, :, 0:d], xts(Y, b, 0, NT, 0, d)).then_inc(ha_loaded, 16)
                e.dma_start(h[1:P, :, d:D], xts(Y, b, 0, NT, d, D, 0, P - 1)).then_inc(ha_loaded, 16)
                e.dma_start(h[0:1, 1:NT, d:D], xts(Y, b, 0, NT - 1, d, D, P - 1, P)).then_inc(ha_loaded, 16)

            def load_h2(L, b, half):
                d = D // 2
                t = 2 * half
                e.wait_ge(xa_done, at(xa_done, idx(L, b, t + 1) + 1))
                settle(e)
                e.wait_ge(h2n_done, at(h2n_done, idx(L, b, t + 1) + 1 - 4))
                settle(e)
                q = h2_loaded[half]
                e.dma_start(h2[:, t:t + 2, 0:d], xts(Y, b, t, 2, 0, d)).then_inc(q, 16)
                e.dma_start(h2[1:P, t:t + 2, d:D], xts(Y, b, t, 2, d, D, 0, P - 1)).then_inc(q, 16)
                if half == 0:
                    e.dma_start(h2[0:1, 1:2, d:D], xts(Y, b, 0, 1, d, D, P - 1, P)).then_inc(q, 16)
                else:
                    e.dma_start(h2[0:1, 2:4, d:D], xts(Y, b, 1, 2, d, D, P - 1, P)).then_inc(q, 16)

            def sequence(L, b, nxt):
                if nxt:
                    load_h(*nxt)
                load_h2(L, b, 0)
                load_h2(L, b, 1)

            def transformer(ps):
                load_h(DEPTH * ps, 0)
                for L in range(DEPTH * ps, DEPTH * ps + DEPTH):
                    with e.Fori(0, B - 1) as b:
                        sequence(L, b, (L, b + 1))
                    last = L == DEPTH * ps + DEPTH - 1
                    sequence(L, B - 1, None if last else (L + 1, 0))

            w = s_w
            e.dma_start(ident[:, :], A["ident"]).then_inc(w, 16)
            e.dma_start(maskf[:, :], A["mask"]).then_inc(w, 16)
            e.dma_start(rot[:, 0, :, :, :].rearrange("p t f d -> p (t f d)"), A["rot"]).then_inc(w, 16)
            e.dma_start(rot[:, 1, :, :, :].rearrange("p t f d -> p (t f d)"), A["rot"]).then_inc(w, 16)
            e.dma_start(t1[:, 0, :], A["qks"]).then_inc(w, 16)
            e.dma_start(lng[:, :, :], A["lng"]).then_inc(w, 16)
            e.dma_start(lnb[:, :, :], A["lnb"]).then_inc(w, 16)
            e.dma_start(b1[:, :, :, :].rearrange("p a b c -> p (a b c)"), A["b1"]).then_inc(w, 16)
            e.dma_start(b2[:, :, :].rearrange("p a b -> p (a b)"), A["b2"]).then_inc(w, 16)
            for d in range(DEPTH):
                e.dma_start(wqkv[:, d, :, :], A["wqkv"][d].rearrange("(k p) n -> p k n", p=P)).then_inc(w, 16)
                e.dma_start(wo[:, d, :, :], A["wo"][d].rearrange("(k p) n -> p k n", p=P)).then_inc(w, 16)
                e.dma_start(w1[:, d, :, :], A["w1"][d].rearrange("(k p) n -> p k n", p=P)).then_inc(w, 16)
                e.dma_start(w2[:, d, 0:MT - 1, :], A["w2"][d, 0:(MT - 1) * P].rearrange("(k p) n -> p k n", p=P)).then_inc(w, 16)
            e.wait_ge(s_const, at(s_const, 4))
            for d in range(DEPTH):
                e.dma_start(w2[0:MLAST, d, MT - 1, :], A["w2"][d, (MT - 1) * P:]).then_inc(w, 16)
            e.wait_ge(s_const, at(s_const, 5))
            sp_entry(e)
            for ps in range(passes):
                transformer(ps)
                if ps == 0 and do_ttt:
                    sp_mid(e)
                else:
                    sp_exit(e, ps)
                if ps == 0 and do_ttt:
                    e.wait_ge(T_DONE, at(T_DONE, 1))

        @block.gpsimd
        def _(e):
            def A1(L, b, t, prev):
                n = idx(L, b, t)
                e.wait_ge(rotq, at(rotq, n + 1))
                e.wait_ge(qt_ps, at(qt_ps, n))
                e.tensor_tensor(qr[:, :], t1[:, 0, :], t2[:, 0, :], ALU.add).then_inc(qrot, 1)
                e.wait_ge(ss_done, at(ss_done, n + 1))
                settle(e)
                e.tensor_scalar(ssg[:, :], ss[:, :], 1e-24, None, ALU.max).then_inc(kr_step, 1)
                e.wait_ge(kr_step, at(kr_step, 2 * n + 1))
                if prev:
                    e.wait_ge(exp_done, at(exp_done, 4 * (n - 4 + 1)))
                e.tensor_tensor(r[:, t, :], ssg[:, :], small[:, 0:1].to_broadcast([P, 2 * HEADS]), ALU.pow).then_inc(r_done, 1)
                e.wait_ge(rotk, at(rotk, n + 1))
                e.wait_ge(kt_ps, at(kt_ps, n))
                e.tensor_tensor(kr[:, :], t1[:, 1, :], t2[:, 1, :], ALU.add).then_inc(kr_step, 1)
                e.wait_ge(kr_step, at(kr_step, 2 * n + 2))
                e.wait_ge(r_done, at(r_done, n + 1))
                e.tensor_tensor(kr[:, :].rearrange("p (h d) -> p h d", h=HEADS), kr[:, :].rearrange("p (h d) -> p h d", h=HEADS),
                                r[:, t, HEADS:].unsqueeze(2).to_broadcast([P, HEADS, DH]), ALU.mult).then_inc(krot, 1)

            def NP(L, b, t, j):
                n = idx(L, b, t)
                lo = 0 if t else WINDOW
                e.wait_ge(rden_done, at(rden_done, 4 * n + j + 1))
                e.tensor_tensor(pr[:, 2 * j:2 * j + 2, lo:], pr[:, 2 * j:2 * j + 2, lo:],
                                rden[:, 2 * j:2 * j + 2].unsqueeze(2).to_broadcast([P, 2, 2 * WINDOW - lo]), ALU.mult).then_inc(pn_done, 1)

            def XB(L, b, t):
                n, dd = idx(L, b, t), L % 2
                e.wait_ge(xa_done, at(xa_done, n + 1))
                e.wait_ge(xf_done, at(xf_done, n + 1 - 4))
                e.tensor_tensor(xb[:, t, :], xt(Y, b, t), b2[:, dd, :], ALU.add).then_inc(xb_done, 1)

            def LN(L, b, half):
                e.wait_ge(mv_done, at(mv_done, idx(L, b, 2 * half + 1) + 1))
                sl = slice(2 * half, 2 * half + 2)
                settle(e)
                e.tensor_scalar(vare[:, sl], mv[:, sl, 1], LN_EPS, None, ALU.add).then_inc(s_pln, 1)
                e.wait_ge(s_pln, at(s_pln, 2 * b + (16 * L + half + 1)))
                e.tensor_tensor(rs[:, sl], vare[:, sl], small[:, 0:1].to_broadcast([P, 2]), ALU.pow).then_inc(rs_done, 1)

            def sequence(L, b, nxt):
                for t in range(NT):
                    for j in range(4):
                        NP(L, b, t, j)
                    if nxt and t:
                        A1(*nxt, t - 1, True)
                    XB(L, b, t)
                if nxt:
                    A1(*nxt, 3, True)
                LN(L, b, 0)
                LN(L, b, 1)

            def transformer(ps):
                for t in range(NT):
                    A1(DEPTH * ps, 0, t, False)
                for L in range(DEPTH * ps, DEPTH * ps + DEPTH):
                    with e.Fori(0, B - 1) as b:
                        sequence(L, b, (L, b + 1))
                    last = L == DEPTH * ps + DEPTH - 1
                    sequence(L, B - 1, None if last else (L + 1, 0))

            def ttt(bb, i):
                g = 2 * bb + i

                def rstd(k):
                    e.wait_ge(t_mv, at(t_mv, 3 * g + k + 1))
                    settle(e)
                    e.tensor_scalar(va0[:, :], mv0[:, :, 1], LN_EPS, None, ALU.add).then_inc(t_va, 1)
                    e.wait_ge(t_va, at(t_va, 3 * g + k + 1))
                    e.tensor_tensor(rs0[:, :], va0[:, :], small[:, 0:1].to_broadcast([P, NT]), ALU.pow).then_inc(t_rs, 1)

                rstd(0)
                rstd(1)
                e.wait_ge(t_w, at(t_w, NT * g))
                e.wait_ge(t_y_ps, at(t_y_ps, NT * g))
                settle(e)
                e.memset(state, 0.0).then_inc(T_ZERO, 1)
                e.wait_ge(t_g, at(t_g, g + 1))
                for l in range(LV):
                    e.wait_ge(t_p_ps, at(t_p_ps, LV * g + l - 1))
                    e.tensor_tensor(m_up[l % 2], n_up, tri[:, 5 + l:6 + l, :].to_broadcast([P, NT, P]), ALU.mult).then_inc(t_m, 1)
                rstd(2)

            e.memset(small[:, 0:1], -0.5).then_inc(s_const, 1)
            e.memset(kT[:, :, :, :, :], 0.0)
            e.memset(uT0[:, MT - 1, :], 0.0)
            e.memset(h[0:1, 0, :], 0.0)
            e.memset(h2[0:1, 0, :], 0.0)
            e.memset(w2[:, :, MT - 1, :], 0.0).then_inc(s_const, 3)
            e.wait_ge(s_const, at(s_const, 4))
            for made, credit in credits.values():
                if credit:
                    e.sem_inc(made, credit)
            e.sem_inc(s_const, 1)
            pool_entry(e)
            for ps in range(passes):
                e.wait_ge(s_const, at(s_const, 8))
                transformer(ps)
                if ps == 0 and do_ttt:
                    e.wait_ge(xf_done, at(xf_done, idx(DEPTH - 1, B - 1, NT - 1) + 1))
                    e.memset(flat(qT[:, :, :, :], 0, 2 * N)[64:P, :], 0.0).then_inc(T_ZERO0, 1)
                    with e.Fori(0, B // 2) as bb:
                        for i in range(2):
                            ttt(bb, i)

        @block.scalar
        def _(e):
            def A1(L, b, t, prev):
                n = idx(L, b, t)
                e.wait_ge(ht_ps, at(ht_ps, n + 1))
                if t >= 2 or prev:
                    e.wait_ge(v_ps, at(v_ps, n - 1))
                e.activation(hT[:, t % 2, :, :].rearrange("p k c -> p (k c)"), bank[7][:, 0:D], ACT.Copy).then_inc(ht_sb, 1)
                e.wait_ge(ss_done, at(ss_done, n))
                e.wait_ge(q_ps, at(q_ps, n + 1))
                e.activation(sq[:, 0, :], bank[0][:, :], ACT.Square).then_inc(sqq, 1)
                e.wait_ge(k_ps, at(k_ps, n + 1))
                e.activation(sq[:, 1, :], bank[1][:, :], ACT.Square).then_inc(sqk, 1)

            def V(L, b, t, prev):
                n = idx(L, b, t)
                e.wait_ge(v_ps, at(v_ps, n + 1))
                if prev:
                    e.wait_ge(pv_ps, at(pv_ps, n - 4 + (2 if t < 3 else 1)))
                e.activation(v[:, t, :], bank[2][:, :], ACT.Copy).then_inc(v_sb, 1)

            def A2(L, b, t, prev):
                n = idx(L, b, t)
                e.wait_ge(qt_ps, at(qt_ps, n + 1))
                if prev:
                    e.wait_ge(s_ps, at(s_ps, 4 * (n - 4 + (2 if t < 3 else 1))))
                e.activation(qT[:, :, t, :], bank[6][:, :].rearrange("p (a c) -> p a c", a=PAIRS), ACT.Copy).then_inc(qt_sb, 1)
                e.wait_ge(kt_ps, at(kt_ps, n + 1))
                e.activation(kT[0:64, :, 0, t, :], bank[5][0:64, :].rearrange("p (a c) -> p a c", a=PAIRS), ACT.Copy).then_inc(ktlo_sb, 1)

            def S(L, b, t):
                n = idx(L, b, t)
                lo = 0 if t else WINDOW
                for j in range(4):
                    e.wait_ge(nb_done, at(nb_done, 4 * n + j + 1))
                    e.wait_ge(pt_ps, at(pt_ps, 4 * (n - 1) + j + 1))
                    if j == 0:
                        e.wait_ge(rden_done, at(rden_done, 4 * n))
                    if j == 0 and t == 0:
                        e.wait_ge(w2_ps, at(w2_ps, n))
                    for g in range(2):
                        hd = 2 * j + g
                        m = e.activation(pr[:, hd, lo:], bank[j][:, g * 256 + lo:(g + 1) * 256], ACT.Exp,
                                         bias=nb[:, hd:hd + 1], scale=r[:, t, hd:hd + 1], accum_out=den[:, hd:hd + 1])
                    m.then_inc(exp_done, 1)

            def PT(L, b, t, j):
                n = idx(L, b, t)
                e.wait_ge(pt_ps, at(pt_ps, 4 * n + j + 1))
                e.wait_ge(pv_ps, at(pv_ps, n))
                w = 0 if t else 1
                e.activation(pT[:, 2 * j:2 * j + 2, w:, :],
                             bank[4][:, :].rearrange("p (h w c) -> p h w c", h=2, w=2)[:, :, w:, :], ACT.Copy).then_inc(pte_sb, 1)

            def O(L, b, t):
                n = idx(L, b, t)
                e.wait_ge(pv_ps, at(pv_ps, n + 1))
                e.wait_ge(wo_ps, at(wo_ps, n))
                e.activation(oT[:, :, :].rearrange("p a c -> p (a c)"), bank[6][:, :], ACT.Copy).then_inc(o_sb, 1)

            def H2T(L, b, half):
                dd = L % 2
                e.wait_ge(h2t_ps, at(h2t_ps, 2 * b + (16 * L + half + 1)))
                e.wait_ge(w1_ps, at(w1_ps, 12 * b + (96 * L + 6 * half + 6 - 12)))
                for k in range(KT):
                    m = e.activation(h2T[:, half, k, :], bank[4][:, k * 256:(k + 1) * 256], ACT.Identity,
                                     bias=lnb[:, dd, k:k + 1], scale=lng[:, dd, k:k + 1])
                m.then_inc(h2t_sb, 1)

            def G(L, b, half):
                dd = L % 2
                for mt in range(MT):
                    job = 6 * half + mt
                    ms = P if mt < MT - 1 else MLAST
                    e.wait_ge(w1_ps, at(w1_ps, 12 * b + (96 * L + job + 1)))
                    e.wait_ge(u_done, at(u_done, 12 * b + (96 * L + job - 1)))
                    e.activation(gg[0:ms, job % 2, :], bank[job % 4][0:ms, 256:512], ACT.Gelu,
                                 bias=b1[0:ms, dd, 1, mt:mt + 1]).then_inc(gelu_done, 1)

            def sequence(L, b, nxt):
                for t in range(NT):
                    S(L, b, t)
                    if nxt and t:
                        A1(*nxt, t - 1, True)
                    PT(L, b, t, 0)
                    PT(L, b, t, 2)
                    O(L, b, t)
                    if nxt and t:
                        A2(*nxt, t - 1, True)
                        V(*nxt, t - 1, True)
                if nxt:
                    A1(*nxt, 3, True)
                    V(*nxt, 3, True)
                H2T(L, b, 0)
                H2T(L, b, 1)
                G(L, b, 0)
                if nxt:
                    A2(*nxt, 3, True)
                G(L, b, 1)

            def transformer(ps):
                for t in range(NT):
                    A1(DEPTH * ps, 0, t, False)
                    A2(DEPTH * ps, 0, t, False)
                    V(DEPTH * ps, 0, t, False)
                for L in range(DEPTH * ps, DEPTH * ps + DEPTH):
                    with e.Fori(0, B - 1) as b:
                        sequence(L, b, (L, b + 1))
                    last = L == DEPTH * ps + DEPTH - 1
                    sequence(L, B - 1, None if last else (L + 1, 0))

            def ttt(bb, i):
                g = 2 * bb + i
                for k in range(KT):
                    e.wait_ge(t_zt_ps, at(t_zt_ps, 2 * g + k + 1))
                    m = e.activation(z_T[:, k, :], bank[k][:, :], ACT.Identity, bias=tv[:, KT + k:KT + k + 1], scale=tv[:, k:k + 1])
                m.then_inc(t_zt, 1)
                for k in range(2):
                    e.wait_ge(t_kq_ps, at(t_kq_ps, 2 * g + k + 1))
                    if k == 0:
                        e.wait_ge(t_y_ps, at(t_y_ps, NT * g))
                    m = e.activation(kqT[0:DS, k, :], bank[2 + k][0:DS, :], ACT.Identity, bias=tv[0:DS, 2 * KT + k:2 * KT + k + 1])
                m.then_inc(t_kq, 1)
                e.wait_ge(t_kn_ps, at(t_kn_ps, g + 1))
                e.activation(kn.rearrange("p a c -> p (a c)"), bank[0][:, 0:NT * DS], ACT.Copy, scale=-TTT_LR).then_inc(t_kn, 1)
                for l in range(LV):
                    e.wait_ge(t_p_ps, at(t_p_ps, LV * g + l + 1))
                    e.wait_ge(t_i_ps, at(t_i_ps, LV * g + l))
                    e.activation(mx.rearrange("p a c -> p (a c)"), bank[0 + l % 2][:, :], ACT.Copy).then_inc(t_p, 1)
                for c in range(NT):
                    k = NT * g + c
                    e.wait_ge(t_e_ps, at(t_e_ps, k + 1))
                    e.wait_ge(t_y_ps, at(t_y_ps, k))
                    e.activation(errT, bank[1][:, 0:D], ACT.Copy).then_inc(t_e, 1)

            e.wait_ge(s_const, at(s_const, 8))
            for ps in range(passes):
                transformer(ps)
                if ps == 0 and do_ttt:
                    e.wait_ge(T_ZERO0, at(T_ZERO0, 1))
                    e.wait_ge(T_W, at(T_W, 16 * 5))
                    with e.Fori(0, B // 2) as bb:
                        for i in range(2):
                            ttt(bb, i)

        @block.tensor
        def _(e):
            def A1(L, b, t, prev):
                n = idx(L, b, t)
                dd = L % 2
                if t == 0:
                    e.wait_ge(ha_loaded, at(ha_loaded, 48 * b + (48 * 8 * L + 48)))
                e.wait_ge(ht_sb, at(ht_sb, n))
                if prev:
                    e.wait_ge(xa_done, at(xa_done, n - 3))
                for k in range(KT):
                    m = e.transpose(bank[7][:, k * P:(k + 1) * P], h[:, t, k * P:(k + 1) * P], ident[:, :])
                m.then_inc(ht_ps, 1)
                for i, (done, used, bk) in enumerate(((q_ps, (rotq, sqq), 0), (k_ps, (rotk, sqk), 1), (v_ps, (v_sb,), 2))):
                    if i == 0:
                        e.wait_ge(ht_sb, at(ht_sb, n + 1))
                    for u in used:
                        e.wait_ge(u, at(u, n))
                    if prev:
                        e.wait_ge(exp_done, at(exp_done, 4 * (n - 4 + (1 if t < 3 else 0)) + i + 1))
                    for k in range(KT):
                        m = e.matmul(bank[bk][:, :], hT[:, t % 2, k, :], wqkv[:, dd, k, i * INNER:(i + 1) * INNER],
                                     start=(k == 0), stop=(k == KT - 1))
                    m.then_inc(done, 1)

            def A2(L, b, t, prev):
                n = idx(L, b, t)
                e.wait_ge(qrot, at(qrot, n + 1))
                e.wait_ge(qt_sb, at(qt_sb, n))
                if prev:
                    e.wait_ge(o_sb, at(o_sb, n - 4 + (2 if t < 3 else 1)))
                for p in range(PAIRS):
                    m = e.transpose(bank[6][:, p * P:(p + 1) * P], qr[:, p * P:(p + 1) * P], ident[:, :])
                m.then_inc(qt_ps, 1)
                e.wait_ge(krot, at(krot, n + 1))
                e.wait_ge(ktlo_sb, at(ktlo_sb, n))
                e.wait_ge(kthi_sb, at(kthi_sb, n))
                if prev:
                    e.wait_ge(pto_sb, at(pto_sb, 2 * (n - 4 + (2 if t < 3 else 1))))
                for p in range(PAIRS):
                    m = e.transpose(bank[5][:, p * P:(p + 1) * P], kr[:, p * P:(p + 1) * P], ident[:, :])
                m.then_inc(kt_ps, 1)

            def S(L, b, t, nxt):
                n = idx(L, b, t)
                if t == 0:
                    nA = n + 4
                    e.wait_ge(u_done, at(u_done, 12 * b + 96 * L))
                elif t >= 2 and nxt:
                    nA = n + 3
                else:
                    nA = None
                e.wait_ge(qt_sb, at(qt_sb, n + 1))
                e.wait_ge(ktlo_sb, at(ktlo_sb, n + 1))
                e.wait_ge(kthi_sb, at(kthi_sb, n + 1))
                lo = 0 if t else WINDOW
                for j in range(4):
                    e.wait_ge(exp_done, at(exp_done, 4 * (n - 1) + j + 1))
                    if nA is not None:
                        for u in ((rotq, sqq), (rotk, sqk), (v_sb,), ())[j]:
                            e.wait_ge(u, at(u, nA))
                    out = bank[j][:, :].rearrange("p (h k) -> p h k", h=2)[:, :, lo:]
                    e.matmul(out, identb[:, :], maskb[:, :, lo:], start=True, stop=False)
                    for g in range(2):
                        rhs = kT[:, j, g, t - 1:t + 1, :] if t else kT[:, j, g, 0, :]
                        m = e.matmul(bank[j][:, g * 256 + lo:(g + 1) * 256], qT[:, j, t, :], rhs,
                                     start=False, stop=(g == 1))
                    m.then_inc(s_ps, 1)

            def PT(L, b, t, j, nxt):
                n = idx(L, b, t)
                k, bk = j // 2, 4 + j % 2
                nA = n + 4 if t == 0 else (n + 3 if (t >= 2 and nxt) else None)
                e.wait_ge(pn_done, at(pn_done, 4 * n + j + 1))
                e.wait_ge(pto_sb if j % 2 else pte_sb, at(pto_sb if j % 2 else pte_sb, 2 * n + k))
                if k == 0 and j == 0 and t == 0:
                    e.wait_ge(h2t_sb, at(h2t_sb, 2 * b + 16 * L))
                if k == 0 and j == 1 and nA is not None:
                    e.wait_ge(ktlo_sb, at(ktlo_sb, nA))
                    e.wait_ge(kthi_sb, at(kthi_sb, nA))
                for g in range(2):
                    for w in ((0, 1) if t else (1,)):
                        m = e.transpose(bank[bk][:, (2 * g + w) * P:(2 * g + w + 1) * P],
                                        pr[:, 2 * j + g, w * P:(w + 1) * P], ident[:, :])
                m.then_inc(pt_ps, 1)

            def PV(L, b, t, j, nxt):
                n = idx(L, b, t)
                if j == 0:
                    e.wait_ge(v_sb, at(v_sb, n + 1))
                    e.wait_ge(o_sb, at(o_sb, n))
                    if t == 0:
                        e.wait_ge(qt_sb, at(qt_sb, n + 4))
                        e.wait_ge(xf_done, at(xf_done, idx(L, b, 3) + 1 - 4))
                    elif t >= 2 and nxt:
                        e.wait_ge(qt_sb, at(qt_sb, n + 3))
                e.wait_ge(pto_sb if j % 2 else pte_sb, at(pto_sb if j % 2 else pte_sb, 2 * n + j // 2 + 1))
                for g in range(2):
                    hd = 2 * j + g
                    ws = (0, 1) if t else (1,)
                    for w in ws:
                        m = e.matmul(bank[6][64 * g:64 * g + 64, j * P:(j + 1) * P],
                                     v[:, t - 1 + w, hd * DH:(hd + 1) * DH], pT[:, hd, w, :],
                                     start=(w == ws[0]), stop=(w == 1))
                if j == 3:
                    m.then_inc(pv_ps, 1)

            def WO(L, b, t, nxt):
                n = idx(L, b, t)
                e.wait_ge(o_sb, at(o_sb, n + 1))
                if t == 0 or nxt:
                    e.wait_ge(ht_sb, at(ht_sb, n + 4))
                e.wait_ge(xa_done, at(xa_done, n))
                for p in range(PAIRS):
                    m = e.matmul(bank[7][:, 0:D], oT[:, p, :], wo[:, L % 2, p, :], start=(p == 0), stop=(p == PAIRS - 1))
                m.then_inc(wo_ps, 1)

            def H2T(L, b, half):
                e.wait_ge(h2n_done, at(h2n_done, idx(L, b, 2 * half + 1) + 1))
                e.wait_ge(pte_sb, at(pte_sb, 2 * (idx(L, b, 3) + 1)))
                e.wait_ge(h2t_sb, at(h2t_sb, 2 * b + (16 * L + half)))
                for k in range(KT):
                    for i in range(2):
                        m = e.transpose(bank[4][:, (2 * k + i) * P:(2 * k + i + 1) * P],
                                        h2n[:, 2 * half + i, k * P:(k + 1) * P], ident[:, :])
                m.then_inc(h2t_ps, 1)

            def W1(L, b, half, nxt):
                dd = L % 2
                e.wait_ge(h2t_sb, at(h2t_sb, 2 * b + (16 * L + half + 1)))
                for mt in range(MT):
                    job = 6 * half + mt
                    if job < 4:
                        e.wait_ge(exp_done, at(exp_done, 4 * idx(L, b, 3) + 4))
                        if nxt:
                            for u in ((rotq, sqq), (rotk, sqk), (v_sb,), ())[job]:
                                e.wait_ge(u, at(u, idx(L, b, 3) + 5))
                    else:
                        e.wait_ge(u_done, at(u_done, 12 * b + (96 * L + job - 3)))
                    ms = P if mt < MT - 1 else MLAST
                    for g in range(2):
                        for k in range(KT):
                            m = e.matmul(bank[mt_bank(job)][0:ms, g * 256:(g + 1) * 256],
                                         w1[:, dd, k, g * HID + mt * P:g * HID + mt * P + ms],
                                         h2T[:, half, k, :], start=(k == 0), stop=(k == KT - 1))
                    m.then_inc(w1_ps, 1)

            def W2(L, b, t, nxt):
                n, dd = idx(L, b, t), L % 2
                e.wait_ge(u_done, at(u_done, 12 * b + (96 * L + 6 * (t // 2) + 6)))
                if t < 2:
                    if t == 0:
                        e.wait_ge(o_sb, at(o_sb, n + 4))
                        if nxt:
                            e.wait_ge(qt_sb, at(qt_sb, n + 8))
                    else:
                        e.wait_ge(xa_done, at(xa_done, n + 3))
                        if nxt:
                            e.wait_ge(ht_sb, at(ht_sb, n + 7))
                else:
                    e.wait_ge(xf_done, at(xf_done, n - 1))
                for mt in range(MT):
                    m = e.matmul(bank[6 + t % 2][:, 0:D], uT[t // 2][:, mt, (t % 2) * P:(t % 2 + 1) * P],
                                 w2[:, dd, mt, :], start=(mt == 0), stop=(mt == MT - 1))
                m.then_inc(w2_ps, 1)

            def sequence(L, b, nxt):
                more = bool(nxt)
                for t in range(NT):
                    S(L, b, t, more)
                    if nxt and t:
                        A1(*nxt, t - 1, True)
                    PT(L, b, t, 0, more)
                    for j in range(1, 4):
                        PT(L, b, t, j, more)
                        PV(L, b, t, j - 1, more)
                    PV(L, b, t, 3, more)
                    if nxt and t:
                        A2(*nxt, t - 1, True)
                    WO(L, b, t, more)
                if nxt:
                    A1(*nxt, 3, True)
                H2T(L, b, 0)
                H2T(L, b, 1)
                W1(L, b, 0, more)
                if nxt:
                    A2(*nxt, 3, True)
                W1(L, b, 1, more)
                for t in range(NT):
                    W2(L, b, t, more)

            def transformer(ps):
                for t in range(NT):
                    A1(DEPTH * ps, 0, t, False)
                    A2(DEPTH * ps, 0, t, False)
                for L in range(DEPTH * ps, DEPTH * ps + DEPTH):
                    with e.Fori(0, B - 1) as b:
                        sequence(L, b, (L, b + 1))
                    last = L == DEPTH * ps + DEPTH - 1
                    sequence(L, B - 1, None if last else (L + 1, 0))

            def ttt(bb, i):
                g = 2 * bb + i
                e.wait_ge(t_h, at(t_h, g + 1))
                e.wait_ge(t_e, at(t_e, NT * g))
                for k in range(KT):
                    for t in range(NT):
                        m = e.transpose(bank[k][:, t * P:(t + 1) * P], h[:, t, k * P:(k + 1) * P], ident[:, :])
                    m.then_inc(t_zt_ps, 1)
                e.wait_ge(t_zt, at(t_zt, g + 1))
                e.wait_ge(t_w, at(t_w, NT * g))
                e.wait_ge(t_y, at(t_y, NT * g))
                for f in range(2):
                    for k in range(KT):
                        m = e.matmul(bank[2 + f][0:DS, :], tw[:, k, f * DS:(f + 1) * DS], z_T[:, k, :], start=(k == 0), stop=(k == KT - 1))
                    m.then_inc(t_kq_ps, 1)
                for c in range(NT):
                    for k in range(KT):
                        m = e.matmul(bank[4 + c // 2][:, (c % 2) * D:(c % 2 + 1) * D], z_T[:, k, c * P:(c + 1) * P], wv[:, k, :],
                                     start=(k == 0), stop=(k == KT - 1))
                    if c % 2:
                        m.then_inc(t_v_ps, 1)
                e.wait_ge(t_kq, at(t_kq, g + 1))
                settle(e)
                for c in range(NT):
                    m = e.transpose(bank[0][:, c * DS:(c + 1) * DS], kqT[0:DS, 0, c * P:(c + 1) * P], ident[0:DS, 0:DS])
                m.then_inc(t_kn_ps, 1)
                for c in range(NT):
                    m = e.matmul(bank[6 + c // 2][:, (c % 2) * 256:(c % 2 + 1) * 256], kqT[:, 0, c * P:(c + 1) * P], kqT[:, :, c * P:(c + 1) * P],
                                 start=True, stop=True)
                    if c % 2:
                        m.then_inc(t_g_ps, 1)
                e.wait_ge(t_kn, at(t_kn, g + 1))
                for l in range(LV):
                    e.wait_ge(t_m, at(t_m, LV * g + l + 1))
                    e.wait_ge(t_i, at(t_i, (LV + 2) * g + l + 2))
                    for c in range(NT):
                        m = e.matmul(bank[l % 2][:, c * P:(c + 1) * P], m_up[l % 2][:, c, :], inv[:, c, :], start=True, stop=True)
                    m.then_inc(t_p_ps, 1)
                    e.wait_ge(t_p, at(t_p, LV * g + l + 1))
                    for c in range(NT):
                        if l < LV - 1:
                            e.matmul(bank[2][:, c * P:(c + 1) * P], invT[:, c, :], mx[:, c, :], start=True, stop=True)
                        m = e.matmul(bank[3][:, c * P:(c + 1) * P], mx[:, c, :], invT[:, c, :], start=True, stop=True)
                    m.then_inc(t_i_ps, 1)
                e.wait_ge(t_i, at(t_i, (LV + 2) * g + LV + 2))
                e.wait_ge(T_ZERO, at(T_ZERO, g + 1))
                for c in range(NT):
                    k = NT * g + c
                    e.wait_ge(t_w, at(t_w, k))
                    e.wait_ge(t_r, at(t_r, k))
                    e.matmul(bank[0][:, 0:D], kqT[:, 0, c * P:(c + 1) * P], state, start=True, stop=True).then_inc(t_r_ps, 1)
                    e.wait_ge(t_r, at(t_r, k + 1))
                    e.wait_ge(t_e, at(t_e, k))
                    e.matmul(bank[1][:, 0:D], invT[:, c, :], residue, start=True, stop=True).then_inc(t_e_ps, 1)
                    e.wait_ge(t_y, at(t_y, k))
                    e.matmul(bank[3][:, 0:D], kqT[:, 1, c * P:(c + 1) * P], state, start=True, stop=False)
                    e.wait_ge(t_e, at(t_e, k + 1))
                    e.matmul(bank[3][:, 0:D], a_up[:, c, :], errT, start=False, stop=True).then_inc(t_y_ps, 1)
                    e.matmul(bank[2][0:DS, 0:D], kn[:, c, :], errT, start=True, stop=True).then_inc(t_w_ps, 1)

            e.wait_ge(s_const, at(s_const, 8))
            for ps in range(passes):
                transformer(ps)
                if ps == 0 and do_ttt:
                    e.wait_ge(T_ZERO0, at(T_ZERO0, 1))
                    e.wait_ge(T_W, at(T_W, 16 * 5))
                    with e.Fori(0, B // 2) as bb:
                        for i in range(2):
                            ttt(bb, i)

        @block.vector
        def _(e):
            def A1(L, b, t, prev):
                n, dd = idx(L, b, t), L % 2

                def heads(ap):
                    return ap.rearrange("p (h c j) -> p h c j", h=HEADS, c=2)

                for i, (squared, bk, done, added) in enumerate(((sqq, 0, rotq, qrot), (sqk, 1, rotk, krot))):
                    e.wait_ge(squared, at(squared, n + 1))
                    e.wait_ge(added, at(added, n))
                    cosf = rot[:, dd, t, 2 * i, :].rearrange("p (c j) -> p c j", c=2)
                    sinf = rot[:, dd, t, 2 * i + 1, :].rearrange("p (c j) -> p c j", c=2)
                    e.tensor_tensor(t1[:, i, :].rearrange("p (h d) -> p h d", h=HEADS),
                                    bank[bk][:, :].rearrange("p (h d) -> p h d", h=HEADS),
                                    rot[:, dd, t, 2 * i:2 * i + 1, :].to_broadcast([P, HEADS, DH]), ALU.mult)
                    e.tensor_tensor(heads(t2[:, i, :]), heads(bank[bk][:, :])[:, :, ::-1, :],
                                    rot[:, dd, t, 2 * i + 1:2 * i + 2, :].to_broadcast([P, HEADS, DH]).rearrange("p h (c j) -> p h c j", c=2),
                                    ALU.mult).then_inc(done, 1)
                e.wait_ge(sqq, at(sqq, n + 1))
                e.wait_ge(sqk, at(sqk, n + 1))
                e.wait_ge(r_done, at(r_done, n))
                e.tensor_reduce(ss[:, :], sq[:, :, :].rearrange("p a (h d) -> p (a h) d", h=HEADS), AX.X, ALU.add).then_inc(ss_done, 1)

            def A2(L, b, t, prev):
                n = idx(L, b, t)
                e.wait_ge(kt_ps, at(kt_ps, n + 1))
                if prev:
                    e.wait_ge(s_ps, at(s_ps, 4 * (n - 4 + (2 if t < 3 else 1))))
                e.tensor_copy(kT[64:P, :, 1, t, :], bank[5][64:P, :].rearrange("p (a c) -> p a c", a=PAIRS)).then_inc(kthi_sb, 1)

            def S(L, b, t):
                n = idx(L, b, t)
                lo = 0 if t else WINDOW
                e.wait_ge(r_done, at(r_done, n + 1))
                for j in range(4):
                    e.wait_ge(s_ps, at(s_ps, 4 * n + j + 1))
                    e.tensor_reduce(nm[:, 2 * j:2 * j + 2], bank[j][:, :].rearrange("p (h k) -> p h k", h=2)[:, :, lo:],
                                    AX.X, ALU.max, negate=True).then_inc(negmax_done, 1)
                    e.wait_ge(exp_done, at(exp_done, 4 * (n - 1) + j + 1))
                    e.wait_ge(negmax_done, at(negmax_done, 4 * n + j + 1))
                    e.tensor_tensor(nb[:, 2 * j:2 * j + 2], nm[:, 2 * j:2 * j + 2], r[:, t, 2 * j:2 * j + 2], ALU.mult).then_inc(nb_done, 1)

            def R(L, b, t, j):
                n = idx(L, b, t)
                e.wait_ge(exp_done, at(exp_done, 4 * n + j + 1))
                e.wait_ge(pn_done, at(pn_done, 4 * n + j - 3))
                e.reciprocal(rden[:, 2 * j:2 * j + 2], den[:, 2 * j:2 * j + 2]).then_inc(rden_done, 1)

            def PT(L, b, t, j):
                n = idx(L, b, t)
                e.wait_ge(pt_ps, at(pt_ps, 4 * n + j + 1))
                e.wait_ge(pv_ps, at(pv_ps, n))
                w = 0 if t else 1
                e.tensor_copy(pT[:, 2 * j:2 * j + 2, w:, :],
                              bank[5][:, :].rearrange("p (h w c) -> p h w c", h=2, w=2)[:, :, w:, :]).then_inc(pto_sb, 1)

            def WO(L, b, t):
                n = idx(L, b, t)
                e.wait_ge(wo_ps, at(wo_ps, n + 1))
                e.tensor_tensor(xt(Y, b, t), bank[7][:, 0:D], xt(Y, b, t), ALU.add).then_inc(xa_done, 1)

            def LN(L, b, half):
                g = 8 * L
                for t in (2 * half, 2 * half + 1):
                    n = idx(L, b, t)
                    if t == 2 * half:
                        e.wait_ge(h2_loaded[half], at(h2_loaded[half], 48 * b + (48 * 8 * L + 48)))
                    e.bn_stats(st[:, t, :], h2[:, t, :]).then_inc(st_done, 1)
                for t in (2 * half, 2 * half + 1):
                    n = idx(L, b, t)
                    e.wait_ge(st_done, at(st_done, n + 1))
                    settle(e)
                    e.bn_aggr(mv[:, t, :], st[:, t, :]).then_inc(mv_done, 1)
                for t in (2 * half, 2 * half + 1):
                    n = idx(L, b, t)
                    if t == 2 * half:
                        e.wait_ge(mv_done, at(mv_done, n + 1))
                        e.wait_ge(rs_done, at(rs_done, 2 * b + (16 * L + half + 1)))
                        e.wait_ge(h2t_ps, at(h2t_ps, 2 * b + (16 * L + half + 1 - 2)))
                    e.tensor_scalar(h2n[:, t, :], h2[:, t, :], mv[:, t, 0:1], rs[:, t:t + 1], ALU.subtract, ALU.mult).then_inc(h2n_done, 1)

            def U(L, b, half):
                dd = L % 2
                for mt in range(MT):
                    job = 6 * half + mt
                    ms = P if mt < MT - 1 else MLAST
                    e.wait_ge(gelu_done, at(gelu_done, 12 * b + (96 * L + job + 1)))
                    if mt == 0 and half == 0:
                        e.wait_ge(w2_ps, at(w2_ps, idx(L, b, 1) + 1 - 4))
                    if mt == 0 and half == 1:
                        e.wait_ge(pt_ps, at(pt_ps, 4 * idx(L, b, 3) + 4))
                    e.scalar_tensor_tensor(uT[half][0:ms, mt, :], bank[job % 4][0:ms, 0:256], b1[0:ms, dd, 0, mt:mt + 1],
                                           gg[0:ms, job % 2, :], ALU.add, ALU.mult).then_inc(u_done, 1)

            def W2(L, b, t):
                n = idx(L, b, t)
                e.wait_ge(w2_ps, at(w2_ps, n + 1))
                e.wait_ge(xb_done, at(xb_done, n + 1))
                e.tensor_tensor(xt(Y, b, t), bank[6 + t % 2][:, 0:D], xb[:, t, :], ALU.add).then_inc(xf_done, 1)

            def sequence(L, b, nxt):
                for t in range(NT):
                    S(L, b, t)
                    for j in range(4):
                        R(L, b, t, j)
                    if nxt and t:
                        A1(*nxt, t - 1, True)
                    PT(L, b, t, 1)
                    PT(L, b, t, 3)
                    if nxt and t:
                        A2(*nxt, t - 1, True)
                    WO(L, b, t)
                if nxt:
                    A1(*nxt, 3, True)
                LN(L, b, 0)
                LN(L, b, 1)
                U(L, b, 0)
                if nxt:
                    A2(*nxt, 3, True)
                U(L, b, 1)
                for t in range(NT):
                    W2(L, b, t)

            def transformer(ps):
                for t in range(NT):
                    A1(DEPTH * ps, 0, t, False)
                    A2(DEPTH * ps, 0, t, False)
                for L in range(DEPTH * ps, DEPTH * ps + DEPTH):
                    with e.Fori(0, B - 1) as b:
                        sequence(L, b, (L, b + 1))
                    last = L == DEPTH * ps + DEPTH - 1
                    sequence(L, B - 1, None if last else (L + 1, 0))

            def ttt(bb, i):
                g, x = 2 * bb + i, xw[i]

                def norm(src, dst, k):
                    for t in range(NT):
                        m = e.bn_stats(st0[:, t, :], src[t])
                    m.then_inc(t_st, 1)
                    e.wait_ge(t_st, at(t_st, 3 * g + k + 1))
                    settle(e)
                    for t in range(NT):
                        m = e.bn_aggr(mv0[:, t, :], st0[:, t, :])
                    m.then_inc(t_mv, 1)
                    e.wait_ge(t_mv, at(t_mv, 3 * g + k + 1))
                    e.wait_ge(t_rs, at(t_rs, 3 * g + k + 1))
                    for t in range(NT):
                        m = e.tensor_scalar(dst[t], src[t], mv0[:, t, 0:1], rs0[:, t:t + 1], ALU.subtract, ALU.mult)
                    return m

                y = Y[:, bass.ds(8 * bb + 4 * i, NT), :].rearrange("p t d -> p (t d)")
                xf = x[:, :, :].rearrange("p t d -> p (t d)")
                ys = [xt(Y, 2 * bb + i, t) for t in range(NT)]
                xs = [x[:, t, :] for t in range(NT)]
                e.wait_ge(xw_loaded[i], at(xw_loaded[i], 16 * bb + 64 + 16))
                e.scalar_tensor_tensor(xf, y, 0.5, xf, ALU.mult, ALU.add).then_inc(t_x, 1)
                e.wait_ge(t_x, at(t_x, 2 * g + 1))
                norm(xs, ys, 0).then_inc(t_z, 1)
                e.wait_ge(t_z, at(t_z, 2 * g + 1))
                e.tensor_tensor(xf, xf, y, ALU.add).then_inc(t_x, 1)
                norm(ys, ys, 1).then_inc(t_z, 1)
                e.wait_ge(t_z, at(t_z, 2 * g + 2))
                settle(e)
                m = e.tensor_copy(h_flat, y)
                m.then_inc(t_h, 1)
                for c in range(2):
                    e.wait_ge(t_v_ps, at(t_v_ps, 2 * g + c + 1))
                    for q in range(2):
                        m = e.tensor_tensor(vt[:, 2 * c + q, :], bank[4 + c][:, q * D:(q + 1) * D], bv, ALU.add)
                m.then_inc(t_v, 1)
                for c in range(2):
                    e.wait_ge(t_g_ps, at(t_g_ps, 2 * g + c + 1))
                    gr = bank[6 + c][:, :].rearrange("p (c f k) -> p c f k", c=2, f=2)
                    e.tensor_tensor(n_low[:, 2 * c:2 * c + 2, :], gr[:, :, 0, :], tri[:, 0:1, :].to_broadcast([P, 2, P]), ALU.mult)
                    e.tensor_tensor(n_up[:, 2 * c:2 * c + 2, :], gr[:, :, 0, :], tri[:, 1:2, :].to_broadcast([P, 2, P]), ALU.mult)
                    m = e.tensor_tensor(a_up[:, 2 * c:2 * c + 2, :], gr[:, :, 1, :], tri[:, 2:3, :].to_broadcast([P, 2, P]), ALU.mult)
                m.then_inc(t_g, 1)
                e.wait_ge(t_g, at(t_g, g + 1))
                e.tensor_tensor(inv, n_low, tri[:, 3:4, :].to_broadcast([P, NT, P]), ALU.mult)
                e.tensor_tensor(invT, n_up, tri[:, 4:5, :].to_broadcast([P, NT, P]), ALU.mult).then_inc(t_i, 1)
                e.wait_ge(t_i, at(t_i, (LV + 2) * g + 1))
                eye = ident[:, :].unsqueeze(1).to_broadcast([P, NT, P])
                e.tensor_tensor(inv, eye, inv, ALU.subtract)
                e.tensor_tensor(invT, eye, invT, ALU.subtract).then_inc(t_i, 1)
                for l in range(LV):
                    e.wait_ge(t_i, at(t_i, (LV + 2) * g + l + 2))
                    e.wait_ge(t_i_ps, at(t_i_ps, LV * g + l + 1))
                    if l < LV - 1:
                        e.tensor_tensor(inv, inv, cut(bank[2][:, :], NT), ALU.subtract)
                    e.tensor_tensor(invT, invT, cut(bank[3][:, :], NT), ALU.subtract).then_inc(t_i, 1)
                for c in range(NT):
                    k = NT * g + c
                    e.wait_ge(t_r_ps, at(t_r_ps, k + 1))
                    if c == 0:
                        e.wait_ge(t_v, at(t_v, g + 1))
                        e.wait_ge(t_e_ps, at(t_e_ps, k))
                    e.tensor_tensor(residue, bank[0][:, 0:D], vt[:, c, :], ALU.subtract).then_inc(t_r, 1)
                    e.wait_ge(t_w_ps, at(t_w_ps, k + 1))
                    e.tensor_tensor(state[0:DS, :], state[0:DS, :], bank[2][0:DS, 0:D], ALU.add).then_inc(t_w, 1)
                    e.wait_ge(t_y_ps, at(t_y_ps, k + 1))
                    e.wait_ge(t_x, at(t_x, 2 * g + 2))
                    e.tensor_tensor(x[:, c, :], x[:, c, :], bank[3][:, 0:D], ALU.add).then_inc(t_y, 1)
                e.wait_ge(t_y, at(t_y, NT * g + NT))
                norm(xs, ys, 2).then_inc(s_ln, 4)

            e.wait_ge(s_const, at(s_const, 5))
            dve_entry(e)
            e.wait_ge(s_w, at(s_w, 16 * 19))
            e.tensor_copy(identb[:, :], ident[:, :])
            for i in range(2):
                e.tensor_copy(maskb[:, i, :], maskf[:, :])
            for d in range(DEPTH):
                for t in range(NT):
                    m = e.tensor_tensor(rot[:, d, t, :, :].rearrange("p f d -> p (f d)"), rot[:, d, t, :, :].rearrange("p f d -> p (f d)"),
                                          t1[:, 0, d * 256:(d + 1) * 256], ALU.mult)
            m.then_inc(s_const, 3)
            e.wait_ge(s_const, at(s_const, 8))
            for ps in range(passes):
                transformer(ps)
                if ps == 0 and do_ttt:
                    e.wait_ge(T_ZERO0, at(T_ZERO0, 1))
                    e.wait_ge(T_W, at(T_W, 16 * 5))
                    with e.Fori(0, B // 2) as bb:
                        for i in range(2):
                            ttt(bb, i)
                    e.memset(h[0:1, 0, :], 0.0).then_inc(T_DONE, 1)
                else:
                    dve_exit(e, ps)


def constants():
    f = np.float32
    half = np.arange(0, DH, 2, dtype=f)
    inv = (f(1.0) / np.power(f(10000.0), half / f(DH))).astype(f)
    t = np.arange(N, dtype=f)
    fr = (t[:, None] * inv[None]).astype(f)
    fr = np.concatenate([fr, fr], -1)
    base = ((half + f(0.4 * DH)) / f(1.4 * DH)).astype(f)
    power = (t - N // 2) / f(WINDOW // 2)
    sc = np.power(base[None], power[:, None]).astype(f)
    sc = np.concatenate([sc, sc], -1)
    sign = np.concatenate([-np.ones(DH // 2, f), np.ones(DH // 2, f)])
    cos, sin = np.cos(fr), np.sin(fr) * sign
    q8 = f(QK_SCALE)
    tab = np.stack([cos * sc * q8, sin * sc * q8, cos / sc, sin / sc], 1).astype(f)
    tab = tab.reshape(NT, P, 4, DH).transpose(1, 0, 2, 3).reshape(P, -1)
    i, j = np.arange(P)[:, None], np.arange(2 * WINDOW)[None]
    mask = np.where((j < WINDOW) & (j < i) | (j >= WINDOW) & (j - WINDOW > i), f(NEG), f(0))
    r_, c_ = np.arange(P)[:, None], np.arange(P)[None]
    lr = f(TTT_LR)
    tri = [np.where(r_ > c_, lr, f(0)), np.where(r_ < c_, lr, f(0)), np.where(r_ < c_, -lr, f(0))]

    def blocks(b, row, col):
        return ((row // (2 * b) == col // (2 * b)) & (row % (2 * b) >= b) & (col % (2 * b) < b)).astype(f)

    tri += [blocks(1, r_, c_)] + [blocks(2 ** l, c_, r_) for l in range(NLEV)]
    tri = np.stack(tri, 1).astype(f)
    return {"tri": tri, "rot": np.ascontiguousarray(tab), "mask": mask.astype(f), "ident": np.eye(P, dtype=f)}


def layouts(I):
    g = {k: np.asarray(v) for k, v in I.items()}
    out = dict(constants())
    out["x"] = g["L0_attn_x"]
    for k in ("wqkv", "wo", "w1", "w2"):
        out[k] = g["L0_ffn_" + k]
    sw = np.r_[DH // 2:DH, 0:DH // 2]
    qs, ks = g["L0_ffn_q_scale"], g["L0_ffn_k_scale"]
    out["qks"] = np.broadcast_to(np.stack([qs, qs[:, sw], ks, ks[:, sw]], 1).reshape(1, -1), (P, DEPTH * 4 * DH))
    out["lng"] = g["L0_ffn_ln_g"].reshape(DEPTH, KT, P).transpose(2, 0, 1)
    out["lnb"] = g["L0_ffn_ln_b"].reshape(DEPTH, KT, P).transpose(2, 0, 1)
    b1 = np.zeros((DEPTH, 2, MT * P), np.float32)
    b1[:, :, :HID] = g["L0_ffn_b1"].reshape(DEPTH, 2, HID)
    out["b1"] = b1.reshape(DEPTH, 2, MT, P).transpose(3, 0, 1, 2).reshape(P, -1)
    out["b2"] = np.broadcast_to(g["L0_ffn_b2"].reshape(1, -1), (P, DEPTH * D))
    out["wv"] = g["L0_attn_Wv"].T.reshape(KT, P, D).transpose(1, 0, 2)
    out["tw"] = np.concatenate([g["L0_attn_Wk"].T, g["L0_attn_Wq"].T], 1).reshape(KT, P, 2 * DS).transpose(1, 0, 2)
    out["bv"] = np.broadcast_to(g["L0_attn_bv"], (P, D))
    tv = np.zeros((P, 2 * KT + 2), np.float32)
    tv[:, 0:KT] = g["L0_attn_gamma"].reshape(KT, P).T
    tv[:, KT:2 * KT] = g["L0_attn_beta"].reshape(KT, P).T
    tv[:DS, 2 * KT] = g["L0_attn_bk"]
    tv[:DS, 2 * KT + 1] = g["L0_attn_bq"]
    out["tv"] = tv
    return {k: np.ascontiguousarray(v) for k, v in out.items()}


def kernel(**inputs):
    import concourse.bacc as _bacc
    from concourse.bass_utils import run_bass_kernel_spmd as _run

    arrays = layouts(inputs)
    nc = _bacc.Bacc("TRN2", target_bir_lowering=False, num_devices=1)
    A = {n: nc.dram_tensor("in_" + n, a.shape, mybir.dt.from_np(a.dtype), kind="ExternalInput").ap() for n, a in arrays.items()}
    A["out"] = nc.dram_tensor("out", (B, N, D), F32, kind="ExternalOutput").ap()
    build(nc, A)
    r = _run(nc, [{"in_" + n: a for n, a in arrays.items()}], core_ids=[0])
    return r.results[0]["out"]
```

```python
import numpy as np
import concourse.bass as bass
from concourse import mybir
from contextlib import ExitStack

F32 = mybir.dt.float32
F32R = mybir.dt.float32r
BF16 = mybir.dt.bfloat16
ALU = mybir.AluOpType
ACT = mybir.ActivationFunctionType
AX = mybir.AxisListType

P = 128
B, N, D = 8, 512, 256
DEPTH, HEADS, DH = 2, 8, 64
INNER = HEADS * DH
WINDOW = 128
HID = int(D * 4 * 2 / 3)
DS = 64
NT = N // P
KT = D // P
PAIRS = HEADS // 2
MT = -(-HID // P)
HP = MT * P
QK_SCALE = 8.0
NEG = -1e30
TTT_LR = 0.01
LN_EPS = 1e-5
LAYERS = 2 * DEPTH
NLEV = 7


def build(nc, A, passes=2, do_ttt=True):
    ctx = ExitStack()
    with ctx:
        def sb(name, shape, dt=F32):
            return ctx.enter_context(nc.sbuf_tensor(name, shape, dt))

        credits = {}

        def sem(name, credit=1):
            made = ctx.enter_context(nc.semaphore(name))
            credits[id(made)] = (made, credit)
            return made

        def at(which, count):
            value = count + credits[id(which)][1]
            return max(value, 1) if isinstance(value, int) else value

        HL = 2
        Y = sb("Y", [P, B * NT, D])
        wqkv = sb("wqkv", [P, KT, HL, 3 * INNER], F32R)
        wo = sb("wo", [P, HL, PAIRS, D], F32R)
        w1 = sb("w1", [P, KT, HL, 2 * HP], F32R)
        w2 = sb("w2", [P, MT, D])
        rot = sb("rot", [P, NT, 4, DH])
        lng = sb("lng", [P, DEPTH, KT])
        lnb = sb("lnb", [P, DEPTH, KT])
        b1 = sb("b1", [P, DEPTH, 2, MT])
        b2 = sb("b2", [P, DEPTH, D])
        ident = sb("ident", [P, P])
        identb = sb("identb", [P, P], BF16)
        maskb = sb("maskb", [P, 2, 2, 2, WINDOW], BF16)
        small = sb("small", [P, 4])
        h = sb("h", [P, NT, D])
        hT = sb("hT", [P, 2, HL, KT, P], F32R)
        sq = sb("sq", [P, 2, INNER])
        ssk = sb("ssk", [P, HEADS])
        ssq = sb("ssq", [P, HEADS])
        ssg = sb("ssg", [P, 2, HEADS])
        r = sb("r", [P, NT, 2, HEADS])
        t1 = sb("t1", [P, 2, INNER])
        t2 = sb("t2", [P, 2, INNER])
        kqr = sb("kqr", [P, 2, INNER])
        kr, qr = kqr[:, 0, :], kqr[:, 1, :]
        qT = sb("qT", [P, HL, PAIRS, 2, P], F32R)
        kT = sb("kT", [P, HL, PAIRS, 2, 2, P], F32R)
        v = sb("v", [P, NT, INNER])
        nm = sb("nm", [P, HEADS])
        nb = sb("nb", [P, HEADS])
        pr = sb("pr", [P, HEADS, 2 * WINDOW])
        den = sb("den", [P, HEADS])
        rden = sb("rden", [P, HEADS])
        pT = sb("pT", [P, HEADS, 2, P])
        oT = sb("oT", [P, HL, PAIRS, P], F32R)
        h2 = sb("h2", [P, NT, D])
        h2T = sb("h2T", [P, 2, HL, KT, 2 * P], F32R)
        st = sb("st", [P, NT, 6])
        mv = sb("mv", [P, NT, 2])
        vare = sb("vare", [P, NT])
        rs = sb("rs", [P, NT])
        gg = sb("gg", [P, 2, 2 * P])
        uT = sb("uT", [P, 2, MT, 2 * P])
        xb = sb("xb", [P, 2, D])

        rot_s = nc.dram_tensor("rot_scaled", (DEPTH, P, NT * 4 * DH), F32).ap()
        wqkv_s = nc.dram_tensor("wqkv_split", (DEPTH, P, KT * HL * 3 * INNER), F32).ap()
        wo_s = nc.dram_tensor("wo_split", (DEPTH, P, HL * PAIRS * D), F32).ap()
        w1_s = nc.dram_tensor("w1_split", (DEPTH, P, KT * HL * 2 * HP), F32).ap()

        bank = [ctx.enter_context(nc.psum_tensor(f"bank{i}", [P, 512], F32)) for i in range(8)]

        s_x = sem("x_loaded", 0)
        s_w = sem("weights_loaded", 0)
        s_const = sem("constants_ready", 0)
        s_settled = sem("settled", 0)
        s_ln = sem("pass_ln_done")
        s_lnst = sem("pass_ln_stats")
        s_lnr = sem("pass_ln_rstd")
        s_res = sem("pass_residual_done")
        s_out = sem("out_stored")
        negmax_done = sem("negmax_done")
        kr_step = sem("kr_step")
        ha_loaded = sem("ha_loaded", 0)
        ht_ps = sem("ht_ps")
        ht_hi, ht_lo = sem("ht_hi"), sem("ht_lo")
        q_ps, k_ps, v_ps = sem("q_ps"), sem("k_ps"), sem("v_ps")
        sqq, sqk = sem("sqq"), sem("sqk")
        rotq, rotk = sem("rotq"), sem("rotk")
        ssk_done, ssq_done = sem("ssk_done"), sem("ssq_done")
        rk_done, rq_done = sem("rk_done"), sem("rq_done")
        guard_k, guard_q = sem("guard_k"), sem("guard_q")
        wqkv_loaded = [sem(f"w{c}_loaded", 0) for c in "qkv"]
        wo_loaded = sem("wo_loaded", 0)
        w1_loaded, w2_loaded = sem("w1_loaded", 0), sem("w2_loaded", 0)
        qrot, krot = sem("qrot"), sem("krot")
        qt_ps, kt_ps = sem("qt_ps"), sem("kt_ps")
        qt_hi, qt_lo, kt_hi, kt_lo, v_sb = sem("qt_hi"), sem("qt_lo"), sem("kt_hi"), sem("kt_lo"), sem("v_sb")
        s_ps = sem("s_ps")
        nb_done = sem("nb_done")
        exp_done = sem("exp_done", 4)
        rden_done = sem("rden_done")
        pn_done = sem("pn_done", 4)
        pt_ps = sem("pt_ps", 4)
        pte_sb, pto_sb = sem("pte_sb"), sem("pto_sb")
        pv_ps = sem("pv_ps")
        o_hi, o_lo = sem("o_hi"), sem("o_lo")
        wo_ps = sem("wo_ps")
        xa_done = sem("xa_done")
        h2_loaded = [sem("h2_loaded0", 0), sem("h2_loaded1", 0)]
        st_done, mv_done, rs_done = sem("st_done"), sem("mv_done"), sem("rs_done")
        h2n_done = sem("h2n_done", 4)
        h2t_ps = sem("h2t_ps", 2)
        h2t_hi, h2t_lo = sem("h2t_hi"), sem("h2t_lo")
        w1_ps = sem("w1_ps", 12)
        gelu_done = sem("gelu_done")
        u_done = sem("u_done", 3)
        w2_ps = sem("w2_ps", 4)
        xb_done = sem("xb_done")
        xf_done = sem("xf_done", 4)

        def settle(e):
            e.sem_inc(s_settled, 1)

        def idx(L, b, t):
            return 4 * b + (32 * L + t)

        def xt(buf, b, t):
            if isinstance(b, int):
                return buf[:, 4 * b + t, :]
            return buf[:, bass.ds(4 * b + t, 1), :].rearrange("p a d -> p (a d)")

        def xts(buf, b, t, k, lo, hi, p0=0, p1=P):
            if isinstance(b, int):
                return buf[p0:p1, 4 * b + t:4 * b + t + k, lo:hi]
            return buf[p0:p1, bass.ds(4 * b + t, k), lo:hi]

        nX = 16 * 8
        W_DMAS = 2 * (1 + 1 + 1 + 2) + 12

        def mt_bank(job):
            return job % 4

        s_pln = sem("variance_guarded")

        st0 = sb("st0", [P, NT, 6])
        mv0 = sb("mv0", [P, NT, 2])
        va0 = sb("va0", [P, NT])
        rs0 = sb("rs0", [P, NT])
        s_mv0, s_va0, s_rs0 = sem("pass_mv"), sem("pass_var"), sem("pass_rstd")

        def flat(ap, lo, n):
            names = "abcde"[:len(ap.shape) - 1]
            return ap.rearrange("p " + " ".join(names) + " -> p (" + " ".join(names) + ")")[:, lo:lo + n]

        def cut(ap, n):
            return ap.rearrange("p (a c) -> p a c", a=n)

        xw = [cut(flat(uT[:, :, :, :], (1 + i) * N * KT, NT * D), NT) for i in range(2)]
        x_in = A["x"].rearrange("b (t p) d -> p b t d", p=P)
        x_out = A["out"].rearrange("b (t p) d -> p b t d", p=P)
        xw_loaded = [sem("xw0_loaded", 0), sem("xw1_loaded", 0)]
        xw_used = [sem("xw0_used", 1), sem("xw1_used", 1)]
        xw_mixed = [sem("xw0_mixed"), sem("xw1_mixed")]
        xw_stored = [sem("xw0_stored", 16), sem("xw1_stored", 16)]

        def seq(ap, b):
            return ap[:, bass.ds(b, 1), :, :].rearrange("p b t d -> p (b t) d")

        def two(b, i):
            return 2 * b + i

        def sp_entry(e):
            with e.Fori(0, B // 2) as bb:
                for i in range(2):
                    e.wait_ge(xw_used[i], at(xw_used[i], bb))
                    settle(e)
                    e.dma_start(xw[i], seq(x_in, 2 * bb + i)).then_inc(xw_loaded[i], 16)

        def dve_entry(e):
            with e.Fori(0, B // 2) as bb:
                for i in range(2):
                    x = xw[i]
                    e.wait_ge(xw_loaded[i], at(xw_loaded[i], 16 * bb + 16))
                    for t in range(NT):
                        m = e.bn_stats(st0[:, t, :], x[:, t, :])
                    m.then_inc(s_lnst, 1)
                    e.wait_ge(s_lnst, at(s_lnst, 2 * bb + i + 1))
                    settle(e)
                    for t in range(NT):
                        m = e.bn_aggr(mv0[:, t, :], st0[:, t, :])
                    m.then_inc(s_mv0, 1)
                    e.wait_ge(s_rs0, at(s_rs0, 2 * bb + i + 1))
                    e.wait_ge(s_mv0, at(s_mv0, 2 * bb + i + 1))
                    for t in range(NT):
                        m = e.tensor_scalar(xt(Y, 2 * bb + i, t), x[:, t, :], mv0[:, t, 0:1], rs0[:, t:t + 1], ALU.subtract, ALU.mult)
                        m.then_inc(s_ln, 1)
                    e.wait_ge(s_ln, at(s_ln, 8 * bb + 4 * i + 4))
                    m = e.nop()
                    m.then_inc(xw_used[i], 1)

        def pool_entry(e):
            with e.Fori(0, B // 2) as bb:
                for i in range(2):
                    g = 2 * bb + i
                    e.wait_ge(s_mv0, at(s_mv0, g + 1))
                    settle(e)
                    e.tensor_scalar(va0[:, :], mv0[:, :, 1], LN_EPS, None, ALU.add).then_inc(s_va0, 1)
                    e.wait_ge(s_va0, at(s_va0, g + 1))
                    e.tensor_tensor(rs0[:, :], va0[:, :], small[:, 0:1].to_broadcast([P, NT]), ALU.pow).then_inc(s_rs0, 1)

        def sp_exit(e, ps):
            src = x_in if ps == 0 else x_out
            e.wait_ge(xf_done, at(xf_done, idx(DEPTH * ps + DEPTH - 1, B - 1, NT - 1) + 1))
            settle(e)
            with e.Fori(0, B // 2) as bb:
                for i in range(2):
                    e.wait_ge(xw_stored[i], at(xw_stored[i], 16 * bb + (64 * ps - 0)))
                    settle(e)
                    e.dma_start(xw[i], seq(src, 2 * bb + i)).then_inc(xw_loaded[i], 16)
                for i in range(2):
                    e.wait_ge(xw_mixed[i], at(xw_mixed[i], bb + 1))
                    settle(e)
                    e.dma_start(seq(x_out, 2 * bb + i), xw[i]).then_inc(xw_stored[i], 16)
            for i in range(2):
                e.wait_ge(xw_stored[i], at(xw_stored[i], 64 * ps + 64))
                settle(e)

        def dve_exit(e, ps):
            with e.Fori(0, B // 2) as bb:
                for i in range(2):
                    e.wait_ge(xw_loaded[i], at(xw_loaded[i], 16 * bb + (64 + 64 * ps) + 16))
                    y = Y[:, bass.ds(8 * bb + 4 * i, NT), :].rearrange("p t d -> p (t d)")
                    x = xw[i].rearrange("p t d -> p (t d)")
                    e.scalar_tensor_tensor(x, y, 0.5, x, ALU.mult, ALU.add).then_inc(xw_mixed[i], 1)

        z_T = cut(flat(sq[:, :, :], 0, KT * N), KT)
        kqT = cut(flat(uT[:, :, :, :], 0, 2 * N), 2)
        vt = cut(flat(kqr[:, :, :], 0, NT * D), NT)
        n_low = cut(flat(pr[:, :, :], 0, N), NT)
        n_up = cut(flat(pr[:, :, :], N, N), NT)
        a_up = cut(flat(pr[:, :, :], 2 * N, N), NT)
        inv = cut(flat(pr[:, :, :], 3 * N, N), NT)
        invT = cut(flat(pT[:, :, :, :], 0, N), NT)
        mx = cut(flat(pT[:, :, :, :], N, N), NT)
        m_up = [cut(flat(pT[:, :, :, :], (2 + i) * N, N), NT) for i in range(2)]
        state = flat(t2[:, :, :], 0, D)
        residue = flat(t2[:, :, :], D, D)
        errT = flat(t2[:, :, :], 2 * D, D)
        kn = cut(flat(t2[:, :, :], 3 * D, NT * DS), NT)
        wv = cut(flat(t1[:, :, :], 0, KT * D), KT)
        tw = cut(flat(t1[:, :, :], KT * D, KT * 2 * DS), KT)
        tri = cut(flat(v[:, :, :], 0, 11 * P), 11)
        bv = flat(v[:, :, :], 11 * P, D)
        tv = flat(v[:, :, :], 11 * P + D, 6)
        T_W = sem("ttt_weights", 0)
        T_ZERO = sem("ttt_zeroed")
        t_x, t_st, t_mv, t_va, t_rs = sem("ttt_x"), sem("ttt_stats"), sem("ttt_mv"), sem("ttt_var"), sem("ttt_rstd")
        t_z, t_h = sem("ttt_z"), sem("ttt_h")
        t_zt_ps, t_zt = sem("ttt_zT_ps"), sem("ttt_zT")
        t_kq_ps, t_kq = sem("ttt_kq_ps"), sem("ttt_kq")
        t_v_ps, t_v = sem("ttt_v_ps"), sem("ttt_v")
        t_kn_ps, t_kn = sem("ttt_kn_ps"), sem("ttt_kn")
        t_g_ps, t_g = sem("ttt_gram_ps"), sem("ttt_gram")
        t_m = sem("ttt_level_masked")
        t_p_ps, t_p = sem("ttt_mx_ps", 2), sem("ttt_mx")
        t_i_ps, t_i = sem("ttt_inverse_ps"), sem("ttt_inverse")
        t_r_ps, t_r = sem("ttt_r_ps"), sem("ttt_r")
        t_e_ps, t_e = sem("ttt_e_ps"), sem("ttt_e")
        t_y_ps, t_y = sem("ttt_y_ps"), sem("ttt_y")
        t_w_ps, t_w = sem("ttt_w_ps"), sem("ttt_w")
        LV = NLEV - 1

        h_flat = h[:, :, :].rearrange("p t d -> p (t d)")

        def sp_mid(e):
            e.wait_ge(xf_done, at(xf_done, idx(DEPTH - 1, B - 1, NT - 1) + 1))
            settle(e)
            for dst, name in ((wv, "wv"), (tw, "tw"), (tri, "tri"), (bv, "bv"), (tv, "tv")):
                e.dma_start(dst, A[name]).then_inc(T_W, 16)
            with e.Fori(0, B // 2) as bb:
                for i in range(2):
                    e.wait_ge(xw_stored[i], at(xw_stored[i], 16 * bb))
                    settle(e)
                    e.dma_start(xw[i], seq(x_in, 2 * bb + i)).then_inc(xw_loaded[i], 16)
                for i in range(2):
                    e.wait_ge(s_ln, at(s_ln, 8 * bb + 4 * i + 32 + 4))
                    settle(e)
                    e.dma_start(seq(x_out, 2 * bb + i), xw[i]).then_inc(xw_stored[i], 16)
            for i in range(2):
                e.wait_ge(xw_stored[i], at(xw_stored[i], 64))
                settle(e)

        T_ZERO0 = sem("ttt_zero_rows")
        T_DONE = sem("ttt_done")

        chunks = [(d, name, k) for d in (1, 0) for name, k in (("wqkv", 0), ("wqkv", 1), ("w1", 0), ("w1", 1), ("wo", 0))]
        wp_loaded = [sem(f"chunk{i}_loaded", 0) for i in range(3)]
        wp_raw, wp_scaled, wp_hi, wp_lo = sem("chunk_raw_used"), sem("chunk_scaled"), sem("chunk_hi"), sem("chunk_lo")
        wp_stored, rot_stored = sem("split_stored", 0), sem("rot_stored", 0)
        rot_scaled, rot_loaded = sem("rot_scaled", 0), sem("rot_loaded", 0)
        b1_step = sem("beta_added")

        def staged(c, n):
            return flat((pr, pT, v)[c % 3][:, :, :] if c % 3 != 1 else pT[:, :, :, :], 0, n)

        def split_of(name, k, part):
            if name == "wo":
                return wo[:, part, :, :].rearrange("p a n -> p (a n)")
            return (wqkv if name == "wqkv" else w1)[:, k, part, :]

        def extent(name):
            return PAIRS * D if name == "wo" else 3 * INNER

        block = ctx.enter_context(nc.Block())

        @block.sync
        def _(e):
            def load_h(L, b):
                d = D // 2
                if L % 2 == 0:
                    e.wait_ge(s_ln, at(s_ln, 32 * (L // 2) + 4 * b + 4))
                    settle(e)
                else:
                    e.wait_ge(xf_done, at(xf_done, idx(L - 1, b, 3) + 1))
                    settle(e)
                e.wait_ge(ht_ps, at(ht_ps, idx(L, b, 0)))
                settle(e)
                e.dma_start(h[:, :, 0:d], xts(Y, b, 0, NT, 0, d)).then_inc(ha_loaded, 16)
                e.dma_start(h[1:P, :, d:D], xts(Y, b, 0, NT, d, D, 0, P - 1)).then_inc(ha_loaded, 16)
                e.dma_start(h[0:1, 1:NT, d:D], xts(Y, b, 0, NT - 1, d, D, P - 1, P)).then_inc(ha_loaded, 16)

            def load_h2(L, b, half):
                d = D // 2
                t = 2 * half
                e.wait_ge(xa_done, at(xa_done, idx(L, b, t + 1) + 1))
                settle(e)
                e.wait_ge(h2t_ps, at(h2t_ps, 2 * b + (16 * L + half - 1)))
                settle(e)
                q = h2_loaded[half]
                e.dma_start(h2[:, t:t + 2, 0:d], xts(Y, b, t, 2, 0, d)).then_inc(q, 16)
                e.dma_start(h2[1:P, t:t + 2, d:D], xts(Y, b, t, 2, d, D, 0, P - 1)).then_inc(q, 16)
                if half == 0:
                    e.dma_start(h2[0:1, 0, d:D], A["zero"]).then_inc(q, 16)
                    e.dma_start(h2[0:1, 1:2, d:D], xts(Y, b, 0, 1, d, D, P - 1, P)).then_inc(q, 16)
                else:
                    e.dma_start(h2[0:1, 2:4, d:D], xts(Y, b, 1, 2, d, D, P - 1, P)).then_inc(q, 16)

            def load_wqkv(L):
                view = wqkv_s[L % 2].rearrange("p (k s c n) -> p k s c n", k=KT, s=HL, c=3)
                for c, used in ((1, k_ps), (0, q_ps), (2, v_ps)):
                    e.wait_ge(used, at(used, 32 * L))
                    for k in range(KT):
                        e.dma_start(wqkv[:, k, :, c * INNER:(c + 1) * INNER].bitcast(F32), view[:, k, :, c, :]).then_inc(wqkv_loaded[c], 16)
                e.wait_ge(rotq, at(rotq, 32 * L))
                e.dma_start(rot[:, :, :, :].rearrange("p t f d -> p (t f d)"), rot_s[L % 2]).then_inc(rot_loaded, 16)

            def load_rest(L):
                dd = L % 2
                e.wait_ge(wo_ps, at(wo_ps, 32 * L))
                e.dma_start(wo[:, :, :, :].rearrange("p s a n -> p (s a n)").bitcast(F32), wo_s[dd]).then_inc(wo_loaded, 16)
                e.wait_ge(w1_ps, at(w1_ps, 96 * L))
                e.dma_start(w1[:, :, :, :].rearrange("p k s n -> p (k s n)").bitcast(F32), w1_s[dd]).then_inc(w1_loaded, 16)
                if dd == 0:
                    load_w2(L)

            def load_w2(L):
                e.wait_ge(w2_ps, at(w2_ps, 32 * L))
                e.dma_start(w2[:, :, :], A["w2"][L % 2].rearrange("(k p) n -> p k n", p=P)).then_inc(w2_loaded, 16)

            def sequence(L, b, nxt, last=False):
                if nxt:
                    load_h(*nxt)
                load_h2(L, b, 0)
                if last and L + 1 < DEPTH * passes:
                    load_wqkv(L + 1)
                load_h2(L, b, 1)
                if L % 2 and isinstance(b, int) and b == 0:
                    load_w2(L)
                if last and L + 1 < DEPTH * passes:
                    load_rest(L + 1)

            def transformer(ps):
                load_h(DEPTH * ps, 0)
                for L in range(DEPTH * ps, DEPTH * ps + DEPTH):
                    sequence(L, 0, (L, 1))
                    with e.Fori(1, B - 1) as b:
                        sequence(L, b, (L, b + 1))
                    end = L == DEPTH * ps + DEPTH - 1
                    sequence(L, B - 1, None if end else (L + 1, 0), True)

            def store_split(d):
                e.wait_ge(rot_scaled, at(rot_scaled, 2 - d))
                e.dma_start(rot_s[d], rot[:, :, :, :].rearrange("p t f d -> p (t f d)")).then_inc(rot_stored, 16)
                e.dma_start(wqkv_s[d], wqkv[:, :, :, :].rearrange("p k s n -> p (k s n)").bitcast(F32)).then_inc(wp_stored, 16)
                e.dma_start(w1_s[d], w1[:, :, :, :].rearrange("p k s n -> p (k s n)").bitcast(F32)).then_inc(wp_stored, 16)
                e.dma_start(wo_s[d], wo[:, :, :, :].rearrange("p s a n -> p (s a n)").bitcast(F32)).then_inc(wp_stored, 16)

            w = s_w
            e.dma_start(lng[:, :, :], A["lng"]).then_inc(w, 16)
            e.dma_start(lnb[:, :, :], A["lnb"]).then_inc(w, 16)
            e.dma_start(b1[:, :, :, :].rearrange("p a b c -> p (a b c)"), A["b1"]).then_inc(w, 16)
            e.dma_start(ident[:, :], A["ident"]).then_inc(w, 16)
            e.dma_start(t2[:, 0, :], A["mask"]).then_inc(w, 16)
            e.dma_start(h2[:, :, :].rearrange("p t d -> p (t d)"), A["rot"]).then_inc(w, 16)
            e.dma_start(t1[:, 0, :], A["qks"]).then_inc(w, 16)
            e.dma_start(b2[:, :, :].rearrange("p a b -> p (a b)"), A["b2"]).then_inc(w, 16)
            for c, (d, name, k) in enumerate(chunks):
                if c >= 3:
                    e.wait_ge(wp_lo, at(wp_lo, c - 2))
                if c == 7:
                    store_split(1)
                if name == "wo":
                    src = A["wo"][d].rearrange("(k p) n -> p k n", p=P)
                    dst = staged(c, PAIRS * D).rearrange("p (k n) -> p k n", k=PAIRS)
                else:
                    src = A[name][d, k * P:(k + 1) * P, :]
                    dst = staged(c, 3 * INNER)
                e.dma_start(dst, src).then_inc(wp_loaded[c % 3], 16)
            e.dma_start(w2[:, :, :], A["w2"][0].rearrange("(k p) n -> p k n", p=P)).then_inc(w2_loaded, 16)
            e.wait_ge(s_const, at(s_const, 5))
            sp_entry(e)
            e.wait_ge(wp_lo, at(wp_lo, 10))
            store_split(0)
            e.wait_ge(wp_stored, at(wp_stored, 16 * 6))
            e.wait_ge(rot_stored, at(rot_stored, 32))
            for ps in range(passes):
                transformer(ps)
                if ps == 0 and do_ttt:
                    sp_mid(e)
                    e.wait_ge(T_DONE, at(T_DONE, 1))
                else:
                    sp_exit(e, ps)

        @block.gpsimd
        def _(e):
            def A1(L, b, t):
                m = idx(L, b, t)
                minus_half = small[:, 0:1].to_broadcast([P, HEADS])

                def heads(ap):
                    return ap.rearrange("p (h d) -> p h d", h=HEADS)

                e.wait_ge(ssk_done, at(ssk_done, m + 1))
                settle(e)
                e.tensor_scalar(ssg[:, 0, :], ssk[:, :], 1e-24, None, ALU.max).then_inc(guard_k, 1)
                e.wait_ge(guard_k, at(guard_k, m + 1))
                e.tensor_tensor(r[:, t, 0, :], ssg[:, 0, :], minus_half, ALU.pow).then_inc(rk_done, 1)
                e.wait_ge(rotk, at(rotk, m + 1))
                e.wait_ge(kt_ps, at(kt_ps, m))
                e.tensor_tensor(kr, t1[:, 0, :], t2[:, 0, :], ALU.add).then_inc(kr_step, 1)
                e.wait_ge(kr_step, at(kr_step, m + 1))
                e.wait_ge(rk_done, at(rk_done, m + 1))
                e.tensor_tensor(heads(kr), heads(kr), r[:, t, 0, :].unsqueeze(2).to_broadcast([P, HEADS, DH]), ALU.mult).then_inc(krot, 1)
                e.wait_ge(rotq, at(rotq, m + 1))
                e.wait_ge(qt_ps, at(qt_ps, m))
                e.tensor_tensor(qr, t1[:, 1, :], t2[:, 1, :], ALU.add).then_inc(qrot, 1)
                e.wait_ge(ssq_done, at(ssq_done, m + 1))
                settle(e)
                e.tensor_scalar(ssg[:, 1, :], ssq[:, :], 1e-24, None, ALU.max).then_inc(guard_q, 1)
                e.wait_ge(guard_q, at(guard_q, m + 1))
                e.wait_ge(exp_done, at(exp_done, 4 * (m - 1)))
                e.tensor_tensor(r[:, t, 1, :], ssg[:, 1, :], minus_half, ALU.pow).then_inc(rq_done, 1)

            def NP(L, b, t, j):
                n = idx(L, b, t)
                wide = 2 * WINDOW if t else WINDOW
                e.wait_ge(rden_done, at(rden_done, 4 * n + j + 1))
                e.tensor_tensor(pr[:, 2 * j:2 * j + 2, 0:wide], pr[:, 2 * j:2 * j + 2, 0:wide],
                                rden[:, 2 * j:2 * j + 2].unsqueeze(2).to_broadcast([P, 2, wide]), ALU.mult).then_inc(pn_done, 1)

            def XB(L, b, t):
                n, dd = idx(L, b, t), L % 2
                e.wait_ge(xa_done, at(xa_done, n + 1))
                e.wait_ge(xf_done, at(xf_done, n - 1))
                e.tensor_tensor(xb[:, t % 2, :], xt(Y, b, t), b2[:, dd, :], ALU.add).then_inc(xb_done, 1)

            def LN(L, b, half):
                e.wait_ge(mv_done, at(mv_done, idx(L, b, 2 * half + 1) + 1))
                sl = slice(2 * half, 2 * half + 2)
                settle(e)
                e.tensor_scalar(vare[:, sl], mv[:, sl, 1], LN_EPS, None, ALU.add).then_inc(s_pln, 1)
                e.wait_ge(s_pln, at(s_pln, 2 * b + (16 * L + half + 1)))
                e.tensor_tensor(rs[:, sl], vare[:, sl], small[:, 0:1].to_broadcast([P, 2]), ALU.pow).then_inc(rs_done, 1)

            def sequence(L, b, prev, nxt):
                for t in range(NT):
                    ahead = (L, b, t + 1) if t < NT - 1 else nxt and (*nxt, 0)
                    if prev:
                        XB(*prev, t)
                    for j in range(4):
                        NP(L, b, t, j)
                    if t == 2:
                        LN(L, b, 0)
                    if ahead:
                        A1(*ahead)
                LN(L, b, 1)

            def transformer(ps):
                A1(DEPTH * ps, 0, 0)
                for L in range(DEPTH * ps, DEPTH * ps + DEPTH):
                    first, last = L == DEPTH * ps, L == DEPTH * ps + DEPTH - 1
                    sequence(L, 0, None if first else (L - 1, B - 1), (L, 1))
                    with e.Fori(1, B - 1) as b:
                        sequence(L, b, (L, b - 1), (L, b + 1))
                    sequence(L, B - 1, (L, B - 2), None if last else (L + 1, 0))
                for t in range(NT):
                    XB(L, B - 1, t)

            def ttt(bb, i):
                g = 2 * bb + i

                def rstd(k):
                    e.wait_ge(t_mv, at(t_mv, 3 * g + k + 1))
                    settle(e)
                    e.tensor_scalar(va0[:, :], mv0[:, :, 1], LN_EPS, None, ALU.add).then_inc(t_va, 1)
                    e.wait_ge(t_va, at(t_va, 3 * g + k + 1))
                    e.tensor_tensor(rs0[:, :], va0[:, :], small[:, 0:1].to_broadcast([P, NT]), ALU.pow).then_inc(t_rs, 1)

                rstd(0)
                rstd(1)
                e.wait_ge(t_w, at(t_w, NT * g))
                e.wait_ge(t_y_ps, at(t_y_ps, NT * g))
                settle(e)
                e.memset(state, 0.0).then_inc(T_ZERO, 1)
                e.wait_ge(t_g, at(t_g, g + 1))
                for l in range(LV):
                    e.wait_ge(t_p_ps, at(t_p_ps, LV * g + l - 1))
                    e.tensor_tensor(m_up[l % 2], n_up, tri[:, 5 + l:6 + l, :].to_broadcast([P, NT, P]), ALU.mult).then_inc(t_m, 1)
                rstd(2)

            e.memset(small[:, 0:1], -0.5).then_inc(s_const, 1)
            for s_ in range(HL):
                e.memset(kT[:, s_, :, :, :, :].bitcast(F32), 0.0)
            e.memset(h[0:1, 0, :], 0.0)
            e.memset(small[:, 1:2], 1e-24).then_inc(s_const, 3)
            e.wait_ge(s_const, at(s_const, 4))
            for made, credit in credits.values():
                if credit:
                    e.sem_inc(made, credit)
            e.sem_inc(s_const, 1)
            pool_entry(e)
            for ps in range(passes):
                e.wait_ge(s_const, at(s_const, 8))
                transformer(ps)
                if ps == 0 and do_ttt:
                    e.wait_ge(xf_done, at(xf_done, idx(DEPTH - 1, B - 1, NT - 1) + 1))
                    e.memset(flat(uT[:, :, :, :], 0, 2 * N)[64:P, :], 0.0).then_inc(T_ZERO0, 1)
                    with e.Fori(0, B // 2) as bb:
                        for i in range(2):
                            ttt(bb, i)

        @block.scalar
        def _(e):
            def A0(L, b, t):
                m = idx(L, b, t)
                e.wait_ge(ht_ps, at(ht_ps, m + 1))
                e.wait_ge(v_ps, at(v_ps, m - 1))
                e.activation(hT[:, t % 2, 0, :, :].rearrange("p k c -> p (k c)"), bank[2][:, 0:D], ACT.Copy).then_inc(ht_hi, 1)

            def A1(L, b, t):
                m = idx(L, b, t)
                e.wait_ge(k_ps, at(k_ps, m + 1))
                e.wait_ge(ssk_done, at(ssk_done, m))
                e.activation(sq[:, 0, :], bank[0][:, :], ACT.Square).then_inc(sqk, 1)
                e.wait_ge(q_ps, at(q_ps, m + 1))
                e.wait_ge(ssq_done, at(ssq_done, m))
                e.activation(sq[:, 1, :], bank[1][:, :], ACT.Square).then_inc(sqq, 1)
                e.wait_ge(v_ps, at(v_ps, m + 1))
                e.wait_ge(pv_ps, at(pv_ps, m - 2))
                e.activation(v[:, t, :], bank[2][:, :], ACT.Copy).then_inc(v_sb, 1)

            def A2(L, b, t):
                m = idx(L, b, t)
                e.wait_ge(kt_ps, at(kt_ps, m + 1))
                e.wait_ge(s_ps, at(s_ps, 4 * m))
                for g in range(2):
                    last = e.activation(kT[64 * g:64 * g + 64, 0, :, g, t % 2, :], cut(bank[0][64 * g:64 * g + 64, :], PAIRS), ACT.Copy)
                last.then_inc(kt_hi, 1)
                e.wait_ge(qt_ps, at(qt_ps, m + 1))
                e.activation(qT[:, 0, :, t % 2, :], cut(bank[1][:, :], PAIRS), ACT.Copy).then_inc(qt_hi, 1)

            def S(L, b, t, j):
                n = idx(L, b, t)
                wide = 2 * WINDOW if t else WINDOW
                e.wait_ge(nb_done, at(nb_done, 4 * n + j + 1))
                e.wait_ge(pt_ps, at(pt_ps, 4 * (n - 1) + j + 1))
                if j == 0:
                    e.wait_ge(rden_done, at(rden_done, 4 * n))
                for g in range(2):
                    hd = 2 * j + g
                    last = e.activation(pr[:, hd, 0:wide], bank[j][:, g * 256:g * 256 + wide], ACT.Exp,
                                        bias=nb[:, hd:hd + 1], scale=r[:, t, 1, hd:hd + 1], accum_out=den[:, hd:hd + 1])
                last.then_inc(exp_done, 1)

            def PT(L, b, t, j):
                n = idx(L, b, t)
                e.wait_ge(pt_ps, at(pt_ps, 4 * n + j + 1))
                e.wait_ge(pv_ps, at(pv_ps, n))
                w = 2 if t else 1
                e.activation(pT[:, 2 * j:2 * j + 2, 0:w, :],
                             bank[4][:, :].rearrange("p (h w c) -> p h w c", h=2, w=2)[:, :, 0:w, :], ACT.Copy).then_inc(pte_sb, 1)

            def O(L, b, t):
                n = idx(L, b, t)
                e.wait_ge(pv_ps, at(pv_ps, n + 1))
                e.wait_ge(wo_ps, at(wo_ps, n))
                e.activation(oT[:, 0, :, :].rearrange("p a c -> p (a c)"), bank[6][:, :], ACT.Copy).then_inc(o_hi, 1)

            def H2T(L, b, half):
                e.wait_ge(h2t_ps, at(h2t_ps, 2 * b + (16 * L + half + 1)))
                e.wait_ge(w1_ps, at(w1_ps, 12 * b + (96 * L + 6 * half - 6)))
                e.activation(h2T[:, half, 0, :, :].rearrange("p k c -> p (k c)"), bank[4][:, :], ACT.Copy).then_inc(h2t_hi, 1)

            def G(L, b, half, mt):
                job = 6 * half + mt
                e.wait_ge(w1_ps, at(w1_ps, 12 * b + (96 * L + job + 1)))
                e.wait_ge(u_done, at(u_done, 12 * b + (96 * L + job - 1)))
                e.activation(gg[:, job % 2, :], bank[job % 4][:, 256:512], ACT.Gelu,
                             bias=b1[:, L % 2, 1, mt:mt + 1]).then_inc(gelu_done, 1)

            def sequence(L, b, prev, nxt):
                for t in range(NT):
                    ahead = (L, b, t + 1) if t < NT - 1 else nxt and (*nxt, 0)
                    ahead2 = (L, b, t + 2) if t < NT - 2 else nxt and (*nxt, t - 2)
                    for j in range(4):
                        S(L, b, t, j)
                    if ahead:
                        A1(*ahead)
                    if t == 3:
                        H2T(L, b, 0)
                    PT(L, b, t, 0)
                    PT(L, b, t, 2)
                    O(L, b, t)
                    if ahead2:
                        A0(*ahead2)
                    if ahead:
                        A2(*ahead)
                for mt in range(MT):
                    G(L, b, 0, mt)
                    if mt == 4:
                        H2T(L, b, 1)
                for mt in range(MT):
                    G(L, b, 1, mt)

            def transformer(ps):
                A0(DEPTH * ps, 0, 0)
                A1(DEPTH * ps, 0, 0)
                A0(DEPTH * ps, 0, 1)
                A2(DEPTH * ps, 0, 0)
                for L in range(DEPTH * ps, DEPTH * ps + DEPTH):
                    first, last = L == DEPTH * ps, L == DEPTH * ps + DEPTH - 1
                    sequence(L, 0, None if first else (L - 1, B - 1), (L, 1))
                    with e.Fori(1, B - 1) as b:
                        sequence(L, b, (L, b - 1), (L, b + 1))
                    sequence(L, B - 1, (L, B - 2), None if last else (L + 1, 0))

            def ttt(bb, i):
                g = 2 * bb + i
                for k in range(KT):
                    e.wait_ge(t_zt_ps, at(t_zt_ps, 2 * g + k + 1))
                    m = e.activation(z_T[:, k, :], bank[k][:, :], ACT.Identity, bias=tv[:, KT + k:KT + k + 1], scale=tv[:, k:k + 1])
                m.then_inc(t_zt, 1)
                for k in range(2):
                    e.wait_ge(t_kq_ps, at(t_kq_ps, 2 * g + k + 1))
                    if k == 0:
                        e.wait_ge(t_y_ps, at(t_y_ps, NT * g))
                    m = e.activation(kqT[0:DS, k, :], bank[2 + k][0:DS, :], ACT.Identity, bias=tv[0:DS, 2 * KT + k:2 * KT + k + 1])
                m.then_inc(t_kq, 1)
                e.wait_ge(t_kn_ps, at(t_kn_ps, g + 1))
                e.activation(kn.rearrange("p a c -> p (a c)"), bank[0][:, 0:NT * DS], ACT.Copy, scale=-TTT_LR).then_inc(t_kn, 1)
                for l in range(LV):
                    e.wait_ge(t_p_ps, at(t_p_ps, LV * g + l + 1))
                    e.wait_ge(t_i_ps, at(t_i_ps, LV * g + l))
                    e.activation(mx.rearrange("p a c -> p (a c)"), bank[0 + l % 2][:, :], ACT.Copy).then_inc(t_p, 1)
                for c in range(NT):
                    k = NT * g + c
                    e.wait_ge(t_e_ps, at(t_e_ps, k + 1))
                    e.wait_ge(t_y_ps, at(t_y_ps, k))
                    e.activation(errT, bank[1][:, 0:D], ACT.Copy).then_inc(t_e, 1)

            e.wait_ge(s_const, at(s_const, 5))
            scaled = 0
            for c, (d, name, k) in enumerate(chunks):
                if c == 5:
                    e.wait_ge(wp_stored, at(wp_stored, 16 * 3))
                if name == "w1":
                    scaled += 1
                    e.wait_ge(wp_scaled, at(wp_scaled, scaled))
                else:
                    e.wait_ge(wp_loaded[c % 3], at(wp_loaded[c % 3], 16 * (c // 3 + 1)))
                e.activation(split_of(name, k, 0), staged(c, extent(name)), ACT.Copy).then_inc(wp_hi, 1)
            e.wait_ge(s_const, at(s_const, 8))
            for ps in range(passes):
                transformer(ps)
                if ps == 0 and do_ttt:
                    e.wait_ge(T_ZERO0, at(T_ZERO0, 1))
                    e.wait_ge(T_W, at(T_W, 16 * 5))
                    with e.Fori(0, B // 2) as bb:
                        for i in range(2):
                            ttt(bb, i)

        @block.tensor
        def _(e):
            def split_product(out, left, right, first=True, last=True):
                e.matmul(out, left[0], right[0], start=first, stop=False)
                e.matmul(out, left[0], right[1], start=False, stop=False)
                return e.matmul(out, left[1], right[0], start=False, stop=last)

            def A0(L, b, t):
                m = idx(L, b, t)
                if t == 0:
                    e.wait_ge(ha_loaded, at(ha_loaded, 48 * b + (48 * 8 * L + 48)))
                e.wait_ge(v_sb, at(v_sb, m))
                for k in range(KT):
                    mm = e.transpose(bank[2][:, k * P:(k + 1) * P], h[:, t, k * P:(k + 1) * P], ident[:, :])
                mm.then_inc(ht_ps, 1)

            def A1(L, b, t):
                m = idx(L, b, t)
                e.wait_ge(ht_lo, at(ht_lo, m + 1))
                for i, (done, col) in enumerate(((k_ps, 1), (q_ps, 0), (v_ps, 2))):
                    if L and isinstance(b, int) and b == 0 and t == 0:
                        e.wait_ge(wqkv_loaded[col], at(wqkv_loaded[col], 32 * L))
                    e.wait_ge(exp_done, at(exp_done, 4 * (m - 1) + i + 1))
                    for k in range(KT):
                        mm = split_product(bank[i][:, :], [hT[:, t % 2, s_, k, :] for s_ in range(HL)],
                                           [wqkv[:, k, s_, col * INNER:(col + 1) * INNER] for s_ in range(HL)],
                                           k == 0, k == KT - 1)
                    mm.then_inc(done, 1)

            def A2(L, b, t, i):
                m = idx(L, b, t)
                src, added, done = ((kr, krot, kt_ps), (qr, qrot, qt_ps))[i]
                e.wait_ge(added, at(added, m + 1))
                for p in range(PAIRS):
                    mm = e.transpose(bank[i][:, p * P:(p + 1) * P], src[:, p * P:(p + 1) * P], ident[:, :])
                mm.then_inc(done, 1)

            def S(L, b, t, j, more):
                n = idx(L, b, t)
                if j == 0:
                    e.wait_ge(kt_lo, at(kt_lo, n + 1))
                    e.wait_ge(qt_lo, at(qt_lo, n + 1))
                if j == 2 and (t < NT - 1 or more):
                    e.wait_ge(ht_lo, at(ht_lo, n + 2))
                if j == 3:
                    e.wait_ge(xa_done, at(xa_done, n))
                if t == 0:
                    e.wait_ge(u_done, at(u_done, 12 * b + (96 * L + j - 3)))
                slots = slice(0, 2) if t else slice(0, 1)
                out = bank[j][:, :].rearrange("p (h w k) -> p h w k", h=2, w=2)[:, :, slots, :]
                e.matmul(out, identb[:, :], maskb[:, t % 2, :, slots, :], start=True, stop=False)
                split_product(out, [qT[:, s_, j, t % 2, :] for s_ in range(HL)],
                              [kT[:, s_, j, :, slots, :] for s_ in range(HL)], False, True).then_inc(s_ps, 1)

            def PT(L, b, t, j):
                n = idx(L, b, t)
                k, bk = j // 2, 4 + j % 2
                e.wait_ge(pn_done, at(pn_done, 4 * n + j + 1))
                copied = pto_sb if j % 2 else pte_sb
                e.wait_ge(copied, at(copied, 2 * n + k))
                if j == 0 and t in (0, 3):
                    e.wait_ge(h2t_lo, at(h2t_lo, 2 * b + (16 * L + (t == 3))))
                for g in range(2):
                    for w in range(2 if t else 1):
                        mm = e.transpose(bank[bk][:, (2 * g + w) * P:(2 * g + w + 1) * P],
                                         pr[:, 2 * j + g, w * P:(w + 1) * P], ident[:, :])
                mm.then_inc(pt_ps, 1)

            def PV(L, b, t, j):
                n = idx(L, b, t)
                if j == 0:
                    e.wait_ge(o_lo, at(o_lo, n))
                copied = pto_sb if j % 2 else pte_sb
                e.wait_ge(copied, at(copied, 2 * n + j // 2 + 1))
                for g in range(2):
                    hd = 2 * j + g
                    ws = (0, 1) if t else (0,)
                    for w in ws:
                        tile = t if w == t % 2 else t - 1
                        mm = e.matmul(bank[6][64 * g:64 * g + 64, j * P:(j + 1) * P],
                                      v[:, tile, hd * DH:(hd + 1) * DH], pT[:, hd, w, :],
                                      start=(w == 0), stop=(w == ws[-1]))
                if j == 3:
                    mm.then_inc(pv_ps, 1)

            def WO(L, b, t):
                n = idx(L, b, t)
                if L and t == 0:
                    e.wait_ge(wo_loaded, at(wo_loaded, 16 * L))
                e.wait_ge(exp_done, at(exp_done, 4 * n + 4))
                e.wait_ge(o_lo, at(o_lo, n + 1))
                for p in range(PAIRS):
                    mm = split_product(bank[3][:, 0:D], [oT[:, s_, p, :] for s_ in range(HL)],
                                       [wo[:, s_, p, :] for s_ in range(HL)], p == 0, p == PAIRS - 1)
                mm.then_inc(wo_ps, 1)

            def H2T(L, b, half):
                e.wait_ge(h2n_done, at(h2n_done, idx(L, b, 2 * half + 1) + 1))
                e.wait_ge(pte_sb, at(pte_sb, 2 * idx(L, b, 3) + 2 * half))
                for k in range(KT):
                    for i in range(2):
                        mm = e.transpose(bank[4][:, (2 * k + i) * P:(2 * k + i + 1) * P],
                                         h2[:, 2 * half + i, k * P:(k + 1) * P], ident[:, :])
                mm.then_inc(h2t_ps, 1)

            def W1(L, b, half, mt, more):
                job, n = 6 * half + mt, idx(L, b, 3)
                if L and job == 0:
                    e.wait_ge(w1_loaded, at(w1_loaded, 16 * L))
                if mt == 0:
                    e.wait_ge(h2t_lo, at(h2t_lo, 2 * b + (16 * L + half + 1)))
                if job == 3:
                    e.wait_ge(xa_done, at(xa_done, n + 1))
                elif job < 3:
                    e.wait_ge(exp_done, at(exp_done, 4 * n + 4))
                    if more:
                        if job == 0:
                            e.wait_ge(kt_lo, at(kt_lo, n + 2))
                        if job == 1:
                            e.wait_ge(qt_lo, at(qt_lo, n + 2))
                        if job == 2:
                            e.wait_ge(ht_lo, at(ht_lo, n + 3))
                else:
                    e.wait_ge(u_done, at(u_done, 12 * b + (96 * L + job - 3)))
                for g in range(2):
                    for k in range(KT):
                        mm = split_product(bank[job % 4][:, g * 256:(g + 1) * 256],
                                           [w1[:, k, s_, g * HP + mt * P:g * HP + (mt + 1) * P] for s_ in range(HL)],
                                           [h2T[:, half, s_, k, :] for s_ in range(HL)], k == 0, k == KT - 1)
                mm.then_inc(w1_ps, 1)

            def W2(L, b, t, lo, hi):
                n = idx(L, b, t)
                if lo == 0:
                    if t == 0:
                        e.wait_ge(w2_loaded, at(w2_loaded, 16 * L + 16))
                    e.wait_ge(u_done, at(u_done, 12 * b + (96 * L + 6 * (t // 2) + 6)))
                    e.wait_ge(xf_done, at(xf_done, n))
                for mt in range(lo, hi):
                    mm = e.matmul(bank[7][:, 0:D], uT[:, t // 2, mt, (t % 2) * P:(t % 2 + 1) * P],
                                  w2[:, mt, :], start=(mt == 0), stop=(mt == MT - 1))
                if hi == MT:
                    mm.then_inc(w2_ps, 1)

            def sequence(L, b, prev, nxt):
                for t in range(NT):
                    ahead = (L, b, t + 1) if t < NT - 1 else nxt and (*nxt, 0)
                    ahead2 = (L, b, t + 2) if t < NT - 2 else nxt and (*nxt, t - 2)
                    for j in range(4):
                        S(L, b, t, j, bool(nxt))
                    if ahead:
                        A1(*ahead)
                    if t == 3:
                        H2T(L, b, 0)
                    PT(L, b, t, 0)
                    PT(L, b, t, 1)
                    if prev:
                        W2(*prev, t, 0, 2)
                    PT(L, b, t, 2)
                    PV(L, b, t, 0)
                    PT(L, b, t, 3)
                    for j in range(1, 4):
                        PV(L, b, t, j)
                    if ahead2:
                        A0(*ahead2)
                    if ahead:
                        A2(*ahead, 0)
                    if prev:
                        W2(*prev, t, 2, 4)
                    if ahead:
                        A2(*ahead, 1)
                    WO(L, b, t)
                    if prev:
                        W2(*prev, t, 4, MT)
                for mt in range(MT):
                    W1(L, b, 0, mt, bool(nxt))
                    if mt == 4:
                        H2T(L, b, 1)
                for mt in range(MT):
                    W1(L, b, 1, mt, bool(nxt))

            def transformer(ps):
                A0(DEPTH * ps, 0, 0)
                A1(DEPTH * ps, 0, 0)
                A0(DEPTH * ps, 0, 1)
                A2(DEPTH * ps, 0, 0, 0)
                A2(DEPTH * ps, 0, 0, 1)
                for L in range(DEPTH * ps, DEPTH * ps + DEPTH):
                    first, last = L == DEPTH * ps, L == DEPTH * ps + DEPTH - 1
                    sequence(L, 0, None if first else (L - 1, B - 1), (L, 1))
                    with e.Fori(1, B - 1) as b:
                        sequence(L, b, (L, b - 1), (L, b + 1))
                    sequence(L, B - 1, (L, B - 2), None if last else (L + 1, 0))
                for t in range(NT):
                    W2(L, B - 1, t, 0, MT)

            def ttt(bb, i):
                g = 2 * bb + i
                e.wait_ge(t_h, at(t_h, g + 1))
                e.wait_ge(t_e, at(t_e, NT * g))
                for k in range(KT):
                    for t in range(NT):
                        m = e.transpose(bank[k][:, t * P:(t + 1) * P], h[:, t, k * P:(k + 1) * P], ident[:, :])
                    m.then_inc(t_zt_ps, 1)
                e.wait_ge(t_zt, at(t_zt, g + 1))
                e.wait_ge(t_w, at(t_w, NT * g))
                e.wait_ge(t_y, at(t_y, NT * g))
                for f in range(2):
                    for k in range(KT):
                        m = e.matmul(bank[2 + f][0:DS, :], tw[:, k, f * DS:(f + 1) * DS], z_T[:, k, :], start=(k == 0), stop=(k == KT - 1))
                    m.then_inc(t_kq_ps, 1)
                for c in range(NT):
                    for k in range(KT):
                        m = e.matmul(bank[4 + c // 2][:, (c % 2) * D:(c % 2 + 1) * D], z_T[:, k, c * P:(c + 1) * P], wv[:, k, :],
                                     start=(k == 0), stop=(k == KT - 1))
                    if c % 2:
                        m.then_inc(t_v_ps, 1)
                e.wait_ge(t_kq, at(t_kq, g + 1))
                settle(e)
                for c in range(NT):
                    m = e.transpose(bank[0][:, c * DS:(c + 1) * DS], kqT[0:DS, 0, c * P:(c + 1) * P], ident[0:DS, 0:DS])
                m.then_inc(t_kn_ps, 1)
                for c in range(NT):
                    m = e.matmul(bank[6 + c // 2][:, (c % 2) * 256:(c % 2 + 1) * 256], kqT[:, 0, c * P:(c + 1) * P], kqT[:, :, c * P:(c + 1) * P],
                                 start=True, stop=True)
                    if c % 2:
                        m.then_inc(t_g_ps, 1)
                e.wait_ge(t_kn, at(t_kn, g + 1))
                for l in range(LV):
                    e.wait_ge(t_m, at(t_m, LV * g + l + 1))
                    e.wait_ge(t_i, at(t_i, (LV + 2) * g + l + 2))
                    for c in range(NT):
                        m = e.matmul(bank[l % 2][:, c * P:(c + 1) * P], m_up[l % 2][:, c, :], inv[:, c, :], start=True, stop=True)
                    m.then_inc(t_p_ps, 1)
                    e.wait_ge(t_p, at(t_p, LV * g + l + 1))
                    for c in range(NT):
                        if l < LV - 1:
                            e.matmul(bank[2][:, c * P:(c + 1) * P], invT[:, c, :], mx[:, c, :], start=True, stop=True)
                        m = e.matmul(bank[3][:, c * P:(c + 1) * P], mx[:, c, :], invT[:, c, :], start=True, stop=True)
                    m.then_inc(t_i_ps, 1)
                e.wait_ge(t_i, at(t_i, (LV + 2) * g + LV + 2))
                e.wait_ge(T_ZERO, at(T_ZERO, g + 1))
                for c in range(NT):
                    k = NT * g + c
                    e.wait_ge(t_w, at(t_w, k))
                    e.wait_ge(t_r, at(t_r, k))
                    e.matmul(bank[0][:, 0:D], kqT[:, 0, c * P:(c + 1) * P], state, start=True, stop=True).then_inc(t_r_ps, 1)
                    e.wait_ge(t_r, at(t_r, k + 1))
                    e.wait_ge(t_e, at(t_e, k))
                    e.matmul(bank[1][:, 0:D], invT[:, c, :], residue, start=True, stop=True).then_inc(t_e_ps, 1)
                    e.wait_ge(t_y, at(t_y, k))
                    e.matmul(bank[3][:, 0:D], kqT[:, 1, c * P:(c + 1) * P], state, start=True, stop=False)
                    e.wait_ge(t_e, at(t_e, k + 1))
                    e.matmul(bank[3][:, 0:D], a_up[:, c, :], errT, start=False, stop=True).then_inc(t_y_ps, 1)
                    e.matmul(bank[2][0:DS, 0:D], kn[:, c, :], errT, start=True, stop=True).then_inc(t_w_ps, 1)

            e.wait_ge(s_const, at(s_const, 5))
            e.wait_ge(s_w, at(s_w, 16 * 8))
            for c, (d, name, k) in enumerate(chunks):
                if name == "w1":
                    e.wait_ge(wp_loaded[c % 3], at(wp_loaded[c % 3], 16 * (c // 3 + 1)))
                    raw = staged(c, extent(name))
                    for mt in range(2 * MT):
                        mm = e.matmul(bank[d][:, 12 * k + mt:12 * k + mt + 1], raw[:, mt * P:(mt + 1) * P], lnb[:, d, k:k + 1], start=True, stop=True)
                    mm.then_inc(wp_raw, 1)
            e.wait_ge(s_const, at(s_const, 8))
            for ps in range(passes):
                transformer(ps)
                if ps == 0 and do_ttt:
                    e.wait_ge(T_ZERO0, at(T_ZERO0, 1))
                    e.wait_ge(T_W, at(T_W, 16 * 5))
                    with e.Fori(0, B // 2) as bb:
                        for i in range(2):
                            ttt(bb, i)

        @block.vector
        def _(e):
            def A0(L, b, t):
                m = idx(L, b, t)
                e.wait_ge(ht_hi, at(ht_hi, m + 1))
                e.tensor_tensor(hT[:, t % 2, 1, :, :].rearrange("p k c -> p (k c)"), bank[2][:, 0:D],
                                hT[:, t % 2, 0, :, :].rearrange("p k c -> p (k c)"), ALU.subtract).then_inc(ht_lo, 1)

            def A1(L, b, t):
                m = idx(L, b, t)
                if L and isinstance(b, int) and b == 0 and t == 0:
                    e.wait_ge(rot_loaded, at(rot_loaded, 16 * L))

                def heads(ap):
                    return ap.rearrange("p (h c j) -> p h c j", h=HEADS, c=2)

                for i, (squared, rotated, added, sums, summed, read) in enumerate((
                        (sqk, rotk, krot, ssk, ssk_done, guard_k), (sqq, rotq, qrot, ssq, ssq_done, guard_q))):
                    f = 2 * (1 - i)
                    e.wait_ge(squared, at(squared, m + 1))
                    e.wait_ge(read, at(read, m))
                    e.tensor_reduce(sums[:, :], sq[:, i, :].rearrange("p (h d) -> p h d", h=HEADS), AX.X, ALU.add).then_inc(summed, 1)
                    e.wait_ge(added, at(added, m))
                    e.tensor_tensor(t1[:, i, :].rearrange("p (h d) -> p h d", h=HEADS),
                                    bank[i][:, :].rearrange("p (h d) -> p h d", h=HEADS),
                                    rot[:, t, f:f + 1, :].to_broadcast([P, HEADS, DH]), ALU.mult)
                    e.tensor_tensor(heads(t2[:, i, :]), heads(bank[i][:, :])[:, :, ::-1, :],
                                    rot[:, t, f + 1:f + 2, :].to_broadcast([P, HEADS, DH]).rearrange("p h (c j) -> p h c j", c=2),
                                    ALU.mult).then_inc(rotated, 1)

            def A2(L, b, t):
                m = idx(L, b, t)
                e.wait_ge(kt_hi, at(kt_hi, m + 1))
                for g in range(2):
                    rows = slice(64 * g, 64 * g + 64)
                    last = e.tensor_tensor(kT[rows, 1, :, g, t % 2, :], cut(bank[0][rows, :], PAIRS), kT[rows, 0, :, g, t % 2, :], ALU.subtract)
                last.then_inc(kt_lo, 1)
                e.wait_ge(qt_hi, at(qt_hi, m + 1))
                e.tensor_tensor(qT[:, 1, :, t % 2, :], cut(bank[1][:, :], PAIRS), qT[:, 0, :, t % 2, :], ALU.subtract).then_inc(qt_lo, 1)

            def S(L, b, t, j):
                n = idx(L, b, t)
                wide = 2 * WINDOW if t else WINDOW
                if j == 0:
                    e.wait_ge(rq_done, at(rq_done, n + 1))
                e.wait_ge(s_ps, at(s_ps, 4 * n + j + 1))
                e.tensor_reduce(nm[:, 2 * j:2 * j + 2], bank[j][:, :].rearrange("p (h k) -> p h k", h=2)[:, :, 0:wide],
                                AX.X, ALU.max, negate=True).then_inc(negmax_done, 1)
                e.wait_ge(exp_done, at(exp_done, 4 * (n - 1) + j + 1))
                e.wait_ge(negmax_done, at(negmax_done, 4 * n + j + 1))
                e.tensor_tensor(nb[:, 2 * j:2 * j + 2], nm[:, 2 * j:2 * j + 2], r[:, t, 1, 2 * j:2 * j + 2], ALU.mult).then_inc(nb_done, 1)

            def R(L, b, t, j):
                n = idx(L, b, t)
                e.wait_ge(exp_done, at(exp_done, 4 * n + j + 1))
                e.wait_ge(pn_done, at(pn_done, 4 * n + j - 3))
                e.reciprocal(rden[:, 2 * j:2 * j + 2], den[:, 2 * j:2 * j + 2]).then_inc(rden_done, 1)

            def PT(L, b, t, j):
                n = idx(L, b, t)
                e.wait_ge(pt_ps, at(pt_ps, 4 * n + j + 1))
                e.wait_ge(pv_ps, at(pv_ps, n))
                w = 2 if t else 1
                e.tensor_copy(pT[:, 2 * j:2 * j + 2, 0:w, :],
                              bank[5][:, :].rearrange("p (h w c) -> p h w c", h=2, w=2)[:, :, 0:w, :]).then_inc(pto_sb, 1)

            def O(L, b, t):
                n = idx(L, b, t)
                e.wait_ge(o_hi, at(o_hi, n + 1))
                e.tensor_tensor(oT[:, 1, :, :].rearrange("p a c -> p (a c)"), bank[6][:, :],
                                oT[:, 0, :, :].rearrange("p a c -> p (a c)"), ALU.subtract).then_inc(o_lo, 1)

            def WO(L, b, t):
                n = idx(L, b, t)
                e.wait_ge(wo_ps, at(wo_ps, n + 1))
                e.tensor_tensor(xt(Y, b, t), bank[3][:, 0:D], xt(Y, b, t), ALU.add).then_inc(xa_done, 1)

            def H2T(L, b, half):
                e.wait_ge(h2t_hi, at(h2t_hi, 2 * b + (16 * L + half + 1)))
                e.tensor_tensor(h2T[:, half, 1, :, :].rearrange("p k c -> p (k c)"), bank[4][:, :],
                                h2T[:, half, 0, :, :].rearrange("p k c -> p (k c)"), ALU.subtract).then_inc(h2t_lo, 1)

            def LN_moments(L, b, half):
                for t in (2 * half, 2 * half + 1):
                    if t == 2 * half:
                        dmas = 16 * (4 - half)
                        e.wait_ge(h2_loaded[half], at(h2_loaded[half], dmas * b + (dmas * 8 * L + dmas)))
                    e.bn_stats(st[:, t, :], h2[:, t, :]).then_inc(st_done, 1)
                for t in (2 * half, 2 * half + 1):
                    e.wait_ge(st_done, at(st_done, idx(L, b, t) + 1))
                    settle(e)
                    e.bn_aggr(mv[:, t, :], st[:, t, :]).then_inc(mv_done, 1)

            def LN_apply(L, b, half):
                for t in (2 * half, 2 * half + 1):
                    if t == 2 * half:
                        e.wait_ge(mv_done, at(mv_done, idx(L, b, t + 1) + 1))
                        e.wait_ge(rs_done, at(rs_done, 2 * b + (16 * L + half + 1)))
                    e.tensor_scalar(h2[:, t, :], h2[:, t, :], mv[:, t, 0:1], rs[:, t:t + 1], ALU.subtract, ALU.mult).then_inc(h2n_done, 1)

            def U(L, b, half, mt):
                job = 6 * half + mt
                e.wait_ge(gelu_done, at(gelu_done, 12 * b + (96 * L + job + 1)))
                if mt == 0:
                    e.wait_ge(w2_ps, at(w2_ps, idx(L, b, 0) + 2 * half - 2))
                e.scalar_tensor_tensor(uT[:, half, mt, :], bank[job % 4][:, 0:256], b1[:, L % 2, 0, mt:mt + 1],
                                       gg[:, job % 2, :], ALU.add, ALU.mult).then_inc(u_done, 1)

            def W2(L, b, t):
                n = idx(L, b, t)
                e.wait_ge(w2_ps, at(w2_ps, n + 1))
                e.wait_ge(xb_done, at(xb_done, n + 1))
                e.tensor_tensor(xt(Y, b, t), bank[7][:, 0:D], xb[:, t % 2, :], ALU.add).then_inc(xf_done, 1)

            def sequence(L, b, prev, nxt):
                for t in range(NT):
                    ahead = (L, b, t + 1) if t < NT - 1 else nxt and (*nxt, 0)
                    ahead2 = (L, b, t + 2) if t < NT - 2 else nxt and (*nxt, t - 2)
                    S(L, b, t, 0)
                    S(L, b, t, 1)
                    R(L, b, t, 0)
                    S(L, b, t, 2)
                    R(L, b, t, 1)
                    S(L, b, t, 3)
                    R(L, b, t, 2)
                    R(L, b, t, 3)
                    if prev and t:
                        W2(*prev, t - 1)
                    if t == 2:
                        LN_moments(L, b, 0)
                    if ahead:
                        A1(*ahead)
                    if t == 3:
                        H2T(L, b, 0)
                    PT(L, b, t, 1)
                    if t == 2:
                        LN_apply(L, b, 0)
                    PT(L, b, t, 3)
                    O(L, b, t)
                    if ahead2:
                        A0(*ahead2)
                    if ahead:
                        A2(*ahead)
                    WO(L, b, t)
                if prev:
                    W2(*prev, NT - 1)
                for mt in range(MT):
                    U(L, b, 0, mt)
                    if mt == 0:
                        LN_moments(L, b, 1)
                    if mt == 1:
                        LN_apply(L, b, 1)
                    if mt == 4:
                        H2T(L, b, 1)
                for mt in range(MT):
                    U(L, b, 1, mt)

            def transformer(ps):
                A0(DEPTH * ps, 0, 0)
                A1(DEPTH * ps, 0, 0)
                A0(DEPTH * ps, 0, 1)
                A2(DEPTH * ps, 0, 0)
                for L in range(DEPTH * ps, DEPTH * ps + DEPTH):
                    first, last = L == DEPTH * ps, L == DEPTH * ps + DEPTH - 1
                    sequence(L, 0, None if first else (L - 1, B - 1), (L, 1))
                    with e.Fori(1, B - 1) as b:
                        sequence(L, b, (L, b - 1), (L, b + 1))
                    sequence(L, B - 1, (L, B - 2), None if last else (L + 1, 0))
                for t in range(NT):
                    W2(L, B - 1, t)

            def ttt(bb, i):
                g, x = 2 * bb + i, xw[i]

                def norm(src, dst, k):
                    for t in range(NT):
                        m = e.bn_stats(st0[:, t, :], src[t])
                    m.then_inc(t_st, 1)
                    e.wait_ge(t_st, at(t_st, 3 * g + k + 1))
                    settle(e)
                    for t in range(NT):
                        m = e.bn_aggr(mv0[:, t, :], st0[:, t, :])
                    m.then_inc(t_mv, 1)
                    e.wait_ge(t_mv, at(t_mv, 3 * g + k + 1))
                    e.wait_ge(t_rs, at(t_rs, 3 * g + k + 1))
                    for t in range(NT):
                        m = e.tensor_scalar(dst[t], src[t], mv0[:, t, 0:1], rs0[:, t:t + 1], ALU.subtract, ALU.mult)
                    return m

                y = Y[:, bass.ds(8 * bb + 4 * i, NT), :].rearrange("p t d -> p (t d)")
                xf = x.rearrange("p t d -> p (t d)")
                ys = [xt(Y, 2 * bb + i, t) for t in range(NT)]
                xs = [x[:, t, :] for t in range(NT)]
                e.wait_ge(xw_loaded[i], at(xw_loaded[i], 16 * bb + 64 + 16))
                e.scalar_tensor_tensor(xf, y, 0.5, xf, ALU.mult, ALU.add).then_inc(t_x, 1)
                e.wait_ge(t_x, at(t_x, 2 * g + 1))
                norm(xs, ys, 0).then_inc(t_z, 1)
                e.wait_ge(t_z, at(t_z, 2 * g + 1))
                e.tensor_tensor(xf, xf, y, ALU.add).then_inc(t_x, 1)
                norm(ys, ys, 1).then_inc(t_z, 1)
                e.wait_ge(t_z, at(t_z, 2 * g + 2))
                settle(e)
                m = e.tensor_copy(h_flat, y)
                m.then_inc(t_h, 1)
                for c in range(2):
                    e.wait_ge(t_v_ps, at(t_v_ps, 2 * g + c + 1))
                    for q in range(2):
                        m = e.tensor_tensor(vt[:, 2 * c + q, :], bank[4 + c][:, q * D:(q + 1) * D], bv, ALU.add)
                m.then_inc(t_v, 1)
                for c in range(2):
                    e.wait_ge(t_g_ps, at(t_g_ps, 2 * g + c + 1))
                    gr = bank[6 + c][:, :].rearrange("p (c f k) -> p c f k", c=2, f=2)
                    e.tensor_tensor(n_low[:, 2 * c:2 * c + 2, :], gr[:, :, 0, :], tri[:, 0:1, :].to_broadcast([P, 2, P]), ALU.mult)
                    e.tensor_tensor(n_up[:, 2 * c:2 * c + 2, :], gr[:, :, 0, :], tri[:, 1:2, :].to_broadcast([P, 2, P]), ALU.mult)
                    m = e.tensor_tensor(a_up[:, 2 * c:2 * c + 2, :], gr[:, :, 1, :], tri[:, 2:3, :].to_broadcast([P, 2, P]), ALU.mult)
                m.then_inc(t_g, 1)
                e.wait_ge(t_g, at(t_g, g + 1))
                e.tensor_tensor(inv, n_low, tri[:, 3:4, :].to_broadcast([P, NT, P]), ALU.mult)
                e.tensor_tensor(invT, n_up, tri[:, 4:5, :].to_broadcast([P, NT, P]), ALU.mult).then_inc(t_i, 1)
                e.wait_ge(t_i, at(t_i, (LV + 2) * g + 1))
                eye = ident[:, :].unsqueeze(1).to_broadcast([P, NT, P])
                e.tensor_tensor(inv, eye, inv, ALU.subtract)
                e.tensor_tensor(invT, eye, invT, ALU.subtract).then_inc(t_i, 1)
                for l in range(LV):
                    e.wait_ge(t_i, at(t_i, (LV + 2) * g + l + 2))
                    e.wait_ge(t_i_ps, at(t_i_ps, LV * g + l + 1))
                    if l < LV - 1:
                        e.tensor_tensor(inv, inv, cut(bank[2][:, :], NT), ALU.subtract)
                    e.tensor_tensor(invT, invT, cut(bank[3][:, :], NT), ALU.subtract).then_inc(t_i, 1)
                for c in range(NT):
                    k = NT * g + c
                    e.wait_ge(t_r_ps, at(t_r_ps, k + 1))
                    if c == 0:
                        e.wait_ge(t_v, at(t_v, g + 1))
                        e.wait_ge(t_e_ps, at(t_e_ps, k))
                    e.tensor_tensor(residue, bank[0][:, 0:D], vt[:, c, :], ALU.subtract).then_inc(t_r, 1)
                    e.wait_ge(t_w_ps, at(t_w_ps, k + 1))
                    e.tensor_tensor(state[0:DS, :], state[0:DS, :], bank[2][0:DS, 0:D], ALU.add).then_inc(t_w, 1)
                    e.wait_ge(t_y_ps, at(t_y_ps, k + 1))
                    e.wait_ge(t_x, at(t_x, 2 * g + 2))
                    e.tensor_tensor(x[:, c, :], x[:, c, :], bank[3][:, 0:D], ALU.add).then_inc(t_y, 1)
                e.wait_ge(t_y, at(t_y, NT * g + NT))
                norm(xs, ys, 2).then_inc(s_ln, 4)

            def scale_rot(d):
                for t in range(NT):
                    m = e.tensor_tensor(rot[:, t, :, :].rearrange("p f d -> p (f d)"), h2[:, t, :],
                                        t1[:, 0, d * 256:(d + 1) * 256], ALU.mult)
                m.then_inc(rot_scaled, 1)

            e.wait_ge(s_const, at(s_const, 5))
            e.wait_ge(s_w, at(s_w, 16 * 8))
            e.tensor_copy(identb[:, :], ident[:, :])
            e.tensor_copy(maskb[:, 0, 0, :, :].rearrange("p w k -> p (w k)"), t2[:, 0, 0:256])
            e.tensor_copy(maskb[:, 0, 1, :, :].rearrange("p w k -> p (w k)"), t2[:, 0, 0:256])
            e.tensor_copy(maskb[:, 1, 0, :, :].rearrange("p w k -> p (w k)"), t2[:, 0, 256:512])
            e.tensor_copy(maskb[:, 1, 1, :, :].rearrange("p w k -> p (w k)"), t2[:, 0, 256:512])
            scale_rot(1)
            scaled = 0
            for c, (d, name, k) in enumerate(chunks):
                n, raw = extent(name), staged(c, extent(name))
                if name == "w1":
                    scaled += 1
                    e.wait_ge(wp_loaded[c % 3], at(wp_loaded[c % 3], 16 * (c // 3 + 1)))
                    e.wait_ge(wp_raw, at(wp_raw, scaled))
                    e.tensor_scalar(raw, raw, lng[:, d, k:k + 1], None, ALU.mult).then_inc(wp_scaled, 1)
                if c == 5:
                    e.wait_ge(rot_stored, at(rot_stored, 16))
                    scale_rot(0)
                    e.wait_ge(wp_stored, at(wp_stored, 16 * 3))
                e.wait_ge(wp_hi, at(wp_hi, c + 1))
                e.tensor_tensor(split_of(name, k, 1), raw, split_of(name, k, 0), ALU.subtract).then_inc(wp_lo, 1)
                if name == "w1" and k == 1:
                    for half in range(2):
                        src = bank[d][:, 12 * half:12 * half + 12]
                        e.tensor_tensor(b1[:, d, :, :].rearrange("p a b -> p (a b)"), b1[:, d, :, :].rearrange("p a b -> p (a b)"), src, ALU.add).then_inc(b1_step, 1)
                        e.wait_ge(b1_step, at(b1_step, 2 * (1 - d) + half + 1))
            dve_entry(e)
            e.wait_ge(rot_scaled, at(rot_scaled, 2))
            e.sem_inc(s_const, 3)
            e.wait_ge(s_const, at(s_const, 8))
            for ps in range(passes):
                transformer(ps)
                if ps == 0 and do_ttt:
                    e.wait_ge(T_ZERO0, at(T_ZERO0, 1))
                    e.wait_ge(T_W, at(T_W, 16 * 5))
                    with e.Fori(0, B // 2) as bb:
                        for i in range(2):
                            ttt(bb, i)
                    e.memset(h[0:1, 0, :], 0.0).then_inc(T_DONE, 1)
                else:
                    dve_exit(e, ps)


def constants():
    f = np.float32
    half = np.arange(0, DH, 2, dtype=f)
    inv = (f(1.0) / np.power(f(10000.0), half / f(DH))).astype(f)
    t = np.arange(N, dtype=f)
    fr = (t[:, None] * inv[None]).astype(f)
    fr = np.concatenate([fr, fr], -1)
    base = ((half + f(0.4 * DH)) / f(1.4 * DH)).astype(f)
    power = (t - N // 2) / f(WINDOW // 2)
    sc = np.power(base[None], power[:, None]).astype(f)
    sc = np.concatenate([sc, sc], -1)
    sign = np.concatenate([-np.ones(DH // 2, f), np.ones(DH // 2, f)])
    cos, sin = np.cos(fr), np.sin(fr) * sign
    q8 = f(QK_SCALE)
    tab = np.stack([cos * sc * q8, sin * sc * q8, cos / sc, sin / sc], 1).astype(f)
    tab = tab.reshape(NT, P, 4, DH).transpose(1, 0, 2, 3).reshape(P, -1)
    i, j = np.arange(P)[:, None], np.arange(2 * WINDOW)[None]
    own = np.where(j[:, :WINDOW] > i, f(NEG), f(0))
    before = np.where(j[:, :WINDOW] < i, f(NEG), f(0))
    mask = np.concatenate([own, before, before, own], 1)
    r_, c_ = np.arange(P)[:, None], np.arange(P)[None]
    lr = f(TTT_LR)
    tri = [np.where(r_ > c_, lr, f(0)), np.where(r_ < c_, lr, f(0)), np.where(r_ < c_, -lr, f(0))]

    def blocks(b, row, col):
        return ((row // (2 * b) == col // (2 * b)) & (row % (2 * b) >= b) & (col % (2 * b) < b)).astype(f)

    tri += [blocks(1, r_, c_)] + [blocks(2 ** l, c_, r_) for l in range(NLEV)]
    tri = np.stack(tri, 1).astype(f)
    return {"zero": np.zeros((1, D // 2), f), "tri": tri, "rot": np.ascontiguousarray(tab), "mask": mask.astype(f), "ident": np.eye(P, dtype=f)}


def layouts(I):
    g = {k: np.asarray(v) for k, v in I.items()}
    out = dict(constants())
    out["x"] = g["L0_attn_x"]
    for k in ("wqkv", "wo"):
        out[k] = g["L0_ffn_" + k]
    out["w1"] = np.zeros((DEPTH, D, 2, HP), np.float32)
    out["w1"][..., :HID] = g["L0_ffn_w1"].reshape(DEPTH, D, 2, HID)
    out["w1"] = out["w1"].reshape(DEPTH, D, 2 * HP)
    out["w2"] = np.zeros((DEPTH, HP, D), np.float32)
    out["w2"][:, :HID] = g["L0_ffn_w2"]
    sw = np.r_[DH // 2:DH, 0:DH // 2]
    qs, ks = g["L0_ffn_q_scale"], g["L0_ffn_k_scale"]
    out["qks"] = np.broadcast_to(np.stack([qs, qs[:, sw], ks, ks[:, sw]], 1).reshape(1, -1), (P, DEPTH * 4 * DH))
    out["lng"] = g["L0_ffn_ln_g"].reshape(DEPTH, KT, P).transpose(2, 0, 1)
    out["lnb"] = g["L0_ffn_ln_b"].reshape(DEPTH, KT, P).transpose(2, 0, 1)
    b1 = np.zeros((DEPTH, 2, MT * P), np.float32)
    b1[:, :, :HID] = g["L0_ffn_b1"].reshape(DEPTH, 2, HID)
    out["b1"] = b1.reshape(DEPTH, 2, MT, P).transpose(3, 0, 1, 2).reshape(P, -1)
    out["b2"] = np.broadcast_to(g["L0_ffn_b2"].reshape(1, -1), (P, DEPTH * D))
    out["wv"] = g["L0_attn_Wv"].T.reshape(KT, P, D).transpose(1, 0, 2)
    out["tw"] = np.concatenate([g["L0_attn_Wk"].T, g["L0_attn_Wq"].T], 1).reshape(KT, P, 2 * DS).transpose(1, 0, 2)
    out["bv"] = np.broadcast_to(g["L0_attn_bv"], (P, D))
    tv = np.zeros((P, 2 * KT + 2), np.float32)
    tv[:, 0:KT] = g["L0_attn_gamma"].reshape(KT, P).T
    tv[:, KT:2 * KT] = g["L0_attn_beta"].reshape(KT, P).T
    tv[:DS, 2 * KT] = g["L0_attn_bk"]
    tv[:DS, 2 * KT + 1] = g["L0_attn_bq"]
    out["tv"] = tv
    return {k: np.ascontiguousarray(v) for k, v in out.items()}


def kernel(**inputs):
    import concourse.bacc as _bacc
    from concourse.bass_utils import run_bass_kernel_spmd as _run

    arrays = layouts(inputs)
    nc = _bacc.Bacc("TRN2", target_bir_lowering=False, num_devices=1)
    A = {n: nc.dram_tensor("in_" + n, a.shape, mybir.dt.from_np(a.dtype), kind="ExternalInput").ap() for n, a in arrays.items()}
    A["out"] = nc.dram_tensor("out", (B, N, D), F32, kind="ExternalOutput").ap()
    build(nc, A)
    r = _run(nc, [{"in_" + n: a for n, a in arrays.items()}], core_ids=[0])
    return r.results[0]["out"]
```

```python
import numpy as np
import concourse.bass as bass
from concourse import mybir
from contextlib import ExitStack

F32 = mybir.dt.float32
F32R = mybir.dt.float32r
BF16 = mybir.dt.bfloat16
ALU = mybir.AluOpType
ACT = mybir.ActivationFunctionType
AX = mybir.AxisListType

P = 128
B, N, D = 8, 512, 256
DEPTH, HEADS, DH = 2, 8, 64
INNER = HEADS * DH
WINDOW = 128
HID = int(D * 4 * 2 / 3)
DS = 64
NT = N // P
KT = D // P
PAIRS = HEADS // 2
MT = -(-HID // P)
HP = MT * P
QK_SCALE = 8.0
NEG = -1e30
TTT_LR = 0.01
LN_EPS = 1e-5
LAYERS = 2 * DEPTH
NLEV = 7


def build(nc, A, passes=2, do_ttt=True):
    ctx = ExitStack()
    with ctx:
        def sb(name, shape, dt=F32):
            return ctx.enter_context(nc.sbuf_tensor(name, shape, dt))

        credits = {}

        def sem(name, credit=1):
            made = ctx.enter_context(nc.semaphore(name))
            credits[id(made)] = (made, credit)
            return made

        def at(which, count):
            value = count + credits[id(which)][1]
            return max(value, 1) if isinstance(value, int) else value

        HL = 2
        Y = sb("Y", [P, B * NT, D])
        wqkv = sb("wqkv", [P, KT, HL, 3 * INNER], F32R)
        wo = sb("wo", [P, HL, PAIRS, D], F32R)
        w1 = sb("w1", [P, KT, HL, 2 * HP], F32R)
        w2 = sb("w2", [P, MT, D])
        rot = sb("rot", [P, NT, 4, DH])
        lng = sb("lng", [P, DEPTH, KT])
        lnb = sb("lnb", [P, DEPTH, KT])
        b1 = sb("b1", [P, DEPTH, 2, MT])
        b2 = sb("b2", [P, DEPTH, D])
        ident = sb("ident", [P, P])
        identb = sb("identb", [P, P], BF16)
        maskb = sb("maskb", [P, 2, 2, WINDOW], BF16)
        small = sb("small", [P, 4])
        h = sb("h", [P, NT, D])
        hT = sb("hT", [P, 2, HL, KT, P], F32R)
        sq = sb("sq", [P, 2, INNER])
        ssk = sb("ssk", [P, HEADS])
        ssq = sb("ssq", [P, HEADS])
        ssg = sb("ssg", [P, 2, HEADS])
        r = sb("r", [P, NT, 2, HEADS])
        t1 = sb("t1", [P, 2, INNER])
        t2 = sb("t2", [P, 2, INNER])
        kqr = sb("kqr", [P, 2, INNER])
        kr, qr = kqr[:, 0, :], kqr[:, 1, :]
        qT = sb("qT", [P, HL, PAIRS, 2, P], F32R)
        kT = sb("kT", [P, HL, PAIRS, 2, 2, P], F32R)
        v = sb("v", [P, NT, INNER])
        nm = sb("nm", [P, HEADS])
        nb = sb("nb", [P, HEADS])
        pr = sb("pr", [P, HEADS, 2 * WINDOW])
        den = sb("den", [P, HEADS])
        rden = sb("rden", [P, HEADS])
        pT = sb("pT", [P, HEADS, 2, P])
        oT = sb("oT", [P, HL, PAIRS, P], F32R)
        h2 = sb("h2", [P, NT, D])
        h2T = sb("h2T", [P, 2, HL, KT, 2 * P], F32R)
        st = sb("st", [P, NT, 6])
        mv = sb("mv", [P, NT, 2])
        vare = sb("vare", [P, NT])
        rs = sb("rs", [P, NT])
        gg = sb("gg", [P, 2, 2 * P])
        uT = sb("uT", [P, 2, MT, 2 * P])
        xb = sb("xb", [P, 2, D])

        rot_s = nc.dram_tensor("rot_scaled", (DEPTH, P, NT * 4 * DH), F32).ap()
        wqkv_s = nc.dram_tensor("wqkv_split", (DEPTH, P, KT * HL * 3 * INNER), F32).ap()
        wo_s = nc.dram_tensor("wo_split", (DEPTH, P, HL * PAIRS * D), F32).ap()
        w1_s = nc.dram_tensor("w1_split", (DEPTH, P, KT * HL * 2 * HP), F32).ap()

        bank = [ctx.enter_context(nc.psum_tensor(f"bank{i}", [P, 512], F32)) for i in range(8)]

        s_w = sem("weights_loaded", 0)
        s_const = sem("constants_ready", 0)
        s_settled = sem("settled", 0)
        s_ln = sem("pass_ln_done")
        s_lnst = sem("pass_ln_stats")
        negmax_done = sem("negmax_done")
        kr_step = sem("kr_step")
        ha_loaded = sem("ha_loaded", 0)
        ht_ps = sem("ht_ps")
        ht_hi, ht_lo = sem("ht_hi"), sem("ht_lo")
        q_ps, k_ps, v_ps = sem("q_ps"), sem("k_ps"), sem("v_ps")
        sqq, sqk = sem("sqq"), sem("sqk")
        rotq, rotk = sem("rotq"), sem("rotk")
        ssk_done, ssq_done = sem("ssk_done"), sem("ssq_done")
        rk_done, rq_done = sem("rk_done"), sem("rq_done")
        guard_k, guard_q = sem("guard_k"), sem("guard_q")
        wqkv_loaded = [sem(f"w{c}_loaded", 0) for c in "qkv"]
        wo_loaded = sem("wo_loaded", 0)
        w1_loaded, w2_loaded = sem("w1_loaded", 0), sem("w2_loaded", 0)
        qrot, krot = sem("qrot"), sem("krot")
        qt_ps, kt_ps = sem("qt_ps"), sem("kt_ps")
        qt_hi, qt_lo, kt_hi, kt_lo, v_sb = sem("qt_hi"), sem("qt_lo"), sem("kt_hi"), sem("kt_lo"), sem("v_sb")
        s_ps = sem("s_ps")
        nb_done = sem("nb_done")
        exp_done = sem("exp_done", 4)
        rden_done = sem("rden_done")
        pn_done = sem("pn_done", 4)
        pt_ps = sem("pt_ps", 4)
        pt_sb = sem("pt_sb")
        pv_ps = sem("pv_ps")
        o_hi, o_lo = sem("o_hi"), sem("o_lo")
        wo_ps = sem("wo_ps")
        xa_done = sem("xa_done")
        h2_loaded = [sem("h2_loaded0", 0), sem("h2_loaded1", 0)]
        st_done, mv_done, rs_done = sem("st_done"), sem("mv_done"), sem("rs_done")
        h2n_done = sem("h2n_done", 4)
        h2t_ps = sem("h2t_ps", 2)
        h2t_hi, h2t_lo = sem("h2t_hi"), sem("h2t_lo")
        w1_ps = sem("w1_ps", 12)
        gelu_done = sem("gelu_done")
        u_done = sem("u_done", 3)
        w2_ps = sem("w2_ps", 4)
        xb_done = sem("xb_done")
        xf_done = sem("xf_done", 4)

        def settle(e):
            e.sem_inc(s_settled, 1)

        def idx(L, b, t):
            return 4 * b + (32 * L + t)

        def xt(buf, b, t):
            if isinstance(b, int):
                return buf[:, 4 * b + t, :]
            return buf[:, bass.ds(4 * b + t, 1), :].rearrange("p a d -> p (a d)")

        def xts(buf, b, t, k, lo, hi, p0=0, p1=P):
            if isinstance(b, int):
                return buf[p0:p1, 4 * b + t:4 * b + t + k, lo:hi]
            return buf[p0:p1, bass.ds(4 * b + t, k), lo:hi]


        s_pln = sem("variance_guarded")

        st0 = sb("st0", [P, 2, NT, 6])
        mv0 = sb("mv0", [P, 2, NT, 2])
        va0 = sb("va0", [P, 2, NT])
        rs0 = sb("rs0", [P, 2, NT])
        s_mv0, s_va0, s_rs0 = sem("pass_mv"), sem("pass_var"), sem("pass_rstd")

        def flat(ap, lo, n):
            names = "abcde"[:len(ap.shape) - 1]
            return ap.rearrange("p " + " ".join(names) + " -> p (" + " ".join(names) + ")")[:, lo:lo + n]

        def cut(ap, n):
            return ap.rearrange("p (a c) -> p a c", a=n)

        xw = [cut(flat(uT[:, :, :, :], (1 + i) * N * KT, NT * D), NT) for i in range(2)]
        x_in = A["x"].rearrange("b (t p) d -> p b t d", p=P)
        x_out = A["out"].rearrange("b (t p) d -> p b t d", p=P)
        xw_loaded = [sem("xw0_loaded", 0), sem("xw1_loaded", 0)]
        xw_used = [sem("xw0_used", 1), sem("xw1_used", 1)]
        xw_mixed = [sem("xw0_mixed"), sem("xw1_mixed")]
        xw_stored = [sem("xw0_stored", 16), sem("xw1_stored", 16)]

        def seq(ap, b):
            return ap[:, bass.ds(b, 1), :, :].rearrange("p b t d -> p (b t) d")

        def sp_entry(e):
            with e.Fori(0, B // 2) as bb:
                for i in range(2):
                    e.wait_ge(xw_used[i], at(xw_used[i], bb))
                    settle(e)
                    e.dma_start(xw[i], seq(x_in, 2 * bb + i)).then_inc(xw_loaded[i], 16)

        def dve_entry(e):
            with e.Fori(0, B // 2) as bb:
                for i in range(2):
                    x = xw[i]
                    e.wait_ge(xw_loaded[i], at(xw_loaded[i], 16 * bb + 16))
                    for t in range(NT):
                        m = e.bn_stats(st0[:, i, t, :], x[:, t, :])
                    m.then_inc(s_lnst, 1)
                    e.wait_ge(s_lnst, at(s_lnst, 2 * bb + i + 1))
                    settle(e)
                    for t in range(NT):
                        m = e.bn_aggr(mv0[:, i, t, :], st0[:, i, t, :])
                    m.then_inc(s_mv0, 1)
                    e.wait_ge(s_rs0, at(s_rs0, 2 * bb + i + 1))
                    e.wait_ge(s_mv0, at(s_mv0, 2 * bb + i + 1))
                    for t in range(NT):
                        m = e.tensor_scalar(xt(Y, 2 * bb + i, t), x[:, t, :], mv0[:, i, t, 0:1], rs0[:, i, t:t + 1], ALU.subtract, ALU.mult)
                        m.then_inc(s_ln, 1)
                    e.wait_ge(s_ln, at(s_ln, 8 * bb + 4 * i + 4))
                    m = e.nop()
                    m.then_inc(xw_used[i], 1)

        def pool_entry(e):
            with e.Fori(0, B // 2) as bb:
                for i in range(2):
                    g = 2 * bb + i
                    e.wait_ge(s_mv0, at(s_mv0, g + 1))
                    settle(e)
                    e.tensor_scalar(va0[:, i, :], mv0[:, i, :, 1], LN_EPS, None, ALU.add).then_inc(s_va0, 1)
                    e.wait_ge(s_va0, at(s_va0, g + 1))
                    e.tensor_tensor(rs0[:, i, :], va0[:, i, :], small[:, 0:1].to_broadcast([P, NT]), ALU.pow).then_inc(s_rs0, 1)

        def sp_exit(e, ps):
            src = x_in if ps == 0 else x_out
            e.wait_ge(xf_done, at(xf_done, idx(DEPTH * ps + DEPTH - 1, B - 1, NT - 1) + 1))
            settle(e)
            with e.Fori(0, B // 2) as bb:
                for i in range(2):
                    e.wait_ge(xw_stored[i], at(xw_stored[i], 16 * bb + 64 * ps))
                    settle(e)
                    e.dma_start(xw[i], seq(src, 2 * bb + i)).then_inc(xw_loaded[i], 16)
                for i in range(2):
                    e.wait_ge(xw_mixed[i], at(xw_mixed[i], bb + 1))
                    settle(e)
                    e.dma_start(seq(x_out, 2 * bb + i), xw[i]).then_inc(xw_stored[i], 16)
            for i in range(2):
                e.wait_ge(xw_stored[i], at(xw_stored[i], 64 * ps + 64))
                settle(e)

        def dve_exit(e, ps):
            with e.Fori(0, B // 2) as bb:
                for i in range(2):
                    e.wait_ge(xw_loaded[i], at(xw_loaded[i], 16 * bb + (64 + 64 * ps) + 16))
                    y = Y[:, bass.ds(8 * bb + 4 * i, NT), :].rearrange("p t d -> p (t d)")
                    x = xw[i].rearrange("p t d -> p (t d)")
                    e.scalar_tensor_tensor(x, y, 0.5, x, ALU.mult, ALU.add).then_inc(xw_mixed[i], 1)

        blocks = [[h[:, :, :], 0], [sq[:, :, :], 0], [uT[:, :, :, :], 0], [kqr[:, :, :], 0], [pr[:, :, :], 0], [t2[:, :, :], 0],
                  [h2[:, :, :], 0], [pr[:, :, :], 1], [t1[:, :, :], 0], [v[:, :, :], 0], [pT[:, :, :, :], 0], [pT[:, :, :, :], 1]]

        def block_of(i, which, lo, n):
            ap, k = blocks[6 * i + which]
            return flat(ap, 1024 * k + lo, n)

        pair = range(2)
        hn = [cut(block_of(i, 0, 0, NT * D), NT) for i in pair]
        n_low = [cut(block_of(i, 0, 0, N), NT) for i in pair]
        n_up = [cut(block_of(i, 0, N, N), NT) for i in pair]
        z_T = [cut(block_of(i, 1, 0, KT * N), KT) for i in pair]
        a_up = [cut(block_of(i, 1, 0, N), NT) for i in pair]
        inv = [cut(block_of(i, 1, N, N), NT) for i in pair]
        kqT = [cut(block_of(i, 2, 0, 2 * N), 2) for i in pair]
        vt = [cut(block_of(i, 3, 0, NT * D), NT) for i in pair]
        invT = [cut(block_of(i, 4, 0, N), NT) for i in pair]
        mx = [cut(block_of(i, 4, N, N), NT) for i in pair]
        state = [block_of(i, 5, 0, D) for i in pair]
        residue = [block_of(i, 5, D, D) for i in pair]
        errT = [block_of(i, 5, 2 * D, D) for i in pair]
        kn = [cut(block_of(i, 5, 3 * D, NT * DS), NT) for i in pair]
        m_up = [[cut(flat(uT[:, :, :, :], (1 + i) * N * KT + par * N, N), NT) for par in range(2)] for i in pair]
        wv = cut(flat(v[:, :, :], 1024, KT * D), KT)
        tw = cut(flat(v[:, :, :], 1024 + KT * D, KT * 2 * DS), KT)
        bv = flat(v[:, :, :], 1024 + KT * D + KT * 2 * DS, D)
        tv = flat(gg[:, :, :], 0, 6)
        tri = cut(flat(w2[:, :, :], 0, 11 * P), 11)
        T_W = sem("ttt_weights", 0)

        def two_sems(name, credit=1):
            return [sem(f"{name}{i}", credit) for i in pair]

        T_ZERO = two_sems("ttt_zeroed")
        t_x, t_st, t_mv, t_va, t_rs = (two_sems("ttt_" + k) for k in ("x", "stats", "mv", "var", "rstd"))
        t_z, t_h, t_zt_ps, t_zt = (two_sems("ttt_" + k) for k in ("z", "h", "zT_ps", "zT"))
        t_kq_ps, t_kq, t_v_ps, t_v = (two_sems("ttt_" + k) for k in ("kq_ps", "kq", "v_ps", "v"))
        t_kn_ps, t_kn, t_g_ps, t_g = (two_sems("ttt_" + k) for k in ("kn_ps", "kn", "gram_ps", "gram"))
        t_m, t_p, t_i_ps, t_i = (two_sems("ttt_" + k) for k in ("level_masked", "mx", "inverse_ps", "inverse"))
        t_p_ps = two_sems("ttt_mx_ps", 2)
        t_r_ps, t_r, t_e_ps, t_e = (two_sems("ttt_" + k) for k in ("r_ps", "r", "e_ps", "e"))
        t_y_ps, t_y, t_w_ps, t_w = (two_sems("ttt_" + k) for k in ("y_ps", "y", "w_ps", "w"))
        LV = NLEV - 1
        TI = 2 * LV + 1

        def sp_mid(e):
            e.wait_ge(xf_done, at(xf_done, idx(DEPTH - 1, B - 1, NT - 1) + 1))
            settle(e)
            def load_x(bb, i):
                e.dma_start(xw[i], seq(x_in, 2 * bb + i)).then_inc(xw_loaded[i], 16)

            def store_y(bb, i):
                e.wait_ge(t_y[i], at(t_y[i], NT * bb + NT))
                settle(e)
                e.dma_start(seq(x_out, 2 * bb + i), Y[:, bass.ds(8 * bb + 4 * i, NT), :]).then_inc(xw_stored[i], 16)

            for i in pair:
                load_x(0, i)
            for dst, name in ((tv, "tv"), (tw, "tw"), (wv, "wv"), (bv, "bv"), (tri, "tri")):
                e.dma_start(dst, A[name]).then_inc(T_W, 16)
            with e.Fori(0, B // 2 - 1) as bb:
                for i in pair:
                    e.wait_ge(t_p_ps[i], at(t_p_ps[i], LV * bb + LV))
                    settle(e)
                    load_x(bb + 1, i)
                for i in pair:
                    store_y(bb, i)
            for i in pair:
                store_y(B // 2 - 1, i)
            for i in pair:
                e.wait_ge(xw_stored[i], at(xw_stored[i], 64))
                settle(e)

        T_ZERO0 = sem("ttt_zero_rows")
        T_DONE = sem("ttt_done")

        chunks = [(d, name, k) for d in (1, 0) for name, k in (("wqkv", 0), ("wqkv", 1), ("w1", 0), ("w1", 1), ("wo", 0))]
        wp_loaded = [sem(f"chunk{i}_loaded", 0) for i in range(3)]
        wp_raw, wp_scaled, wp_hi, wp_lo = sem("chunk_raw_used"), sem("chunk_scaled"), sem("chunk_hi"), sem("chunk_lo")
        wp_stored, rot_stored = sem("split_stored", 0), sem("rot_stored", 0)
        rot_scaled, rot_loaded = sem("rot_scaled", 0), sem("rot_loaded", 0)
        b1_step = sem("beta_added")

        def staged(c, n):
            return flat((pr, pT, v)[c % 3][:, :, :] if c % 3 != 1 else pT[:, :, :, :], 0, n)

        def split_of(name, k, part):
            if name == "wo":
                return wo[:, part, :, :].rearrange("p a n -> p (a n)")
            return (wqkv if name == "wqkv" else w1)[:, k, part, :]

        def extent(name):
            return PAIRS * D if name == "wo" else 3 * INNER

        def load_chunk(e, c):
            d, name, k = chunks[c]
            if c >= 3:
                e.wait_ge(wp_lo, at(wp_lo, c - 2))
            if name == "wo":
                src = A["wo"][d].rearrange("(k p) n -> p k n", p=P)
                dst = staged(c, PAIRS * D).rearrange("p (k n) -> p k n", k=PAIRS)
            else:
                src = A[name][d, k * P:(k + 1) * P, :]
                dst = staged(c, 3 * INNER)
            e.dma_start(dst, src).then_inc(wp_loaded[c % 3], 16)

        def store_split(e, d):
            e.wait_ge(wp_lo, at(wp_lo, 10 - 5 * d))
            e.wait_ge(rot_scaled, at(rot_scaled, 2 - d))
            e.dma_start(rot_s[d], rot[:, :, :, :].rearrange("p t f d -> p (t f d)")).then_inc(rot_stored, 16)
            e.dma_start(wqkv_s[d], wqkv[:, :, :, :].rearrange("p k s n -> p (k s n)").bitcast(F32)).then_inc(wp_stored, 16)
            e.dma_start(w1_s[d], w1[:, :, :, :].rearrange("p k s n -> p (k s n)").bitcast(F32)).then_inc(wp_stored, 16)
            e.dma_start(wo_s[d], wo[:, :, :, :].rearrange("p s a n -> p (s a n)").bitcast(F32)).then_inc(wp_stored, 16)

        block = ctx.enter_context(nc.Block())

        @block.sync
        def _(e):
            def load_h(L, b):
                d = D // 2
                if L % 2 == 0:
                    e.wait_ge(s_ln, at(s_ln, 32 * (L // 2) + 4 * b + 4))
                    settle(e)
                else:
                    e.wait_ge(xf_done, at(xf_done, idx(L - 1, b, 3) + 1))
                    settle(e)
                e.wait_ge(ht_ps, at(ht_ps, idx(L, b, 0)))
                settle(e)
                e.dma_start(h[:, :, 0:d], xts(Y, b, 0, NT, 0, d)).then_inc(ha_loaded, 16)
                e.dma_start(h[1:P, :, d:D], xts(Y, b, 0, NT, d, D, 0, P - 1)).then_inc(ha_loaded, 16)
                e.dma_start(h[0:1, 1:NT, d:D], xts(Y, b, 0, NT - 1, d, D, P - 1, P)).then_inc(ha_loaded, 16)

            def load_h2(L, b, half):
                d = D // 2
                t = 2 * half
                e.wait_ge(xa_done, at(xa_done, idx(L, b, t + 1) + 1))
                settle(e)
                e.wait_ge(h2t_ps, at(h2t_ps, 2 * b + (16 * L + half - 1)))
                settle(e)
                q = h2_loaded[half]
                e.dma_start(h2[:, t:t + 2, 0:d], xts(Y, b, t, 2, 0, d)).then_inc(q, 16)
                e.dma_start(h2[1:P, t:t + 2, d:D], xts(Y, b, t, 2, d, D, 0, P - 1)).then_inc(q, 16)
                if half == 0:
                    e.dma_start(h2[0:1, 0, d:D], A["zero"]).then_inc(q, 16)
                    e.dma_start(h2[0:1, 1:2, d:D], xts(Y, b, 0, 1, d, D, P - 1, P)).then_inc(q, 16)
                else:
                    e.dma_start(h2[0:1, 2:4, d:D], xts(Y, b, 1, 2, d, D, P - 1, P)).then_inc(q, 16)

            def load_wqkv(L):
                e.wait_ge(wp_stored, at(wp_stored, 16 * 6))
                e.wait_ge(rot_stored, at(rot_stored, 32))
                view = wqkv_s[L % 2].rearrange("p (k s c n) -> p k s c n", k=KT, s=HL, c=3)
                for c, used in ((1, k_ps), (0, q_ps), (2, v_ps)):
                    e.wait_ge(used, at(used, 32 * L))
                    for k in range(KT):
                        e.dma_start(wqkv[:, k, :, c * INNER:(c + 1) * INNER].bitcast(F32), view[:, k, :, c, :]).then_inc(wqkv_loaded[c], 16)
                e.wait_ge(rotq, at(rotq, 32 * L))
                e.dma_start(rot[:, :, :, :].rearrange("p t f d -> p (t f d)"), rot_s[L % 2]).then_inc(rot_loaded, 16)

            def load_rest(L):
                dd = L % 2
                e.wait_ge(wo_ps, at(wo_ps, 32 * L))
                e.dma_start(wo[:, :, :, :].rearrange("p s a n -> p (s a n)").bitcast(F32), wo_s[dd]).then_inc(wo_loaded, 16)
                e.wait_ge(w1_ps, at(w1_ps, 96 * L))
                e.dma_start(w1[:, :, :, :].rearrange("p k s n -> p (k s n)").bitcast(F32), w1_s[dd]).then_inc(w1_loaded, 16)
                if L % DEPTH and dd == 0:
                    load_w2(L)

            def load_w2(L):
                e.wait_ge(w2_ps, at(w2_ps, 32 * L))
                e.dma_start(w2[:, :, :], A["w2"][L % 2].rearrange("(k p) n -> p k n", p=P)).then_inc(w2_loaded, 16)

            def sequence(L, b, nxt, last=False):
                if nxt:
                    load_h(*nxt)
                load_h2(L, b, 0)
                if last and L + 1 < DEPTH * passes:
                    load_wqkv(L + 1)
                load_h2(L, b, 1)
                if L % 2 and isinstance(b, int) and b == 0:
                    load_w2(L)
                if last and L + 1 < DEPTH * passes:
                    load_rest(L + 1)

            def transformer(ps):
                load_h(DEPTH * ps, 0)
                if ps == 0:
                    store_split(e, 0)
                for L in range(DEPTH * ps, DEPTH * ps + DEPTH):
                    sequence(L, 0, (L, 1))
                    with e.Fori(1, B - 1) as b:
                        sequence(L, b, (L, b + 1))
                    end = L == DEPTH * ps + DEPTH - 1
                    sequence(L, B - 1, None if end else (L + 1, 0), True)

            w = s_w
            e.dma_start(lng[:, :, :], A["lng"]).then_inc(w, 16)
            e.dma_start(lnb[:, :, :], A["lnb"]).then_inc(w, 16)
            e.dma_start(b1[:, :, :, :].rearrange("p a b c -> p (a b c)"), A["b1"]).then_inc(w, 16)
            e.dma_start(ident[:, :], A["ident"]).then_inc(w, 16)
            e.dma_start(t2[:, 0, :], A["mask"]).then_inc(w, 16)
            e.dma_start(h2[:, :, :].rearrange("p t d -> p (t d)"), A["rot"]).then_inc(w, 16)
            e.dma_start(t1[:, 0, :], A["qks"]).then_inc(w, 16)
            e.dma_start(b2[:, :, :].rearrange("p a b -> p (a b)"), A["b2"]).then_inc(w, 16)
            for c in range(8):
                load_chunk(e, c)
            sp_entry(e)
            e.dma_start(w2[:, :, :], A["w2"][0].rearrange("(k p) n -> p k n", p=P)).then_inc(w2_loaded, 16)
            e.wait_ge(s_const, at(s_const, 5))
            for ps in range(passes):
                transformer(ps)
                if ps == 0 and do_ttt:
                    sp_mid(e)
                    e.wait_ge(T_DONE, at(T_DONE, 1))
                    if passes > 1:
                        load_w2(DEPTH)
                else:
                    sp_exit(e, ps)

        @block.gpsimd
        def _(e):
            def A1(L, b, t):
                m = idx(L, b, t)
                minus_half = small[:, 0:1].to_broadcast([P, HEADS])

                def heads(ap):
                    return ap.rearrange("p (h d) -> p h d", h=HEADS)

                e.wait_ge(ssk_done, at(ssk_done, m + 1))
                settle(e)
                e.tensor_scalar(ssg[:, 0, :], ssk[:, :], 1e-24, None, ALU.max).then_inc(guard_k, 1)
                e.wait_ge(guard_k, at(guard_k, m + 1))
                e.tensor_tensor(r[:, t, 0, :], ssg[:, 0, :], minus_half, ALU.pow).then_inc(rk_done, 1)
                e.wait_ge(kr_step, at(kr_step, m + 1))
                e.wait_ge(rk_done, at(rk_done, m + 1))
                e.tensor_tensor(heads(kr), heads(kr), r[:, t, 0, :].unsqueeze(2).to_broadcast([P, HEADS, DH]), ALU.mult).then_inc(krot, 1)
                e.wait_ge(rotq, at(rotq, m + 1))
                e.wait_ge(qt_ps, at(qt_ps, m))
                e.tensor_tensor(qr, t1[:, 1, :], t2[:, 1, :], ALU.add).then_inc(qrot, 1)
                e.wait_ge(ssq_done, at(ssq_done, m + 1))
                settle(e)
                e.tensor_scalar(ssg[:, 1, :], ssq[:, :], 1e-24, None, ALU.max).then_inc(guard_q, 1)
                e.wait_ge(guard_q, at(guard_q, m + 1))
                e.wait_ge(exp_done, at(exp_done, 4 * (m - 1)))
                e.tensor_tensor(r[:, t, 1, :], ssg[:, 1, :], minus_half, ALU.pow).then_inc(rq_done, 1)

            def NP(L, b, t, j):
                n = idx(L, b, t)
                wide = 2 * WINDOW if t else WINDOW
                e.wait_ge(rden_done, at(rden_done, 4 * n + j + 1))
                e.tensor_tensor(pr[:, 2 * j:2 * j + 2, 0:wide], pr[:, 2 * j:2 * j + 2, 0:wide],
                                rden[:, 2 * j:2 * j + 2].unsqueeze(2).to_broadcast([P, 2, wide]), ALU.mult).then_inc(pn_done, 1)

            def XB(L, b, t):
                n, dd = idx(L, b, t), L % 2
                e.wait_ge(xa_done, at(xa_done, n + 1))
                e.wait_ge(xf_done, at(xf_done, n - 1))
                e.tensor_tensor(xb[:, t % 2, :], xt(Y, b, t), b2[:, dd, :], ALU.add).then_inc(xb_done, 1)

            def LN(L, b, half):
                e.wait_ge(mv_done, at(mv_done, idx(L, b, 2 * half + 1) + 1))
                sl = slice(2 * half, 2 * half + 2)
                settle(e)
                e.tensor_scalar(vare[:, sl], mv[:, sl, 1], LN_EPS, None, ALU.add).then_inc(s_pln, 1)
                e.wait_ge(s_pln, at(s_pln, 2 * b + (16 * L + half + 1)))
                e.tensor_tensor(rs[:, sl], vare[:, sl], small[:, 0:1].to_broadcast([P, 2]), ALU.pow).then_inc(rs_done, 1)

            def sequence(L, b, prev, nxt):
                for t in range(NT):
                    ahead = (L, b, t + 1) if t < NT - 1 else nxt and (*nxt, 0)
                    if prev:
                        XB(*prev, t)
                    for j in range(4):
                        NP(L, b, t, j)
                    if t == 2:
                        LN(L, b, 0)
                    if ahead:
                        A1(*ahead)
                LN(L, b, 1)

            def transformer(ps):
                A1(DEPTH * ps, 0, 0)
                for L in range(DEPTH * ps, DEPTH * ps + DEPTH):
                    first, last = L == DEPTH * ps, L == DEPTH * ps + DEPTH - 1
                    sequence(L, 0, None if first else (L - 1, B - 1), (L, 1))
                    with e.Fori(1, B - 1) as b:
                        sequence(L, b, (L, b - 1), (L, b + 1))
                    sequence(L, B - 1, (L, B - 2), None if last else (L + 1, 0))
                for t in range(NT):
                    XB(L, B - 1, t)

            def rstd(i, count):
                e.wait_ge(t_mv[i], at(t_mv[i], count))
                settle(e)
                e.tensor_scalar(va0[:, i, :], mv0[:, i, :, 1], LN_EPS, None, ALU.add).then_inc(t_va[i], 1)
                e.wait_ge(t_va[i], at(t_va[i], count))
                e.tensor_tensor(rs0[:, i, :], va0[:, i, :], small[:, 0:1].to_broadcast([P, NT]), ALU.pow).then_inc(t_rs[i], 1)

            def ttt_first():
                for k in range(2):
                    for i in pair:
                        rstd(i, k + 1)

            def ttt(bb, more):
                for i in pair:
                    e.wait_ge(t_w[i], at(t_w[i], NT * bb))
                    e.wait_ge(t_y_ps[i], at(t_y_ps[i], NT * bb))
                    settle(e)
                    e.memset(state[i], 0.0).then_inc(T_ZERO[i], 1)
                for l in range(LV):
                    for i in pair:
                        if l == 0:
                            e.wait_ge(t_g[i], at(t_g[i], 2 * bb + 1))
                        e.wait_ge(t_p_ps[i], at(t_p_ps[i], LV * bb + l - 1))
                        e.tensor_tensor(m_up[i][l % 2], n_up[i], tri[:, 5 + l:6 + l, :].to_broadcast([P, NT, P]), ALU.mult).then_inc(t_m[i], 1)
                if more:
                    for k in range(2):
                        for i in pair:
                            rstd(i, 3 * bb + 3 + k)
                for i in pair:
                    rstd(i, 3 * bb + 3 + 2 * more)

            e.memset(small[:, 0:1], -0.5).then_inc(s_const, 1)
            for s_ in range(HL):
                e.memset(kT[:, s_, :, :, :, :].bitcast(F32), 0.0)
            e.memset(h[0:1, 0, :], 0.0)
            e.memset(small[:, 1:2], 1e-24).then_inc(s_const, 3)
            e.wait_ge(s_const, at(s_const, 4))
            for made, credit in credits.values():
                if credit:
                    e.sem_inc(made, credit)
            e.sem_inc(s_const, 1)
            pool_entry(e)
            for ps in range(passes):
                e.wait_ge(s_const, at(s_const, 8))
                transformer(ps)
                if ps == 0 and do_ttt:
                    e.wait_ge(xf_done, at(xf_done, idx(DEPTH - 1, B - 1, NT - 1) + 1))
                    e.memset(block_of(0, 2, 0, 2 * N)[64:P, :], 0.0)
                    e.memset(block_of(1, 2, 0, 2 * N)[64:P, :], 0.0).then_inc(T_ZERO0, 1)
                    ttt_first()
                    with e.Fori(0, B // 2 - 1) as bb:
                        ttt(bb, True)
                    ttt(B // 2 - 1, False)

        @block.scalar
        def _(e):
            def A0(L, b, t):
                m = idx(L, b, t)
                e.wait_ge(ht_ps, at(ht_ps, m + 1))
                e.wait_ge(v_ps, at(v_ps, m - 1))
                e.activation(hT[:, t % 2, 0, :, :].rearrange("p k c -> p (k c)"), bank[2][:, 0:D], ACT.Copy).then_inc(ht_hi, 1)

            def A1(L, b, t):
                m = idx(L, b, t)
                e.wait_ge(k_ps, at(k_ps, m + 1))
                e.wait_ge(ssk_done, at(ssk_done, m))
                e.activation(sq[:, 0, :], bank[0][:, :], ACT.Square).then_inc(sqk, 1)
                e.wait_ge(q_ps, at(q_ps, m + 1))
                e.wait_ge(ssq_done, at(ssq_done, m))
                e.activation(sq[:, 1, :], bank[1][:, :], ACT.Square).then_inc(sqq, 1)
                e.wait_ge(v_ps, at(v_ps, m + 1))
                e.wait_ge(pv_ps, at(pv_ps, m - 2))
                e.activation(v[:, t, :], bank[2][:, :], ACT.Copy).then_inc(v_sb, 1)

            def A2(L, b, t):
                m = idx(L, b, t)
                e.wait_ge(kt_ps, at(kt_ps, m + 1))
                e.wait_ge(s_ps, at(s_ps, 4 * m))
                for g in range(2):
                    last = e.activation(kT[64 * g:64 * g + 64, 0, :, g, t % 2, :], cut(bank[0][64 * g:64 * g + 64, :], PAIRS), ACT.Copy)
                last.then_inc(kt_hi, 1)
                e.wait_ge(qt_ps, at(qt_ps, m + 1))
                e.activation(qT[:, 0, :, t % 2, :], cut(bank[1][:, :], PAIRS), ACT.Copy).then_inc(qt_hi, 1)

            def S(L, b, t, j):
                n = idx(L, b, t)
                wide = 2 * WINDOW if t else WINDOW
                e.wait_ge(nb_done, at(nb_done, 4 * n + j + 1))
                e.wait_ge(pt_ps, at(pt_ps, 4 * (n - 1) + j + 1))
                if j == 0:
                    e.wait_ge(rden_done, at(rden_done, 4 * n))
                for g in range(2):
                    hd = 2 * j + g
                    last = e.activation(pr[:, hd, 0:wide], bank[j][:, g * 256:g * 256 + wide], ACT.Exp,
                                        bias=nb[:, hd:hd + 1], scale=r[:, t, 1, hd:hd + 1], accum_out=den[:, hd:hd + 1])
                last.then_inc(exp_done, 1)

            def PT(L, b, t, j):
                n = idx(L, b, t)
                e.wait_ge(pt_ps, at(pt_ps, 4 * n + j + 1))
                e.wait_ge(pv_ps, at(pv_ps, n))
                w = 2 if t else 1
                e.activation(pT[:, 2 * j:2 * j + 2, 0:w, :],
                             bank[4 + j % 2][:, :].rearrange("p (h w c) -> p h w c", h=2, w=2)[:, :, 0:w, :], ACT.Copy).then_inc(pt_sb, 1)

            def O(L, b, t):
                n = idx(L, b, t)
                e.wait_ge(pv_ps, at(pv_ps, n + 1))
                e.wait_ge(wo_ps, at(wo_ps, n))
                e.activation(oT[:, 0, :, :].rearrange("p a c -> p (a c)"), bank[6][:, :], ACT.Copy).then_inc(o_hi, 1)

            def H2T(L, b, half):
                e.wait_ge(h2t_ps, at(h2t_ps, 2 * b + (16 * L + half + 1)))
                e.wait_ge(w1_ps, at(w1_ps, 12 * b + (96 * L + 6 * half - 6)))
                e.activation(h2T[:, half, 0, :, :].rearrange("p k c -> p (k c)"), bank[4][:, :], ACT.Copy).then_inc(h2t_hi, 1)

            def G(L, b, half, mt):
                job = 6 * half + mt
                e.wait_ge(w1_ps, at(w1_ps, 12 * b + (96 * L + job + 1)))
                e.wait_ge(u_done, at(u_done, 12 * b + (96 * L + job - 1)))
                e.activation(gg[:, job % 2, :], bank[job % 4][:, 256:512], ACT.Gelu,
                             bias=b1[:, L % 2, 1, mt:mt + 1]).then_inc(gelu_done, 1)

            def sequence(L, b, prev, nxt):
                for t in range(NT):
                    ahead = (L, b, t + 1) if t < NT - 1 else nxt and (*nxt, 0)
                    ahead2 = (L, b, t + 2) if t < NT - 2 else nxt and (*nxt, t - 2)
                    for j in range(4):
                        S(L, b, t, j)
                    if ahead:
                        A1(*ahead)
                    for j in range(4):
                        PT(L, b, t, j)
                    O(L, b, t)
                    if t == 3:
                        H2T(L, b, 0)
                    if ahead2:
                        A0(*ahead2)
                    if ahead:
                        A2(*ahead)
                for mt in range(MT):
                    G(L, b, 0, mt)
                    if mt == 4:
                        H2T(L, b, 1)
                for mt in range(MT):
                    G(L, b, 1, mt)

            def transformer(ps):
                A0(DEPTH * ps, 0, 0)
                A1(DEPTH * ps, 0, 0)
                A0(DEPTH * ps, 0, 1)
                A2(DEPTH * ps, 0, 0)
                for L in range(DEPTH * ps, DEPTH * ps + DEPTH):
                    first, last = L == DEPTH * ps, L == DEPTH * ps + DEPTH - 1
                    sequence(L, 0, None if first else (L - 1, B - 1), (L, 1))
                    with e.Fori(1, B - 1) as b:
                        sequence(L, b, (L, b - 1), (L, b + 1))
                    sequence(L, B - 1, (L, B - 2), None if last else (L + 1, 0))

            def ttt(bb):
                for i in pair:
                    for k in range(KT):
                        e.wait_ge(t_zt_ps[i], at(t_zt_ps[i], 2 * bb + k + 1))
                        m = e.activation(z_T[i][:, k, :], bank[4 * i + k][:, :], ACT.Identity, bias=tv[:, KT + k:KT + k + 1], scale=tv[:, k:k + 1])
                    m.then_inc(t_zt[i], 1)
                for i in pair:
                    for k in range(2):
                        e.wait_ge(t_kq_ps[i], at(t_kq_ps[i], 2 * bb + k + 1))
                        m = e.activation(kqT[i][0:DS, k, :], bank[4 * i + 2 + k][0:DS, :], ACT.Identity, bias=tv[0:DS, 2 * KT + k:2 * KT + k + 1])
                    m.then_inc(t_kq[i], 1)
                for i in pair:
                    e.wait_ge(t_kn_ps[i], at(t_kn_ps[i], bb + 1))
                    e.activation(kn[i].rearrange("p a c -> p (a c)"), bank[4 * i][:, 0:NT * DS], ACT.Copy, scale=-TTT_LR).then_inc(t_kn[i], 1)
                for l in range(LV):
                    for i in pair:
                        e.wait_ge(t_p_ps[i], at(t_p_ps[i], LV * bb + l + 1))
                        e.activation(mx[i].rearrange("p a c -> p (a c)"), bank[4 * i][:, :], ACT.Copy).then_inc(t_p[i], 1)
                for c in range(NT):
                    for i in pair:
                        e.wait_ge(t_e_ps[i], at(t_e_ps[i], NT * bb + c + 1))
                        e.activation(errT[i], bank[4 * i + 1][:, 0:D], ACT.Copy).then_inc(t_e[i], 1)

            e.wait_ge(s_const, at(s_const, 5))
            scaled = 0
            for c, (d, name, k) in enumerate(chunks):
                if c == 5:
                    store_split(e, 1)
                    e.wait_ge(wp_stored, at(wp_stored, 16 * 3))
                if c in (7, 8):
                    load_chunk(e, c + 1)
                if name == "w1":
                    scaled += 1
                    e.wait_ge(wp_scaled, at(wp_scaled, scaled))
                else:
                    e.wait_ge(wp_loaded[c % 3], at(wp_loaded[c % 3], 16 * (c // 3 + 1)))
                e.activation(split_of(name, k, 0), staged(c, extent(name)), ACT.Copy).then_inc(wp_hi, 1)
            e.wait_ge(s_const, at(s_const, 8))
            for ps in range(passes):
                transformer(ps)
                if ps == 0 and do_ttt:
                    e.wait_ge(T_ZERO0, at(T_ZERO0, 1))
                    e.wait_ge(T_W, at(T_W, 16 * 5))
                    with e.Fori(0, B // 2) as bb:
                        ttt(bb)

        @block.tensor
        def _(e):
            def split_product(out, left, right, first=True, last=True):
                e.matmul(out, left[0], right[0], start=first, stop=False)
                e.matmul(out, left[0], right[1], start=False, stop=False)
                return e.matmul(out, left[1], right[0], start=False, stop=last)

            def A0(L, b, t):
                m = idx(L, b, t)
                if t == 0:
                    e.wait_ge(ha_loaded, at(ha_loaded, 48 * b + (48 * 8 * L + 48)))
                e.wait_ge(v_sb, at(v_sb, m))
                for k in range(KT):
                    mm = e.transpose(bank[2][:, k * P:(k + 1) * P], h[:, t, k * P:(k + 1) * P], ident[:, :])
                mm.then_inc(ht_ps, 1)

            def A1(L, b, t):
                m = idx(L, b, t)
                e.wait_ge(ht_lo, at(ht_lo, m + 1))
                for i, (done, col) in enumerate(((k_ps, 1), (q_ps, 0), (v_ps, 2))):
                    if L and isinstance(b, int) and b == 0 and t == 0:
                        e.wait_ge(wqkv_loaded[col], at(wqkv_loaded[col], 32 * L))
                    e.wait_ge(exp_done, at(exp_done, 4 * (m - 1) + i + 1))
                    for k in range(KT):
                        mm = split_product(bank[i][:, :], [hT[:, t % 2, s_, k, :] for s_ in range(HL)],
                                           [wqkv[:, k, s_, col * INNER:(col + 1) * INNER] for s_ in range(HL)],
                                           k == 0, k == KT - 1)
                    mm.then_inc(done, 1)

            def A2(L, b, t, i):
                m = idx(L, b, t)
                src, added, done = ((kr, krot, kt_ps), (qr, qrot, qt_ps))[i]
                e.wait_ge(added, at(added, m + 1))
                for p in range(PAIRS):
                    mm = e.transpose(bank[i][:, p * P:(p + 1) * P], src[:, p * P:(p + 1) * P], ident[:, :])
                mm.then_inc(done, 1)

            def S(L, b, t, j, more):
                n = idx(L, b, t)
                if j == 0:
                    e.wait_ge(kt_lo, at(kt_lo, n + 1))
                    e.wait_ge(qt_lo, at(qt_lo, n + 1))
                if j == 2 and (t < NT - 1 or more):
                    e.wait_ge(ht_lo, at(ht_lo, n + 2))
                if j == 3:
                    e.wait_ge(xa_done, at(xa_done, n))
                if t == 0:
                    e.wait_ge(u_done, at(u_done, 12 * b + (96 * L + j - 3)))
                slots = slice(0, 2) if t else slice(0, 1)
                out = bank[j][:, :].rearrange("p (h w k) -> p h w k", h=2, w=2)[:, :, slots, :]
                e.matmul(out, identb[:, :], maskb[:, t % 2, slots, :].unsqueeze(1).to_broadcast([P, 2, 2 if t else 1, WINDOW]), start=True, stop=False)
                split_product(out, [qT[:, s_, j, t % 2, :] for s_ in range(HL)],
                              [kT[:, s_, j, :, slots, :] for s_ in range(HL)], False, True).then_inc(s_ps, 1)

            def PT(L, b, t, j):
                n = idx(L, b, t)
                bk = 4 + j % 2
                e.wait_ge(pn_done, at(pn_done, 4 * n + j + 1))
                e.wait_ge(pt_sb, at(pt_sb, 4 * n + j - 1))
                if j == 0 and t == 0:
                    e.wait_ge(h2t_lo, at(h2t_lo, 2 * b + 16 * L))
                for g in range(2):
                    for w in range(2 if t else 1):
                        mm = e.transpose(bank[bk][:, (2 * g + w) * P:(2 * g + w + 1) * P],
                                         pr[:, 2 * j + g, w * P:(w + 1) * P], ident[:, :])
                mm.then_inc(pt_ps, 1)

            def PV(L, b, t, j):
                n = idx(L, b, t)
                if j == 0:
                    e.wait_ge(o_lo, at(o_lo, n))
                e.wait_ge(pt_sb, at(pt_sb, 4 * n + j + 1))
                for g in range(2):
                    hd = 2 * j + g
                    ws = (0, 1) if t else (0,)
                    for w in ws:
                        tile = t if w == t % 2 else t - 1
                        mm = e.matmul(bank[6][64 * g:64 * g + 64, j * P:(j + 1) * P],
                                      v[:, tile, hd * DH:(hd + 1) * DH], pT[:, hd, w, :],
                                      start=(w == 0), stop=(w == ws[-1]))
                if j == 3:
                    mm.then_inc(pv_ps, 1)

            def WO(L, b, t):
                n = idx(L, b, t)
                if L and t == 0:
                    e.wait_ge(wo_loaded, at(wo_loaded, 16 * L))
                e.wait_ge(exp_done, at(exp_done, 4 * n + 4))
                e.wait_ge(o_lo, at(o_lo, n + 1))
                for p in range(PAIRS):
                    mm = split_product(bank[3][:, 0:D], [oT[:, s_, p, :] for s_ in range(HL)],
                                       [wo[:, s_, p, :] for s_ in range(HL)], p == 0, p == PAIRS - 1)
                mm.then_inc(wo_ps, 1)

            def H2T(L, b, half):
                e.wait_ge(h2n_done, at(h2n_done, idx(L, b, 2 * half + 1) + 1))
                e.wait_ge(pt_sb, at(pt_sb, 4 * idx(L, b, 3) + 3))
                for k in range(KT):
                    for i in range(2):
                        mm = e.transpose(bank[4][:, (2 * k + i) * P:(2 * k + i + 1) * P],
                                         h2[:, 2 * half + i, k * P:(k + 1) * P], ident[:, :])
                mm.then_inc(h2t_ps, 1)

            def W1(L, b, half, mt, more):
                job, n = 6 * half + mt, idx(L, b, 3)
                if L and job == 0:
                    e.wait_ge(w1_loaded, at(w1_loaded, 16 * L))
                if mt == 0:
                    e.wait_ge(h2t_lo, at(h2t_lo, 2 * b + (16 * L + half + 1)))
                if job == 3:
                    e.wait_ge(xa_done, at(xa_done, n + 1))
                elif job < 3:
                    e.wait_ge(exp_done, at(exp_done, 4 * n + 4))
                    if more:
                        if job == 0:
                            e.wait_ge(kt_lo, at(kt_lo, n + 2))
                        if job == 1:
                            e.wait_ge(qt_lo, at(qt_lo, n + 2))
                        if job == 2:
                            e.wait_ge(ht_lo, at(ht_lo, n + 3))
                else:
                    e.wait_ge(u_done, at(u_done, 12 * b + (96 * L + job - 3)))
                for g in range(2):
                    for k in range(KT):
                        mm = split_product(bank[job % 4][:, g * 256:(g + 1) * 256],
                                           [w1[:, k, s_, g * HP + mt * P:g * HP + (mt + 1) * P] for s_ in range(HL)],
                                           [h2T[:, half, s_, k, :] for s_ in range(HL)], k == 0, k == KT - 1)
                mm.then_inc(w1_ps, 1)

            def W2(L, b, t, lo, hi):
                n = idx(L, b, t)
                if lo == 0:
                    if t == 0:
                        e.wait_ge(w2_loaded, at(w2_loaded, 16 * L + 16))
                    e.wait_ge(u_done, at(u_done, 12 * b + (96 * L + 6 * (t // 2) + 6)))
                    e.wait_ge(xf_done, at(xf_done, n))
                for mt in range(lo, hi):
                    mm = e.matmul(bank[7][:, 0:D], uT[:, t // 2, mt, (t % 2) * P:(t % 2 + 1) * P],
                                  w2[:, mt, :], start=(mt == 0), stop=(mt == MT - 1))
                if hi == MT:
                    mm.then_inc(w2_ps, 1)

            def sequence(L, b, prev, nxt):
                for t in range(NT):
                    ahead = (L, b, t + 1) if t < NT - 1 else nxt and (*nxt, 0)
                    ahead2 = (L, b, t + 2) if t < NT - 2 else nxt and (*nxt, t - 2)
                    cuts = (0, 4, 4, 5, MT) if t == 0 else (0, 0, 2, 5, MT)

                    def fill(k):
                        if prev and cuts[k] < cuts[k + 1]:
                            W2(*prev, t, cuts[k], cuts[k + 1])

                    for j in range(4):
                        S(L, b, t, j, bool(nxt))
                    fill(0)
                    if ahead:
                        A1(*ahead)
                    PT(L, b, t, 0)
                    PT(L, b, t, 1)
                    fill(1)
                    PT(L, b, t, 2)
                    PV(L, b, t, 0)
                    PT(L, b, t, 3)
                    for j in range(1, 4):
                        PV(L, b, t, j)
                    if t == 3:
                        H2T(L, b, 0)
                    if ahead2:
                        A0(*ahead2)
                    if ahead:
                        A2(*ahead, 0)
                    fill(2)
                    if ahead:
                        A2(*ahead, 1)
                    WO(L, b, t)
                    if t < 3:
                        fill(3)
                for mt in range(MT):
                    W1(L, b, 0, mt, bool(nxt))
                    if mt == 4:
                        fill(3)
                        H2T(L, b, 1)
                for mt in range(MT):
                    W1(L, b, 1, mt, bool(nxt))

            def transformer(ps):
                A0(DEPTH * ps, 0, 0)
                A1(DEPTH * ps, 0, 0)
                A0(DEPTH * ps, 0, 1)
                A2(DEPTH * ps, 0, 0, 0)
                A2(DEPTH * ps, 0, 0, 1)
                for L in range(DEPTH * ps, DEPTH * ps + DEPTH):
                    first, last = L == DEPTH * ps, L == DEPTH * ps + DEPTH - 1
                    sequence(L, 0, None if first else (L - 1, B - 1), (L, 1))
                    with e.Fori(1, B - 1) as b:
                        sequence(L, b, (L, b - 1), (L, b + 1))
                    sequence(L, B - 1, (L, B - 2), None if last else (L + 1, 0))
                for t in range(NT):
                    W2(L, B - 1, t, 0, MT)

            def ttt(bb):
                for i in pair:
                    e.wait_ge(t_h[i], at(t_h[i], bb + 1))
                    e.wait_ge(t_e[i], at(t_e[i], NT * bb))
                    for k in range(KT):
                        for t in range(NT):
                            m = e.transpose(bank[4 * i + k][:, t * P:(t + 1) * P], hn[i][:, t, k * P:(k + 1) * P], ident[:, :])
                        m.then_inc(t_zt_ps[i], 1)
                for i in pair:
                    e.wait_ge(t_zt[i], at(t_zt[i], bb + 1))
                    e.wait_ge(t_w[i], at(t_w[i], NT * bb))
                    e.wait_ge(t_y[i], at(t_y[i], NT * bb))
                    for f in range(2):
                        for k in range(KT):
                            m = e.matmul(bank[4 * i + 2 + f][0:DS, :], tw[:, k, f * DS:(f + 1) * DS], z_T[i][:, k, :], start=(k == 0), stop=(k == KT - 1))
                        m.then_inc(t_kq_ps[i], 1)
                for i in pair:
                    for c in range(NT):
                        for k in range(KT):
                            m = e.matmul(bank[4 * i + c // 2][:, (c % 2) * D:(c % 2 + 1) * D], z_T[i][:, k, c * P:(c + 1) * P], wv[:, k, :],
                                         start=(k == 0), stop=(k == KT - 1))
                        if c % 2:
                            m.then_inc(t_v_ps[i], 1)
                for i in pair:
                    e.wait_ge(t_kq[i], at(t_kq[i], bb + 1))
                    for c in range(NT):
                        m = e.matmul(bank[4 * i + 2 + c // 2][:, (c % 2) * 256:(c % 2 + 1) * 256], kqT[i][:, 0, c * P:(c + 1) * P],
                                     kqT[i][:, :, c * P:(c + 1) * P], start=True, stop=True)
                        if c % 2:
                            m.then_inc(t_g_ps[i], 1)
                for i in pair:
                    e.wait_ge(t_v[i], at(t_v[i], bb + 1))
                    settle(e)
                    for c in range(NT):
                        m = e.transpose(bank[4 * i][:, c * DS:(c + 1) * DS], kqT[i][0:DS, 0, c * P:(c + 1) * P], ident[0:DS, 0:DS])
                    m.then_inc(t_kn_ps[i], 1)
                for l in range(LV):
                    for i in pair:
                        if l == 0:
                            e.wait_ge(t_kn[i], at(t_kn[i], bb + 1))
                        e.wait_ge(t_m[i], at(t_m[i], LV * bb + l + 1))
                        e.wait_ge(t_i[i], at(t_i[i], TI * bb + 2 * l + 2 - (l > 0)))
                        for c in range(NT):
                            m = e.matmul(bank[4 * i][:, c * P:(c + 1) * P], m_up[i][l % 2][:, c, :], inv[i][:, c, :], start=True, stop=True)
                        m.then_inc(t_p_ps[i], 1)
                    for i in pair:
                        if l == 0:
                            e.wait_ge(t_g[i], at(t_g[i], 2 * bb + 2))
                        e.wait_ge(t_p[i], at(t_p[i], LV * bb + l + 1))
                        e.wait_ge(t_i[i], at(t_i[i], TI * bb + 2 * l + 2))
                        if l < LV - 1:
                            for c in range(NT):
                                m = e.matmul(bank[4 * i + 1][:, c * P:(c + 1) * P], invT[i][:, c, :], mx[i][:, c, :], start=True, stop=True)
                            m.then_inc(t_i_ps[i], 1)
                        for c in range(NT):
                            m = e.matmul(bank[4 * i + 2][:, c * P:(c + 1) * P], mx[i][:, c, :], invT[i][:, c, :], start=True, stop=True)
                        m.then_inc(t_i_ps[i], 1)
                for c in range(NT):
                    for i in pair:
                        k = NT * bb + c
                        if c == 0:
                            e.wait_ge(t_i[i], at(t_i[i], TI * bb + TI))
                            e.wait_ge(T_ZERO[i], at(T_ZERO[i], bb + 1))
                        e.wait_ge(t_w[i], at(t_w[i], k))
                        e.wait_ge(t_r[i], at(t_r[i], k))
                        e.matmul(bank[4 * i][:, 0:D], kqT[i][:, 0, c * P:(c + 1) * P], state[i], start=True, stop=True).then_inc(t_r_ps[i], 1)
                    for i in pair:
                        e.wait_ge(t_y[i], at(t_y[i], k))
                        e.matmul(bank[4 * i + 3][:, 0:D], kqT[i][:, 1, c * P:(c + 1) * P], state[i], start=True, stop=False)
                    for i in pair:
                        e.wait_ge(t_r[i], at(t_r[i], k + 1))
                        e.wait_ge(t_e[i], at(t_e[i], k))
                        e.matmul(bank[4 * i + 1][:, 0:D], invT[i][:, c, :], residue[i], start=True, stop=True).then_inc(t_e_ps[i], 1)
                    for i in pair:
                        e.wait_ge(t_e[i], at(t_e[i], k + 1))
                        e.matmul(bank[4 * i + 2][0:DS, 0:D], kn[i][:, c, :], errT[i], start=True, stop=True).then_inc(t_w_ps[i], 1)
                        e.matmul(bank[4 * i + 3][:, 0:D], a_up[i][:, c, :], errT[i], start=False, stop=True).then_inc(t_y_ps[i], 1)

            e.wait_ge(s_const, at(s_const, 5))
            e.wait_ge(s_w, at(s_w, 16 * 8))
            for c, (d, name, k) in enumerate(chunks):
                if name == "w1":
                    e.wait_ge(wp_loaded[c % 3], at(wp_loaded[c % 3], 16 * (c // 3 + 1)))
                    raw = staged(c, extent(name))
                    for mt in range(2 * MT):
                        mm = e.matmul(bank[d][:, 12 * k + mt:12 * k + mt + 1], raw[:, mt * P:(mt + 1) * P], lnb[:, d, k:k + 1], start=True, stop=True)
                    mm.then_inc(wp_raw, 1)
            e.wait_ge(s_const, at(s_const, 8))
            for ps in range(passes):
                transformer(ps)
                if ps == 0 and do_ttt:
                    e.wait_ge(T_ZERO0, at(T_ZERO0, 1))
                    e.wait_ge(T_W, at(T_W, 16 * 5))
                    with e.Fori(0, B // 2) as bb:
                        ttt(bb)

        @block.vector
        def _(e):
            def A0(L, b, t):
                m = idx(L, b, t)
                e.wait_ge(ht_hi, at(ht_hi, m + 1))
                e.tensor_tensor(hT[:, t % 2, 1, :, :].rearrange("p k c -> p (k c)"), bank[2][:, 0:D],
                                hT[:, t % 2, 0, :, :].rearrange("p k c -> p (k c)"), ALU.subtract).then_inc(ht_lo, 1)

            def A1(L, b, t):
                m = idx(L, b, t)
                if L and isinstance(b, int) and b == 0 and t == 0:
                    e.wait_ge(rot_loaded, at(rot_loaded, 16 * L))

                def heads(ap):
                    return ap.rearrange("p (h c j) -> p h c j", h=HEADS, c=2)

                for i, (squared, rotated, added, sums, summed, read) in enumerate((
                        (sqk, rotk, kr_step, ssk, ssk_done, guard_k), (sqq, rotq, qrot, ssq, ssq_done, guard_q))):
                    f = 2 * (1 - i)
                    e.wait_ge(squared, at(squared, m + 1))
                    e.wait_ge(read, at(read, m))
                    e.tensor_reduce(sums[:, :], sq[:, i, :].rearrange("p (h d) -> p h d", h=HEADS), AX.X, ALU.add).then_inc(summed, 1)
                    e.wait_ge(added, at(added, m))
                    e.tensor_tensor(t1[:, i, :].rearrange("p (h d) -> p h d", h=HEADS),
                                    bank[i][:, :].rearrange("p (h d) -> p h d", h=HEADS),
                                    rot[:, t, f:f + 1, :].to_broadcast([P, HEADS, DH]), ALU.mult)
                    e.tensor_tensor(heads(t2[:, i, :]), heads(bank[i][:, :])[:, :, ::-1, :],
                                    rot[:, t, f + 1:f + 2, :].to_broadcast([P, HEADS, DH]).rearrange("p h (c j) -> p h c j", c=2),
                                    ALU.mult).then_inc(rotated, 1)
                    if i == 0:
                        e.wait_ge(rotk, at(rotk, m + 1))
                        e.wait_ge(kt_ps, at(kt_ps, m))
                        e.tensor_tensor(kr, t1[:, 0, :], t2[:, 0, :], ALU.add).then_inc(kr_step, 1)

            def A2(L, b, t):
                m = idx(L, b, t)
                e.wait_ge(kt_hi, at(kt_hi, m + 1))
                for g in range(2):
                    rows = slice(64 * g, 64 * g + 64)
                    last = e.tensor_tensor(kT[rows, 1, :, g, t % 2, :], cut(bank[0][rows, :], PAIRS), kT[rows, 0, :, g, t % 2, :], ALU.subtract)
                last.then_inc(kt_lo, 1)
                e.wait_ge(qt_hi, at(qt_hi, m + 1))
                e.tensor_tensor(qT[:, 1, :, t % 2, :], cut(bank[1][:, :], PAIRS), qT[:, 0, :, t % 2, :], ALU.subtract).then_inc(qt_lo, 1)

            def S(L, b, t, j):
                n = idx(L, b, t)
                wide = 2 * WINDOW if t else WINDOW
                if j == 0:
                    e.wait_ge(rq_done, at(rq_done, n + 1))
                e.wait_ge(s_ps, at(s_ps, 4 * n + j + 1))
                e.tensor_reduce(nm[:, 2 * j:2 * j + 2], bank[j][:, :].rearrange("p (h k) -> p h k", h=2)[:, :, 0:wide],
                                AX.X, ALU.max, negate=True).then_inc(negmax_done, 1)
                e.wait_ge(exp_done, at(exp_done, 4 * (n - 1) + j + 1))
                e.wait_ge(negmax_done, at(negmax_done, 4 * n + j + 1))
                e.tensor_tensor(nb[:, 2 * j:2 * j + 2], nm[:, 2 * j:2 * j + 2], r[:, t, 1, 2 * j:2 * j + 2], ALU.mult).then_inc(nb_done, 1)

            def R(L, b, t, j):
                n = idx(L, b, t)
                e.wait_ge(exp_done, at(exp_done, 4 * n + j + 1))
                e.wait_ge(pn_done, at(pn_done, 4 * n + j - 3))
                e.reciprocal(rden[:, 2 * j:2 * j + 2], den[:, 2 * j:2 * j + 2]).then_inc(rden_done, 1)

            def O(L, b, t):
                n = idx(L, b, t)
                e.wait_ge(o_hi, at(o_hi, n + 1))
                e.tensor_tensor(oT[:, 1, :, :].rearrange("p a c -> p (a c)"), bank[6][:, :],
                                oT[:, 0, :, :].rearrange("p a c -> p (a c)"), ALU.subtract).then_inc(o_lo, 1)

            def WO(L, b, t):
                n = idx(L, b, t)
                e.wait_ge(wo_ps, at(wo_ps, n + 1))
                e.tensor_tensor(xt(Y, b, t), bank[3][:, 0:D], xt(Y, b, t), ALU.add).then_inc(xa_done, 1)

            def H2T(L, b, half):
                e.wait_ge(h2t_hi, at(h2t_hi, 2 * b + (16 * L + half + 1)))
                e.tensor_tensor(h2T[:, half, 1, :, :].rearrange("p k c -> p (k c)"), bank[4][:, :],
                                h2T[:, half, 0, :, :].rearrange("p k c -> p (k c)"), ALU.subtract).then_inc(h2t_lo, 1)

            def LN_moments(L, b, half):
                for t in (2 * half, 2 * half + 1):
                    if t == 2 * half:
                        dmas = 16 * (4 - half)
                        e.wait_ge(h2_loaded[half], at(h2_loaded[half], dmas * b + (dmas * 8 * L + dmas)))
                    e.bn_stats(st[:, t, :], h2[:, t, :]).then_inc(st_done, 1)
                for t in (2 * half, 2 * half + 1):
                    e.wait_ge(st_done, at(st_done, idx(L, b, t) + 1))
                    settle(e)
                    e.bn_aggr(mv[:, t, :], st[:, t, :]).then_inc(mv_done, 1)

            def LN_apply(L, b, half):
                for t in (2 * half, 2 * half + 1):
                    if t == 2 * half:
                        e.wait_ge(mv_done, at(mv_done, idx(L, b, t + 1) + 1))
                        e.wait_ge(rs_done, at(rs_done, 2 * b + (16 * L + half + 1)))
                    e.tensor_scalar(h2[:, t, :], h2[:, t, :], mv[:, t, 0:1], rs[:, t:t + 1], ALU.subtract, ALU.mult).then_inc(h2n_done, 1)

            def U(L, b, half, mt):
                job = 6 * half + mt
                e.wait_ge(gelu_done, at(gelu_done, 12 * b + (96 * L + job + 1)))
                if mt == 0:
                    e.wait_ge(w2_ps, at(w2_ps, idx(L, b, 0) + 2 * half - 2))
                e.scalar_tensor_tensor(uT[:, half, mt, :], bank[job % 4][:, 0:256], b1[:, L % 2, 0, mt:mt + 1],
                                       gg[:, job % 2, :], ALU.add, ALU.mult).then_inc(u_done, 1)

            def W2(L, b, t):
                n = idx(L, b, t)
                e.wait_ge(w2_ps, at(w2_ps, n + 1))
                e.wait_ge(xb_done, at(xb_done, n + 1))
                e.tensor_tensor(xt(Y, b, t), bank[7][:, 0:D], xb[:, t % 2, :], ALU.add).then_inc(xf_done, 1)

            def sequence(L, b, prev, nxt):
                for t in range(NT):
                    ahead = (L, b, t + 1) if t < NT - 1 else nxt and (*nxt, 0)
                    ahead2 = (L, b, t + 2) if t < NT - 2 else nxt and (*nxt, t - 2)
                    S(L, b, t, 0)
                    S(L, b, t, 1)
                    R(L, b, t, 0)
                    S(L, b, t, 2)
                    R(L, b, t, 1)
                    S(L, b, t, 3)
                    R(L, b, t, 2)
                    R(L, b, t, 3)
                    if prev and t:
                        W2(*prev, t - 1)
                    if t == 2:
                        LN_moments(L, b, 0)
                    if ahead:
                        A1(*ahead)
                    if t == 2:
                        LN_apply(L, b, 0)
                    O(L, b, t)
                    if t == 3:
                        H2T(L, b, 0)
                    if ahead2:
                        A0(*ahead2)
                    if ahead:
                        A2(*ahead)
                    WO(L, b, t)
                for mt in range(MT):
                    U(L, b, 0, mt)
                    if mt == 0:
                        LN_moments(L, b, 1)
                    if mt == 1:
                        LN_apply(L, b, 1)
                    if mt == 4:
                        H2T(L, b, 1)
                if prev:
                    W2(*prev, NT - 1)
                for mt in range(MT):
                    U(L, b, 1, mt)

            def transformer(ps):
                A0(DEPTH * ps, 0, 0)
                A1(DEPTH * ps, 0, 0)
                A0(DEPTH * ps, 0, 1)
                A2(DEPTH * ps, 0, 0)
                for L in range(DEPTH * ps, DEPTH * ps + DEPTH):
                    first, last = L == DEPTH * ps, L == DEPTH * ps + DEPTH - 1
                    sequence(L, 0, None if first else (L - 1, B - 1), (L, 1))
                    with e.Fori(1, B - 1) as b:
                        sequence(L, b, (L, b - 1), (L, b + 1))
                    sequence(L, B - 1, (L, B - 2), None if last else (L + 1, 0))
                for t in range(NT):
                    W2(L, B - 1, t)

            def moments(i, src, count):
                for t in range(NT):
                    m = e.bn_stats(st0[:, i, t, :], src[t])
                m.then_inc(t_st[i], 1)
                e.wait_ge(t_st[i], at(t_st[i], count))
                settle(e)
                for t in range(NT):
                    m = e.bn_aggr(mv0[:, i, t, :], st0[:, i, t, :])
                m.then_inc(t_mv[i], 1)

            def normalised(i, src, dst, count):
                e.wait_ge(t_mv[i], at(t_mv[i], count))
                e.wait_ge(t_rs[i], at(t_rs[i], count))
                for t in range(NT):
                    m = e.tensor_scalar(dst[t], src[t], mv0[:, i, t, 0:1], rs0[:, i, t:t + 1], ALU.subtract, ALU.mult)
                return m

            def tiles(bb, i):
                return [xt(Y, 2 * bb + i, t) for t in range(NT)]

            def whole(bb, i):
                return Y[:, bass.ds(8 * bb + 4 * i, NT), :].rearrange("p t d -> p (t d)")

            def ttt_input(bb, count):
                xs = [[xw[i][:, t, :] for t in range(NT)] for i in pair]
                hs = [[hn[i][:, t, :] for t in range(NT)] for i in pair]
                x = [xw[i].rearrange("p t d -> p (t d)") for i in pair]

                def mix(i):
                    e.wait_ge(xw_loaded[i], at(xw_loaded[i], 16 * bb + 64 + 16))
                    e.scalar_tensor_tensor(x[i], whole(bb, i), 0.5, x[i], ALU.mult, ALU.add).then_inc(t_x[i], 1)
                    e.wait_ge(t_x[i], at(t_x[i], 2 * bb + 1))
                    moments(i, xs[i], count + 1)

                def norm(i):
                    normalised(i, xs[i], tiles(bb, i), count + 1).then_inc(t_z[i], 1)
                    e.wait_ge(t_z[i], at(t_z[i], bb + 1))
                    settle(e)
                    moments(i, tiles(bb, i), count + 2)

                def second_norm():
                    for i in pair:
                        normalised(i, tiles(bb, i), hs[i], count + 2).then_inc(t_h[i], 1)
                    for i in pair:
                        e.wait_ge(t_h[i], at(t_h[i], bb + 1))
                        e.tensor_tensor(whole(bb, i), x[i], whole(bb, i), ALU.add).then_inc(t_x[i], 1)

                return mix, norm, second_norm

            def ttt_first():
                mix, norm, second_norm = ttt_input(0, 0)
                for i in pair:
                    mix(i)
                for i in pair:
                    norm(i)
                second_norm()

            def ttt(bb, more):
                if more:
                    mix, norm, second_norm = ttt_input(bb + 1, 3 * bb + 2)
                for i in pair:
                    for c in range(2):
                        e.wait_ge(t_v_ps[i], at(t_v_ps[i], 2 * bb + c + 1))
                        for q in range(2):
                            m = e.tensor_tensor(vt[i][:, 2 * c + q, :], bank[4 * i + c][:, q * D:(q + 1) * D], bv, ALU.add)
                    m.then_inc(t_v[i], 1)
                for i in pair:
                    for c in range(2):
                        e.wait_ge(t_g_ps[i], at(t_g_ps[i], 2 * bb + c + 1))
                        gr = bank[4 * i + 2 + c][:, :].rearrange("p (c f k) -> p c f k", c=2, f=2)
                        e.tensor_tensor(n_low[i][:, 2 * c:2 * c + 2, :], gr[:, :, 0, :], tri[:, 0:1, :].to_broadcast([P, 2, P]), ALU.mult)
                        m = e.tensor_tensor(n_up[i][:, 2 * c:2 * c + 2, :], gr[:, :, 0, :], tri[:, 1:2, :].to_broadcast([P, 2, P]), ALU.mult)
                    m.then_inc(t_g[i], 1)
                    e.wait_ge(t_g[i], at(t_g[i], 2 * bb + 1))
                    e.tensor_tensor(inv[i], n_low[i], tri[:, 3:4, :].to_broadcast([P, NT, P]), ALU.mult)
                    e.tensor_tensor(invT[i], n_up[i], tri[:, 4:5, :].to_broadcast([P, NT, P]), ALU.mult).then_inc(t_i[i], 1)
                    e.wait_ge(t_i[i], at(t_i[i], TI * bb + 1))
                    eye = ident[:, :].unsqueeze(1).to_broadcast([P, NT, P])
                    e.tensor_tensor(inv[i], eye, inv[i], ALU.subtract)
                    e.tensor_tensor(invT[i], eye, invT[i], ALU.subtract).then_inc(t_i[i], 1)
                for i in pair:
                    for c in range(2):
                        gr = bank[4 * i + 2 + c][:, :].rearrange("p (c f k) -> p c f k", c=2, f=2)
                        m = e.tensor_tensor(a_up[i][:, 2 * c:2 * c + 2, :], gr[:, :, 1, :], tri[:, 2:3, :].to_broadcast([P, 2, P]), ALU.mult)
                    m.then_inc(t_g[i], 1)
                for l in range(LV):
                    for i in pair:
                        if l < LV - 1:
                            e.wait_ge(t_i[i], at(t_i[i], TI * bb + 2 * l + 2 - (l > 0)))
                            e.wait_ge(t_i_ps[i], at(t_i_ps[i], (TI - 2) * bb + 2 * l + 1))
                            e.tensor_tensor(inv[i], inv[i], cut(bank[4 * i + 1][:, :], NT), ALU.subtract).then_inc(t_i[i], 1)
                        e.wait_ge(t_i[i], at(t_i[i], TI * bb + 2 * l + 2))
                        e.wait_ge(t_i_ps[i], at(t_i_ps[i], (TI - 2) * bb + 2 * l + 1 + (l < LV - 1)))
                        e.tensor_tensor(invT[i], invT[i], cut(bank[4 * i + 2][:, :], NT), ALU.subtract).then_inc(t_i[i], 1)
                for c in range(NT):
                    k = NT * bb + c
                    for i in pair:
                        e.wait_ge(t_r_ps[i], at(t_r_ps[i], k + 1))
                        e.wait_ge(t_v[i], at(t_v[i], bb + 1))
                        e.tensor_tensor(residue[i], bank[4 * i][:, 0:D], vt[i][:, c, :], ALU.subtract).then_inc(t_r[i], 1)
                    if more:
                        (mix if c < 2 else norm)(c % 2)
                    for i in pair:
                        e.wait_ge(t_w_ps[i], at(t_w_ps[i], k + 1))
                        e.tensor_tensor(state[i][0:DS, :], state[i][0:DS, :], bank[4 * i + 2][0:DS, 0:D], ALU.add).then_inc(t_w[i], 1)
                    for i in pair:
                        e.wait_ge(t_y_ps[i], at(t_y_ps[i], k + 1))
                        if c == 0:
                            e.wait_ge(t_x[i], at(t_x[i], 2 * bb + 2))
                        yt = tiles(bb, i)[c]
                        e.tensor_tensor(yt, yt, bank[4 * i + 3][:, 0:D], ALU.add).then_inc(t_y[i], 1)
                if more:
                    second_norm()
                for i in pair:
                    e.wait_ge(t_y[i], at(t_y[i], NT * bb + NT))
                    settle(e)
                    moments(i, tiles(bb, i), 3 * bb + 3 + 2 * more)
                for i in pair:
                    e.wait_ge(xw_stored[i], at(xw_stored[i], 16 * bb + 16))
                    normalised(i, tiles(bb, i), tiles(bb, i), 3 * bb + 3 + 2 * more).then_inc(s_ln, 4)

            def scale_rot(d):
                for t in range(NT):
                    m = e.tensor_tensor(rot[:, t, :, :].rearrange("p f d -> p (f d)"), h2[:, t, :],
                                        t1[:, 0, d * 256:(d + 1) * 256], ALU.mult)
                m.then_inc(rot_scaled, 1)

            e.wait_ge(s_const, at(s_const, 5))
            e.wait_ge(s_w, at(s_w, 16 * 8))
            e.tensor_copy(identb[:, :], ident[:, :])
            e.tensor_copy(maskb[:, :, :, :].rearrange("p a w k -> p (a w k)"), t2[:, 0, :])
            scale_rot(1)
            scaled = 0
            for c, (d, name, k) in enumerate(chunks):
                n, raw = extent(name), staged(c, extent(name))
                if name == "w1":
                    scaled += 1
                    e.wait_ge(wp_loaded[c % 3], at(wp_loaded[c % 3], 16 * (c // 3 + 1)))
                    e.wait_ge(wp_raw, at(wp_raw, scaled))
                    e.tensor_scalar(raw, raw, lng[:, d, k:k + 1], None, ALU.mult).then_inc(wp_scaled, 1)
                if c == 5:
                    dve_entry(e)
                    e.wait_ge(rot_stored, at(rot_stored, 16))
                    scale_rot(0)
                    e.wait_ge(wp_stored, at(wp_stored, 16 * 3))
                e.wait_ge(wp_hi, at(wp_hi, c + 1))
                e.tensor_tensor(split_of(name, k, 1), raw, split_of(name, k, 0), ALU.subtract).then_inc(wp_lo, 1)
                if name == "w1" and k == 1:
                    for half in range(2):
                        src = bank[d][:, 12 * half:12 * half + 12]
                        e.tensor_tensor(b1[:, d, :, :].rearrange("p a b -> p (a b)"), b1[:, d, :, :].rearrange("p a b -> p (a b)"), src, ALU.add).then_inc(b1_step, 1)
                        e.wait_ge(b1_step, at(b1_step, 2 * (1 - d) + half + 1))
            e.wait_ge(rot_scaled, at(rot_scaled, 2))
            e.sem_inc(s_const, 3)
            e.wait_ge(s_const, at(s_const, 8))
            for ps in range(passes):
                transformer(ps)
                if ps == 0 and do_ttt:
                    e.wait_ge(T_ZERO0, at(T_ZERO0, 1))
                    ttt_first()
                    e.wait_ge(T_W, at(T_W, 16 * 5))
                    with e.Fori(0, B // 2 - 1) as bb:
                        ttt(bb, True)
                    ttt(B // 2 - 1, False)
                    e.memset(h[0:1, 0, :], 0.0).then_inc(T_DONE, 1)
                else:
                    dve_exit(e, ps)


def constants():
    f = np.float32
    half = np.arange(0, DH, 2, dtype=f)
    inv = (f(1.0) / np.power(f(10000.0), half / f(DH))).astype(f)
    t = np.arange(N, dtype=f)
    fr = (t[:, None] * inv[None]).astype(f)
    fr = np.concatenate([fr, fr], -1)
    base = ((half + f(0.4 * DH)) / f(1.4 * DH)).astype(f)
    power = (t - N // 2) / f(WINDOW // 2)
    sc = np.power(base[None], power[:, None]).astype(f)
    sc = np.concatenate([sc, sc], -1)
    sign = np.concatenate([-np.ones(DH // 2, f), np.ones(DH // 2, f)])
    cos, sin = np.cos(fr), np.sin(fr) * sign
    q8 = f(QK_SCALE)
    tab = np.stack([cos * sc * q8, sin * sc * q8, cos / sc, sin / sc], 1).astype(f)
    tab = tab.reshape(NT, P, 4, DH).transpose(1, 0, 2, 3).reshape(P, -1)
    i, j = np.arange(P)[:, None], np.arange(2 * WINDOW)[None]
    own = np.where(j[:, :WINDOW] > i, f(NEG), f(0))
    before = np.where(j[:, :WINDOW] < i, f(NEG), f(0))
    mask = np.concatenate([own, before, before, own], 1)
    r_, c_ = np.arange(P)[:, None], np.arange(P)[None]
    lr = f(TTT_LR)
    tri = [np.where(r_ > c_, lr, f(0)), np.where(r_ < c_, lr, f(0)), np.where(r_ < c_, -lr, f(0))]

    def blocks(b, row, col):
        return ((row // (2 * b) == col // (2 * b)) & (row % (2 * b) >= b) & (col % (2 * b) < b)).astype(f)

    tri += [blocks(1, r_, c_)] + [blocks(2 ** l, c_, r_) for l in range(NLEV)]
    tri = np.stack(tri, 1).astype(f)
    return {"zero": np.zeros((1, D // 2), f), "tri": tri, "rot": np.ascontiguousarray(tab), "mask": mask.astype(f), "ident": np.eye(P, dtype=f)}


def layouts(I):
    g = {k: np.asarray(v) for k, v in I.items()}
    out = dict(constants())
    out["x"] = g["L0_attn_x"]
    for k in ("wqkv", "wo"):
        out[k] = g["L0_ffn_" + k]
    out["w1"] = np.zeros((DEPTH, D, 2, HP), np.float32)
    out["w1"][..., :HID] = g["L0_ffn_w1"].reshape(DEPTH, D, 2, HID)
    out["w1"] = out["w1"].reshape(DEPTH, D, 2 * HP)
    out["w2"] = np.zeros((DEPTH, HP, D), np.float32)
    out["w2"][:, :HID] = g["L0_ffn_w2"]
    sw = np.r_[DH // 2:DH, 0:DH // 2]
    qs, ks = g["L0_ffn_q_scale"], g["L0_ffn_k_scale"]
    out["qks"] = np.broadcast_to(np.stack([qs, qs[:, sw], ks, ks[:, sw]], 1).reshape(1, -1), (P, DEPTH * 4 * DH))
    out["lng"] = g["L0_ffn_ln_g"].reshape(DEPTH, KT, P).transpose(2, 0, 1)
    out["lnb"] = g["L0_ffn_ln_b"].reshape(DEPTH, KT, P).transpose(2, 0, 1)
    b1 = np.zeros((DEPTH, 2, MT * P), np.float32)
    b1[:, :, :HID] = g["L0_ffn_b1"].reshape(DEPTH, 2, HID)
    out["b1"] = b1.reshape(DEPTH, 2, MT, P).transpose(3, 0, 1, 2).reshape(P, -1)
    out["b2"] = np.broadcast_to(g["L0_ffn_b2"].reshape(1, -1), (P, DEPTH * D))
    out["wv"] = g["L0_attn_Wv"].T.reshape(KT, P, D).transpose(1, 0, 2)
    out["tw"] = np.concatenate([g["L0_attn_Wk"].T, g["L0_attn_Wq"].T], 1).reshape(KT, P, 2 * DS).transpose(1, 0, 2)
    out["bv"] = np.broadcast_to(g["L0_attn_bv"], (P, D))
    tv = np.zeros((P, 2 * KT + 2), np.float32)
    tv[:, 0:KT] = g["L0_attn_gamma"].reshape(KT, P).T
    tv[:, KT:2 * KT] = g["L0_attn_beta"].reshape(KT, P).T
    tv[:DS, 2 * KT] = g["L0_attn_bk"]
    tv[:DS, 2 * KT + 1] = g["L0_attn_bq"]
    out["tv"] = tv
    return {k: np.ascontiguousarray(v) for k, v in out.items()}


def kernel(**inputs):
    import concourse.bacc as _bacc
    from concourse.bass_utils import run_bass_kernel_spmd as _run

    arrays = layouts(inputs)
    nc = _bacc.Bacc("TRN2", target_bir_lowering=False, num_devices=1)
    A = {n: nc.dram_tensor("in_" + n, a.shape, mybir.dt.from_np(a.dtype), kind="ExternalInput").ap() for n, a in arrays.items()}
    A["out"] = nc.dram_tensor("out", (B, N, D), F32, kind="ExternalOutput").ap()
    build(nc, A)
    r = _run(nc, [{"in_" + n: a for n, a in arrays.items()}], core_ids=[0])
    return r.results[0]["out"]
```
